# Optimizing a Trainium2 kernel written in Bass

```python
import numpy as np
import jax
import jax.numpy as jnp

def _softmax(x, axis=-1):
    return jax.nn.softmax(x, axis=axis)

def _gelu(x):
    return jax.nn.gelu(x, approximate=True)

def _silu(x):
    return jax.nn.silu(x)

def _sigmoid(x):
    return jax.nn.sigmoid(x)

def _layernorm(x, axis=-1, eps=1e-05):
    m = jnp.mean(x, axis=axis, keepdims=True)
    v = jnp.var(x, axis=axis, keepdims=True)
    return (x - m) / jnp.sqrt(v + eps)

def _scatter_add(tgt, idx, src, axis=0):
    return tgt.at[idx].add(src)

def _segment_sum(src, seg, n):
    return jax.ops.segment_sum(src, seg, n)
kernel_name = 'mk_xattn_ffn_d4_seqx_r8_2e6fd9'

def setup_inputs(seed: int=0):
    np.random.seed(seed)
    _w = jnp.asarray

    def _rec_inputs():
        import jax
        import jax.numpy as jnp
        _rk = jax.random.key(seed)
        x = 7.22e-05 + 1 * jax.random.normal(jax.random.fold_in(_rk, 1), (16, 128, 128), jnp.float32)
        _lenS = 128 - jax.random.randint(jax.random.fold_in(_rk, 7), (16,), 0, max(1, 128 // 4) + 1, jnp.int32)
        _lenS2 = 128 - jax.random.randint(jax.random.fold_in(_rk, 8), (16,), 0, max(1, 128 // 4) + 1, jnp.int32)
        _ctx_1024P = jax.random.normal(jax.random.fold_in(_rk, 11), (16, 16, 128), jnp.float32)
        _ctx_1024c = jax.random.dirichlet(jax.random.fold_in(_rk, 511), 0.3 * jnp.ones((16,), jnp.float32), (16, 128))
        _ctx_1024t = jnp.einsum('bsk,bkd->bsd', _ctx_1024c, _ctx_1024P)
        _ctx_1024t = _ctx_1024t * jax.lax.rsqrt(jnp.mean(jnp.square(_ctx_1024t)) + 1e-12) * 0.953939
        ctx_1024 = 4.13588e-05 + 0.999923 * (_ctx_1024t + 0.3 * jax.random.normal(jax.random.fold_in(_rk, 611), (16, 128, 128), jnp.float32))
        _validS = jnp.arange(128)[None, :] < _lenS[:, None]
        _validS2 = jnp.arange(128)[None, :] < _lenS2[:, None]
        _causal = jnp.tril(jnp.ones((128, 128), dtype=bool))
        mask_BxS2_bk0 = jnp.logical_not(jnp.broadcast_to(_validS2[:, :], (16, 128)))
        return (x, ctx_1024, mask_BxS2_bk0)
    x, ctx_1024, mask_BxS2_bk0 = _rec_inputs()

    def _L0_xattn_setup():
        import math
        import jax, jax.numpy as jnp
        import numpy as np
        B, S, T, H, A, NH = (4, 256, 256, 128, 128, 16)
        HD = A // NH
        key = jax.random.key(seed)
        ks = jax.random.split(key, 12)
        sc = 1.0 / math.sqrt(H)
        return {'x': jax.random.normal(ks[0], (B, S, H), dtype=jnp.float32), 'y': jax.random.normal(ks[1], (B, T, H), dtype=jnp.float32), 'mask': jax.random.randint(ks[2], (B, T), 0, 2).astype(bool), 'wq': jax.random.normal(ks[3], (H, A), dtype=jnp.float32) * sc, 'bq': jnp.zeros((A,), dtype=jnp.float32), 'wk': jax.random.normal(ks[4], (H, A), dtype=jnp.float32) * sc, 'bk': jnp.zeros((A,), dtype=jnp.float32), 'wv': jax.random.normal(ks[5], (H, A), dtype=jnp.float32) * sc, 'bv': jnp.zeros((A,), dtype=jnp.float32), 'wo': jax.random.normal(ks[6], (A, H), dtype=jnp.float32) * sc, 'bo': jnp.zeros((H,), dtype=jnp.float32)}
    _L0_xattn_all = _L0_xattn_setup()
    _L0_xattn_in = {k: v for k, v in _L0_xattn_all.items() if k in ('wq', 'bq', 'wk', 'bk', 'wv', 'bv', 'wo', 'bo')}
    del _L0_xattn_all

    def _L0_ffn_setup():
        import jax, jax.numpy as jnp
        import numpy as np
        D = 128
        E = 8
        K = 2
        NUM_ITER = 2
        DT = 0.1
        H = 64
        CTX = 2 * D

        def _gelu(t):
            return jax.nn.gelu(t, approximate=False)

        def _inl(ctrl, x, v, mu):
            alpha_raw, beta_raw, gate_raw = jnp.split(ctrl, 3, axis=-1)
            alpha = jax.nn.sigmoid(alpha_raw)
            beta = jax.nn.softplus(beta_raw)
            gate = jax.nn.sigmoid(gate_raw)
            error = x - mu
            v_next = alpha * v - beta * error
            x_next = x + DT * gate * v_next
            return (x_next, v_next)
        key = jax.random.key(seed)
        ks = jax.random.split(key, 20)
        s = 0.02
        inp = {'x': jax.random.normal(ks[0], (4, 512, D), jnp.float32), 'w_r1': jax.random.normal(ks[1], (D, D // 4), jnp.float32) * s, 'b_r1': jnp.zeros((D // 4,), jnp.float32), 'w_r2': jax.random.normal(ks[2], (D // 4, E), jnp.float32) * s, 'b_r2': jnp.zeros((E,), jnp.float32), 'w_h1': jax.random.normal(ks[3], (D, D // 4), jnp.float32) * s, 'b_h1': jnp.zeros((D // 4,), jnp.float32), 'w_h2': jax.random.normal(ks[4], (D // 4, 1), jnp.float32) * s, 'b_h2': jnp.zeros((1,), jnp.float32), 'expert_w1': jax.random.normal(ks[5], (E, CTX, H), jnp.float32) * s, 'expert_b1': jnp.zeros((E, H), jnp.float32), 'expert_w2': jax.random.normal(ks[6], (E, H, 3 * D), jnp.float32) * s, 'expert_b2': jnp.zeros((E, 3 * D), jnp.float32), 'w_s1': jax.random.normal(ks[7], (CTX, H), jnp.float32) * s, 'b_s1': jnp.zeros((H,), jnp.float32), 'w_s2': jax.random.normal(ks[8], (H, 3 * D), jnp.float32) * s, 'b_s2': jnp.zeros((3 * D,), jnp.float32), 'shared_weight': jnp.asarray(0.5, jnp.float32), 'w_f1': jax.random.normal(ks[9], (D, 2 * D), jnp.float32) * s, 'b_f1': jnp.zeros((2 * D,), jnp.float32), 'w_f2': jax.random.normal(ks[10], (2 * D, D), jnp.float32) * s, 'b_f2': jnp.zeros((D,), jnp.float32), 'integration_weight': jnp.full((D,), 0.5, jnp.float32), 'mu': jnp.zeros((D,), jnp.float32)}
        return inp
    _L0_ffn_all = _L0_ffn_setup()
    _L0_ffn_in = {k: v for k, v in _L0_ffn_all.items() if k in ('w_r1', 'b_r1', 'w_r2', 'b_r2', 'w_h1', 'b_h1', 'w_h2', 'b_h2', 'expert_w1', 'expert_b1', 'expert_w2', 'expert_b2', 'w_s1', 'b_s1', 'w_s2', 'b_s2', 'shared_weight', 'w_f1', 'b_f1', 'w_f2', 'b_f2', 'integration_weight', 'mu')}
    del _L0_ffn_all

    def _L1_xattn_setup():
        import jax, jax.numpy as jnp
        import numpy as np
        import math
        B, S, D, H = (1, 256, 128, 16)
        DK = D // H
        DH = 64
        LOG_T_MIN = math.log(0.1)
        LOG_T_MAX = math.log(10.0)

        def _linear(x, W, b):
            return x @ W.T + b
        key = jax.random.key(seed)
        ks = jax.random.split(key, 20)
        p = 0.02
        return {'query': jax.random.normal(ks[0], (B, S, D), jnp.float32), 'key': jax.random.normal(ks[1], (B, S, D), jnp.float32), 'value': jax.random.normal(ks[2], (B, S, D), jnp.float32), 'Wq': jax.random.normal(ks[3], (D, D), jnp.float32) * p, 'bq': jax.random.normal(ks[4], (D,), jnp.float32) * p, 'Wk': jax.random.normal(ks[5], (D, D), jnp.float32) * p, 'bk': jax.random.normal(ks[6], (D,), jnp.float32) * p, 'Wv': jax.random.normal(ks[7], (D, D), jnp.float32) * p, 'bv': jax.random.normal(ks[8], (D,), jnp.float32) * p, 'Wo': jax.random.normal(ks[9], (D, D), jnp.float32) * p, 'bo': jax.random.normal(ks[10], (D,), jnp.float32) * p, 'w1': jax.random.normal(ks[11], (DH, 3), jnp.float32) * 0.3, 'b1': jax.random.normal(ks[12], (DH,), jnp.float32) * 0.1, 'w2': jax.random.normal(ks[13], (DH, DH), jnp.float32) * 0.1, 'b2': jax.random.normal(ks[14], (DH,), jnp.float32) * 0.1, 'w3': jax.random.normal(ks[15], (1, DH), jnp.float32) * 0.1, 'b3': jnp.full((1,), (LOG_T_MIN + LOG_T_MAX) / 2, jnp.float32)}
    _L1_xattn_all = _L1_xattn_setup()
    _L1_xattn_in = {k: v for k, v in _L1_xattn_all.items() if k in ('Wq', 'bq', 'Wk', 'bk', 'Wv', 'bv', 'Wo', 'bo', 'w1', 'b1', 'w2', 'b2', 'w3', 'b3')}
    del _L1_xattn_all

    def _L1_ffn_setup():
        import jax, jax.numpy as jnp
        import numpy as np
        B, S, D, E, F = (2, 256, 128, 14, 256)
        key = jax.random.key(seed)
        k = jax.random.split(key, 4)
        h = jax.random.normal(k[0], (B, S, D), dtype=jnp.float32)
        router_w = jax.random.normal(k[1], (D, E), dtype=jnp.float32) * 0.02
        w1 = jax.random.uniform(k[2], (E, D, F), dtype=jnp.float32, minval=-1.0, maxval=1.0) * float(np.sqrt(6.0 / D))
        w2 = jax.random.uniform(k[3], (E, F, D), dtype=jnp.float32, minval=-1.0, maxval=1.0) * float(np.sqrt(6.0 / F))
        b1 = jnp.zeros((E, F), dtype=jnp.float32)
        b2 = jnp.zeros((E, D), dtype=jnp.float32)
        return {'h': h, 'router_w': router_w, 'w1': w1, 'b1': b1, 'w2': w2, 'b2': b2}
    _L1_ffn_all = _L1_ffn_setup()
    _L1_ffn_in = {k: v for k, v in _L1_ffn_all.items() if k in ('router_w', 'w1', 'b1', 'w2', 'b2')}
    del _L1_ffn_all

    def _L2_xattn_setup():
        import jax, jax.numpy as jnp
        import numpy as np
        E = 128
        NUM_HEADS = 16
        DK = E // NUM_HEADS
        EPS = 1e-05
        NEG_INF = -jnp.inf

        def layer_norm(x, g, b):
            mu = jnp.mean(x, axis=-1, keepdims=True)
            var = jnp.var(x, axis=-1, keepdims=True)
            return (x - mu) * jax.lax.rsqrt(var + EPS) * g + b

        def self_attn(x, Wq, Wk, Wv):
            Q, K, V = (x @ Wq, x @ Wk, x @ Wv)
            energy = jnp.einsum('bqd,bkd->bqk', Q, K)
            S = energy.shape[-1]
            lengths = jnp.sum(energy[:, 0] != 0, axis=-1)
            kidx = jnp.arange(S)
            pad = kidx[None, None, :] >= lengths[:, None, None]
            causal = kidx[None, :] < kidx[:, None]
            causal = (kidx[None, :] > kidx[:, None])[None]
            energy = jnp.where(pad | causal, NEG_INF, energy)
            score = jax.nn.softmax(energy / np.sqrt(DK), axis=-1)
            return jnp.einsum('bqk,bkd->bqd', score, V)

        def cross_attn(x, context, Wq, Wk, Wv):
            Q = x @ Wq
            K, V = (context @ Wk, context @ Wv)
            energy = jnp.einsum('bqd,bkd->bqk', Q, K)
            Sk = energy.shape[-1]
            lengths = jnp.sum(energy[:, 0] != 0, axis=-1)
            kidx = jnp.arange(Sk)
            pad = kidx[None, None, :] >= lengths[:, None, None]
            energy = jnp.where(pad, NEG_INF, energy)
            score = jax.nn.softmax(energy / np.sqrt(DK), axis=-1)
            return jnp.einsum('bqk,bkd->bqd', score, V)
        key = jax.random.key(seed)
        ks = jax.random.split(key, 12)
        B, S = (8, 256)
        s = 1.0 / np.sqrt(E)
        inp = {'x': jax.random.normal(ks[0], (B, S, E), jnp.float32), 'context': jax.random.normal(ks[1], (B, S, E), jnp.float32), 'Wq1': jax.random.normal(ks[2], (E, E), jnp.float32) * s, 'Wk1': jax.random.normal(ks[3], (E, E), jnp.float32) * s, 'Wv1': jax.random.normal(ks[4], (E, E), jnp.float32) * s, 'Wq2': jax.random.normal(ks[5], (E, E), jnp.float32) * s, 'Wk2': jax.random.normal(ks[6], (E, E), jnp.float32) * s, 'Wv2': jax.random.normal(ks[7], (E, E), jnp.float32) * s, 'fc1_w': jax.random.normal(ks[8], (E, E), jnp.float32) * s, 'fc1_b': jnp.zeros((E,), jnp.float32), 'fc2_w': jax.random.normal(ks[9], (E, E), jnp.float32) * s, 'fc2_b': jnp.zeros((E,), jnp.float32), 'ln1_g': jnp.ones((E,), jnp.float32), 'ln1_b': jnp.zeros((E,), jnp.float32), 'ln2_g': jnp.ones((E,), jnp.float32), 'ln2_b': jnp.zeros((E,), jnp.float32), 'ln3_g': jnp.ones((E,), jnp.float32), 'ln3_b': jnp.zeros((E,), jnp.float32)}
        return inp
    _L2_xattn_all = _L2_xattn_setup()
    _L2_xattn_in = {k: v for k, v in _L2_xattn_all.items() if k in ('Wq1', 'Wk1', 'Wv1', 'Wq2', 'Wk2', 'Wv2', 'fc1_w', 'fc1_b', 'fc2_w', 'fc2_b', 'ln1_g', 'ln1_b', 'ln2_g', 'ln2_b', 'ln3_g', 'ln3_b')}
    del _L2_xattn_all

    def _L2_ffn_setup():
        import jax, jax.numpy as jnp
        import numpy as np
        B, T, D = (2, 128, 128)
        H, DK, K = (8, 128, 8)
        NKEYS = 32
        NEXP = NKEYS * NKEYS

        def _rmsnorm(x, w, eps=1e-06):
            inv = jax.lax.rsqrt(jnp.mean(x * x, axis=-1, keepdims=True) + eps)
            return x * inv * w
        key = jax.random.key(seed)
        ks = jax.random.split(key, 5)
        return {'x': jax.random.normal(ks[0], (B, T, D), jnp.float32), 'w_q': jax.random.normal(ks[1], (H * 2 * DK, D), jnp.float32) * 0.02, 'keys': jax.random.normal(ks[2], (H, NKEYS, 2, DK), jnp.float32) * 0.02, 'expert_down': jax.random.normal(ks[3], (NEXP, D), jnp.float32) * 0.02, 'expert_up': jax.random.normal(ks[4], (NEXP, D), jnp.float32) * 0.02, 'norm_w': jnp.ones((D,), jnp.float32)}
    _L2_ffn_all = _L2_ffn_setup()
    _L2_ffn_in = {k: v for k, v in _L2_ffn_all.items() if k in ('w_q', 'keys', 'expert_down', 'expert_up', 'norm_w')}
    del _L2_ffn_all

    def _L3_xattn_setup():
        import jax, jax.numpy as jnp
        import numpy as np
        N_HEAD = 16
        key = jax.random.key(seed)
        ks = jax.random.split(key, 8)
        B, T, D = (4, 256, 128)
        s = 0.02
        return {'querys': jax.random.normal(ks[0], (B, T, D), jnp.float32), 'keys': jax.random.normal(ks[1], (B, T, D), jnp.float32), 'values': jax.random.normal(ks[2], (B, T, D), jnp.float32), 'Wq': jax.random.normal(ks[3], (D, D), jnp.float32) * s, 'Wk': jax.random.normal(ks[4], (D, D), jnp.float32) * s, 'Wv': jax.random.normal(ks[5], (D, D), jnp.float32) * s, 'Wo': jax.random.normal(ks[6], (D, D), jnp.float32) * s, 'bo': jnp.zeros((D,), jnp.float32)}
    _L3_xattn_all = _L3_xattn_setup()
    _L3_xattn_in = {k: v for k, v in _L3_xattn_all.items() if k in ('Wq', 'Wk', 'Wv', 'Wo', 'bo')}
    del _L3_xattn_all

    def _L3_ffn_setup():
        import jax, jax.numpy as jnp
        import numpy as np
        key = jax.random.key(seed)
        ks = jax.random.split(key, 5)
        B, S, D_in, D_out, E, R = (4, 128, 128, 128, 8, 16)
        x = jax.random.normal(ks[0], (B, S, D_in), dtype=jnp.float32)
        weight = jax.random.normal(ks[1], (D_out, D_in), dtype=jnp.float32) / np.sqrt(D_in)
        gate_w = jax.random.normal(ks[2], (E, D_in), dtype=jnp.float32) / np.sqrt(D_in)
        lora_U = jax.random.normal(ks[3], (E, R, D_in), dtype=jnp.float32) / np.sqrt(D_in)
        lora_V = jax.random.normal(ks[4], (E, D_out, R), dtype=jnp.float32) / np.sqrt(R)
        return {'x': x, 'weight': weight, 'gate_w': gate_w, 'lora_U': lora_U, 'lora_V': lora_V}
    _L3_ffn_all = _L3_ffn_setup()
    _L3_ffn_in = {k: v for k, v in _L3_ffn_all.items() if k in ('weight', 'gate_w', 'lora_U', 'lora_V')}
    del _L3_ffn_all
    return {'x': x, 'ctx_1024': ctx_1024, 'mask_BxS2_bk0': mask_BxS2_bk0, 'L0_xattn_wq': _L0_xattn_in['wq'], 'L0_xattn_bq': _L0_xattn_in['bq'], 'L0_xattn_wk': _L0_xattn_in['wk'], 'L0_xattn_bk': _L0_xattn_in['bk'], 'L0_xattn_wv': _L0_xattn_in['wv'], 'L0_xattn_bv': _L0_xattn_in['bv'], 'L0_xattn_wo': _L0_xattn_in['wo'], 'L0_xattn_bo': _L0_xattn_in['bo'], 'L0_ffn_w_r1': _L0_ffn_in['w_r1'], 'L0_ffn_b_r1': _L0_ffn_in['b_r1'], 'L0_ffn_w_r2': _L0_ffn_in['w_r2'], 'L0_ffn_b_r2': _L0_ffn_in['b_r2'], 'L0_ffn_w_h1': _L0_ffn_in['w_h1'], 'L0_ffn_b_h1': _L0_ffn_in['b_h1'], 'L0_ffn_w_h2': _L0_ffn_in['w_h2'], 'L0_ffn_b_h2': _L0_ffn_in['b_h2'], 'L0_ffn_expert_w1': _L0_ffn_in['expert_w1'], 'L0_ffn_expert_b1': _L0_ffn_in['expert_b1'], 'L0_ffn_expert_w2': _L0_ffn_in['expert_w2'], 'L0_ffn_expert_b2': _L0_ffn_in['expert_b2'], 'L0_ffn_w_s1': _L0_ffn_in['w_s1'], 'L0_ffn_b_s1': _L0_ffn_in['b_s1'], 'L0_ffn_w_s2': _L0_ffn_in['w_s2'], 'L0_ffn_b_s2': _L0_ffn_in['b_s2'], 'L0_ffn_shared_weight': _L0_ffn_in['shared_weight'], 'L0_ffn_w_f1': _L0_ffn_in['w_f1'], 'L0_ffn_b_f1': _L0_ffn_in['b_f1'], 'L0_ffn_w_f2': _L0_ffn_in['w_f2'], 'L0_ffn_b_f2': _L0_ffn_in['b_f2'], 'L0_ffn_integration_weight': _L0_ffn_in['integration_weight'], 'L0_ffn_mu': _L0_ffn_in['mu'], 'L1_xattn_Wq': _L1_xattn_in['Wq'], 'L1_xattn_bq': _L1_xattn_in['bq'], 'L1_xattn_Wk': _L1_xattn_in['Wk'], 'L1_xattn_bk': _L1_xattn_in['bk'], 'L1_xattn_Wv': _L1_xattn_in['Wv'], 'L1_xattn_bv': _L1_xattn_in['bv'], 'L1_xattn_Wo': _L1_xattn_in['Wo'], 'L1_xattn_bo': _L1_xattn_in['bo'], 'L1_xattn_w1': _L1_xattn_in['w1'], 'L1_xattn_b1': _L1_xattn_in['b1'], 'L1_xattn_w2': _L1_xattn_in['w2'], 'L1_xattn_b2': _L1_xattn_in['b2'], 'L1_xattn_w3': _L1_xattn_in['w3'], 'L1_xattn_b3': _L1_xattn_in['b3'], 'L1_ffn_router_w': _L1_ffn_in['router_w'], 'L1_ffn_w1': _L1_ffn_in['w1'], 'L1_ffn_b1': _L1_ffn_in['b1'], 'L1_ffn_w2': _L1_ffn_in['w2'], 'L1_ffn_b2': _L1_ffn_in['b2'], 'L2_xattn_Wq1': _L2_xattn_in['Wq1'], 'L2_xattn_Wk1': _L2_xattn_in['Wk1'], 'L2_xattn_Wv1': _L2_xattn_in['Wv1'], 'L2_xattn_Wq2': _L2_xattn_in['Wq2'], 'L2_xattn_Wk2': _L2_xattn_in['Wk2'], 'L2_xattn_Wv2': _L2_xattn_in['Wv2'], 'L2_xattn_fc1_w': _L2_xattn_in['fc1_w'], 'L2_xattn_fc1_b': _L2_xattn_in['fc1_b'], 'L2_xattn_fc2_w': _L2_xattn_in['fc2_w'], 'L2_xattn_fc2_b': _L2_xattn_in['fc2_b'], 'L2_xattn_ln1_g': _L2_xattn_in['ln1_g'], 'L2_xattn_ln1_b': _L2_xattn_in['ln1_b'], 'L2_xattn_ln2_g': _L2_xattn_in['ln2_g'], 'L2_xattn_ln2_b': _L2_xattn_in['ln2_b'], 'L2_xattn_ln3_g': _L2_xattn_in['ln3_g'], 'L2_xattn_ln3_b': _L2_xattn_in['ln3_b'], 'L2_ffn_w_q': _L2_ffn_in['w_q'], 'L2_ffn_keys': _L2_ffn_in['keys'], 'L2_ffn_expert_down': _L2_ffn_in['expert_down'], 'L2_ffn_expert_up': _L2_ffn_in['expert_up'], 'L2_ffn_norm_w': _L2_ffn_in['norm_w'], 'L3_xattn_Wq': _L3_xattn_in['Wq'], 'L3_xattn_Wk': _L3_xattn_in['Wk'], 'L3_xattn_Wv': _L3_xattn_in['Wv'], 'L3_xattn_Wo': _L3_xattn_in['Wo'], 'L3_xattn_bo': _L3_xattn_in['bo'], 'L3_ffn_weight': _L3_ffn_in['weight'], 'L3_ffn_gate_w': _L3_ffn_in['gate_w'], 'L3_ffn_lora_U': _L3_ffn_in['lora_U'], 'L3_ffn_lora_V': _L3_ffn_in['lora_V']}

def reference(x, ctx_1024, mask_BxS2_bk0, L0_xattn_wq, L0_xattn_bq, L0_xattn_wk, L0_xattn_bk, L0_xattn_wv, L0_xattn_bv, L0_xattn_wo, L0_xattn_bo, L0_ffn_w_r1, L0_ffn_b_r1, L0_ffn_w_r2, L0_ffn_b_r2, L0_ffn_w_h1, L0_ffn_b_h1, L0_ffn_w_h2, L0_ffn_b_h2, L0_ffn_expert_w1, L0_ffn_expert_b1, L0_ffn_expert_w2, L0_ffn_expert_b2, L0_ffn_w_s1, L0_ffn_b_s1, L0_ffn_w_s2, L0_ffn_b_s2, L0_ffn_shared_weight, L0_ffn_w_f1, L0_ffn_b_f1, L0_ffn_w_f2, L0_ffn_b_f2, L0_ffn_integration_weight, L0_ffn_mu, L1_xattn_Wq, L1_xattn_bq, L1_xattn_Wk, L1_xattn_bk, L1_xattn_Wv, L1_xattn_bv, L1_xattn_Wo, L1_xattn_bo, L1_xattn_w1, L1_xattn_b1, L1_xattn_w2, L1_xattn_b2, L1_xattn_w3, L1_xattn_b3, L1_ffn_router_w, L1_ffn_w1, L1_ffn_b1, L1_ffn_w2, L1_ffn_b2, L2_xattn_Wq1, L2_xattn_Wk1, L2_xattn_Wv1, L2_xattn_Wq2, L2_xattn_Wk2, L2_xattn_Wv2, L2_xattn_fc1_w, L2_xattn_fc1_b, L2_xattn_fc2_w, L2_xattn_fc2_b, L2_xattn_ln1_g, L2_xattn_ln1_b, L2_xattn_ln2_g, L2_xattn_ln2_b, L2_xattn_ln3_g, L2_xattn_ln3_b, L2_ffn_w_q, L2_ffn_keys, L2_ffn_expert_down, L2_ffn_expert_up, L2_ffn_norm_w, L3_xattn_Wq, L3_xattn_Wk, L3_xattn_Wv, L3_xattn_Wo, L3_xattn_bo, L3_ffn_weight, L3_ffn_gate_w, L3_ffn_lora_U, L3_ffn_lora_V):
    import jax
    import jax.numpy as jnp

    def _L0_xattn_ref(x, y, mask, wq, bq, wk, bk, wv, bv, wo, bo):
        import math
        import jax, jax.numpy as jnp
        import numpy as np
        B, S, T, H, A, NH = (4, 256, 256, 128, 128, 16)
        HD = A // NH
        b, s, _ = x.shape
        t = y.shape[1]
        q = (x @ wq + bq).reshape(b, s, NH, HD).transpose(0, 2, 1, 3)
        k = (y @ wk + bk).reshape(b, t, NH, HD).transpose(0, 2, 1, 3)
        v = (y @ wv + bv).reshape(b, t, NH, HD).transpose(0, 2, 1, 3)
        attn = jnp.einsum('bhsd,bhtd->bhst', q, k) / math.sqrt(HD)
        m = mask[:, None, None, :].astype(attn.dtype)
        attn = attn * m - 100000.0 * (1.0 - m)
        attn = jax.nn.softmax(attn, axis=-1)
        o = jnp.einsum('bhst,bhtd->bhsd', attn, v)
        o = o.transpose(0, 2, 1, 3).reshape(b, s, NH * HD)
        return o @ wo + bo

    def _L0_ffn_ref(x, w_r1, b_r1, w_r2, b_r2, w_h1, b_h1, w_h2, b_h2, expert_w1, expert_b1, expert_w2, expert_b2, w_s1, b_s1, w_s2, b_s2, shared_weight, w_f1, b_f1, w_f2, b_f2, integration_weight, mu):
        import jax, jax.numpy as jnp
        import numpy as np
        D = 128
        E = 8
        K = 2
        NUM_ITER = 2
        DT = 0.1
        H = 64
        CTX = 2 * D

        def _gelu(t):
            return jax.nn.gelu(t, approximate=False)

        def _inl(ctrl, x, v, mu):
            alpha_raw, beta_raw, gate_raw = jnp.split(ctrl, 3, axis=-1)
            alpha = jax.nn.sigmoid(alpha_raw)
            beta = jax.nn.softplus(beta_raw)
            gate = jax.nn.sigmoid(gate_raw)
            error = x - mu
            v_next = alpha * v - beta * error
            x_next = x + DT * gate * v_next
            return (x_next, v_next)
        B, N, Dm = x.shape
        xf = x.reshape(B * N, Dm)
        logits = _gelu(xf @ w_r1 + b_r1) @ w_r2 + b_r2
        probs = jax.nn.softmax(logits, axis=-1)
        top_p, top_i = jax.lax.top_k(probs, K)
        top_p = top_p / jnp.sum(top_p, axis=-1, keepdims=True)
        flat_idx = top_i.reshape(-1)
        flat_w = top_p.reshape(-1, 1)
        v = jnp.zeros_like(xf)
        integrated = xf
        for _ in range(NUM_ITER):
            ctx = jnp.concatenate([integrated, v], axis=-1)
            shared_ctrl = _gelu(ctx @ w_s1 + b_s1) @ w_s2 + b_s2
            x_shared, v_shared = _inl(shared_ctrl, integrated, v, mu)
            sw = jax.nn.sigmoid(shared_weight)
            ctx_e = jnp.repeat(ctx, K, axis=0)
            x_e = jnp.repeat(integrated, K, axis=0)
            v_e = jnp.repeat(v, K, axis=0)
            w1 = expert_w1[flat_idx]
            b1 = expert_b1[flat_idx]
            w2 = expert_w2[flat_idx]
            b2 = expert_b2[flat_idx]
            hidden = _gelu(jnp.einsum('tc,tch->th', ctx_e, w1) + b1)
            ctrl = jnp.einsum('th,tho->to', hidden, w2) + b2
            x_r, v_r = _inl(ctrl, x_e, v_e, mu)
            x_r = (x_r * flat_w).reshape(B * N, K, Dm).sum(axis=1)
            v_r = (v_r * flat_w).reshape(B * N, K, Dm).sum(axis=1)
            x_next = sw * x_shared + (1.0 - sw) * x_r
            v_next = sw * v_shared + (1.0 - sw) * v_r
            halt = jax.nn.sigmoid(_gelu(x_next @ w_h1 + b_h1) @ w_h2 + b_h2)
            refined = _gelu(x_next @ w_f1 + b_f1) @ w_f2 + b_f2
            integrated = integrated + halt * refined * integration_weight
            v = v_next
        return integrated.reshape(B, N, Dm)

    def _L1_xattn_ref(query, key, value, Wq, bq, Wk, bk, Wv, bv, Wo, bo, w1, b1, w2, b2, w3, b3):
        import jax, jax.numpy as jnp
        import numpy as np
        import math
        B, S, D, H = (1, 256, 128, 16)
        DK = D // H
        DH = 64
        LOG_T_MIN = math.log(0.1)
        LOG_T_MAX = math.log(10.0)

        def _linear(x, W, b):
            return x @ W.T + b
        b, sq, d = query.shape
        sk = key.shape[1]
        h, dk = (H, DK)
        Q = _linear(query, Wq, bq).reshape(b, sq, h, dk).transpose(0, 2, 1, 3)
        K = _linear(key, Wk, bk).reshape(b, sk, h, dk).transpose(0, 2, 1, 3)
        V = _linear(value, Wv, bv).reshape(b, sk, h, dk).transpose(0, 2, 1, 3)
        qk = jnp.einsum('bhqd,bhkd->bhqk', Q, K)
        scores = qk / math.sqrt(dk)
        mean_sim = scores.mean(axis=(-2, -1))
        max_sim = scores.max(axis=-1).mean(axis=-1)
        probs = jax.nn.softmax(scores, axis=-1)
        entropy_proxy = jnp.var(probs, axis=-1, ddof=1).mean(axis=-1)
        feats = jnp.stack([mean_sim, max_sim, entropy_proxy], axis=-1)
        hidden = jax.nn.gelu(_linear(feats, w1, b1), approximate=False)
        hidden = jax.nn.gelu(_linear(hidden, w2, b2), approximate=False)
        log_t = jnp.clip(_linear(hidden, w3, b3), LOG_T_MIN, LOG_T_MAX)
        t = jnp.exp(log_t)[..., None]
        attn_scores = qk / (2.0 * t)
        attn = jax.nn.softmax(attn_scores, axis=-1)
        attn = jnp.nan_to_num(attn, nan=0.0)
        out = jnp.einsum('bhqk,bhkd->bhqd', attn, V)
        out = out.transpose(0, 2, 1, 3).reshape(b, sq, d)
        return _linear(out, Wo, bo)

    def _L1_ffn_ref(h, router_w, w1, b1, w2, b2):
        import jax, jax.numpy as jnp
        import numpy as np
        B, S, D, E, F = (2, 256, 128, 14, 256)
        Bb, Ss, Dd = h.shape
        x = h.reshape(-1, Dd)
        logits = x @ router_w
        assignments = jnp.argmax(logits, axis=-1)
        probs = jax.nn.softmax(logits, axis=-1)
        weights = jnp.take_along_axis(probs, assignments[:, None], axis=1)[:, 0]
        hid = jnp.einsum('nd,edf->nef', x, w1) + b1
        hid = jax.nn.gelu(hid, approximate=False)
        all_out = jnp.einsum('nef,efd->ned', hid, w2) + b2
        sel = jnp.take_along_axis(all_out, assignments[:, None, None], axis=1)[:, 0, :]
        moe_out = (sel * weights[:, None]).reshape(Bb, Ss, Dd)
        return moe_out

    def _L2_xattn_ref(x, context, Wq1, Wk1, Wv1, Wq2, Wk2, Wv2, fc1_w, fc1_b, fc2_w, fc2_b, ln1_g, ln1_b, ln2_g, ln2_b, ln3_g, ln3_b):
        import jax, jax.numpy as jnp
        import numpy as np
        E = 128
        NUM_HEADS = 16
        DK = E // NUM_HEADS
        EPS = 1e-05
        NEG_INF = -jnp.inf

        def layer_norm(x, g, b):
            mu = jnp.mean(x, axis=-1, keepdims=True)
            var = jnp.var(x, axis=-1, keepdims=True)
            return (x - mu) * jax.lax.rsqrt(var + EPS) * g + b

        def self_attn(x, Wq, Wk, Wv):
            Q, K, V = (x @ Wq, x @ Wk, x @ Wv)
            energy = jnp.einsum('bqd,bkd->bqk', Q, K)
            S = energy.shape[-1]
            lengths = jnp.sum(energy[:, 0] != 0, axis=-1)
            kidx = jnp.arange(S)
            pad = kidx[None, None, :] >= lengths[:, None, None]
            causal = kidx[None, :] < kidx[:, None]
            causal = (kidx[None, :] > kidx[:, None])[None]
            energy = jnp.where(pad | causal, NEG_INF, energy)
            score = jax.nn.softmax(energy / np.sqrt(DK), axis=-1)
            return jnp.einsum('bqk,bkd->bqd', score, V)

        def cross_attn(x, context, Wq, Wk, Wv):
            Q = x @ Wq
            K, V = (context @ Wk, context @ Wv)
            energy = jnp.einsum('bqd,bkd->bqk', Q, K)
            Sk = energy.shape[-1]
            lengths = jnp.sum(energy[:, 0] != 0, axis=-1)
            kidx = jnp.arange(Sk)
            pad = kidx[None, None, :] >= lengths[:, None, None]
            energy = jnp.where(pad, NEG_INF, energy)
            score = jax.nn.softmax(energy / np.sqrt(DK), axis=-1)
            return jnp.einsum('bqk,bkd->bqd', score, V)
        z = self_attn(x, Wq1, Wk1, Wv1)
        x = layer_norm(x + z, ln1_g, ln1_b)
        z = cross_attn(x, context, Wq2, Wk2, Wv2)
        x = layer_norm(x + z, ln2_g, ln2_b)
        z = jax.nn.relu(x @ fc1_w + fc1_b)
        z = z @ fc2_w + fc2_b
        return layer_norm(x + z, ln3_g, ln3_b)

    def _L2_ffn_ref(x, w_q, keys, expert_down, expert_up, norm_w):
        import jax, jax.numpy as jnp
        import numpy as np
        B, T, D = (2, 128, 128)
        H, DK, K = (8, 128, 8)
        NKEYS = 32
        NEXP = NKEYS * NKEYS

        def _rmsnorm(x, w, eps=1e-06):
            inv = jax.lax.rsqrt(jnp.mean(x * x, axis=-1, keepdims=True) + eps)
            return x * inv * w
        b, t, d = x.shape
        xn = _rmsnorm(x, norm_w)
        q = (xn @ w_q.T).reshape(b, t, H, 2, DK)
        sim1 = jnp.einsum('bthd,hkd->bthk', q[..., 0, :], keys[:, :, 0, :])
        sim2 = jnp.einsum('bthd,hkd->bthk', q[..., 1, :], keys[:, :, 1, :])
        s1, i1 = jax.lax.top_k(sim1, K)
        s2, i2 = jax.lax.top_k(sim2, K)
        all_idx = (i1[..., :, None] * NKEYS + i2[..., None, :]).reshape(b, t, H, K * K)
        all_sc = (s1[..., :, None] + s2[..., None, :]).reshape(b, t, H, K * K)
        fs, pk = jax.lax.top_k(all_sc, K)
        fi = jnp.take_along_axis(all_idx, pk, axis=-1)
        wd = expert_down[fi]
        wu = expert_up[fi]
        hidden = jax.nn.gelu(jnp.einsum('btd,bthkd->bthk', xn, wd), approximate=False)
        hidden = hidden * jax.nn.relu(fs)
        return jnp.einsum('bthk,bthkd->btd', hidden, wu)

    def _L3_xattn_ref(querys, keys, values, Wq, Wk, Wv, Wo, bo):
        import jax, jax.numpy as jnp
        import numpy as np
        N_HEAD = 16
        B, T, D = querys.shape
        H = N_HEAD
        Hd = D // H

        def split(x, W):
            return (x @ W.T).reshape(B, T, H, Hd).transpose(0, 2, 1, 3)
        q = split(querys, Wq)
        k = split(keys, Wk)
        v = split(values, Wv)
        scale = 1.0 / jnp.sqrt(jnp.array(Hd, jnp.float32))
        scores = jnp.einsum('bhqd,bhkd->bhqk', q, k) * scale
        causal = jnp.tril(jnp.ones((T, T), bool))
        scores = jnp.where(causal[None, None], scores, -jnp.inf)
        weights = jax.nn.softmax(scores, axis=-1)
        attn = jnp.einsum('bhqk,bhkd->bhqd', weights, v)
        out = attn.transpose(0, 2, 1, 3).reshape(B, T, D)
        return out @ Wo.T + bo

    def _L3_ffn_ref(x, weight, gate_w, lora_U, lora_V):
        import jax, jax.numpy as jnp
        import numpy as np
        scaling = 1.0 / lora_U.shape[1]
        B, S, D_in = x.shape
        xt = x.reshape(-1, D_in)
        gate = jax.nn.softmax(xt @ gate_w.T, axis=-1)
        base = xt @ weight.T
        t = jnp.einsum('nh,erh->ner', xt, lora_U)
        lora = jnp.einsum('ne,eor,ner->no', gate, lora_V, t)
        out = base + scaling * lora
        return out.reshape(B, S, -1)
    x = x + _L0_xattn_ref(_layernorm(x, axis=-1), ctx_1024, mask_BxS2_bk0, L0_xattn_wq, L0_xattn_bq, L0_xattn_wk, L0_xattn_bk, L0_xattn_wv, L0_xattn_bv, L0_xattn_wo, L0_xattn_bo)
    x = x + _L0_ffn_ref(_layernorm(x, axis=-1), L0_ffn_w_r1, L0_ffn_b_r1, L0_ffn_w_r2, L0_ffn_b_r2, L0_ffn_w_h1, L0_ffn_b_h1, L0_ffn_w_h2, L0_ffn_b_h2, L0_ffn_expert_w1, L0_ffn_expert_b1, L0_ffn_expert_w2, L0_ffn_expert_b2, L0_ffn_w_s1, L0_ffn_b_s1, L0_ffn_w_s2, L0_ffn_b_s2, L0_ffn_shared_weight, L0_ffn_w_f1, L0_ffn_b_f1, L0_ffn_w_f2, L0_ffn_b_f2, L0_ffn_integration_weight, L0_ffn_mu)
    x = x + _L1_xattn_ref(_layernorm(x, axis=-1), ctx_1024, ctx_1024, L1_xattn_Wq, L1_xattn_bq, L1_xattn_Wk, L1_xattn_bk, L1_xattn_Wv, L1_xattn_bv, L1_xattn_Wo, L1_xattn_bo, L1_xattn_w1, L1_xattn_b1, L1_xattn_w2, L1_xattn_b2, L1_xattn_w3, L1_xattn_b3)
    x = x + _L1_ffn_ref(_layernorm(x, axis=-1), L1_ffn_router_w, L1_ffn_w1, L1_ffn_b1, L1_ffn_w2, L1_ffn_b2)
    x = x + _L2_xattn_ref(_layernorm(x, axis=-1), ctx_1024, L2_xattn_Wq1, L2_xattn_Wk1, L2_xattn_Wv1, L2_xattn_Wq2, L2_xattn_Wk2, L2_xattn_Wv2, L2_xattn_fc1_w, L2_xattn_fc1_b, L2_xattn_fc2_w, L2_xattn_fc2_b, L2_xattn_ln1_g, L2_xattn_ln1_b, L2_xattn_ln2_g, L2_xattn_ln2_b, L2_xattn_ln3_g, L2_xattn_ln3_b)
    x = x + _L2_ffn_ref(_layernorm(x, axis=-1), L2_ffn_w_q, L2_ffn_keys, L2_ffn_expert_down, L2_ffn_expert_up, L2_ffn_norm_w)
    x = x + _L3_xattn_ref(_layernorm(x, axis=-1), ctx_1024, ctx_1024, L3_xattn_Wq, L3_xattn_Wk, L3_xattn_Wv, L3_xattn_Wo, L3_xattn_bo)
    x = x + _L3_ffn_ref(_layernorm(x, axis=-1), L3_ffn_weight, L3_ffn_gate_w, L3_ffn_lora_U, L3_ffn_lora_V)
    return x

_drawn_inputs = setup_inputs


def setup_inputs(seed=0):
    import zlib

    import numpy as np

    out = dict(_drawn_inputs(seed))
    spreads = {'L0_xattn_bq': (0.0, 0.1),
     'L0_xattn_bk': (0.0, 2.0),
     'L0_xattn_bv': (0.0, 0.1),
     'L0_xattn_bo': (0.0, 0.1),
     'L0_ffn_b_r1': (0.0, 0.8),
     'L0_ffn_b_r2': (0.0, 0.8),
     'L0_ffn_b_h1': (0.0, 0.8),
     'L0_ffn_expert_b1': (0.0, 0.8),
     'L0_ffn_expert_b2': (0.0, 0.8),
     'L0_ffn_b_s1': (0.0, 0.8),
     'L0_ffn_b_s2': (0.0, 0.8),
     'L0_ffn_b_f1': (0.0, 0.8),
     'L0_ffn_b_f2': (0.0, 0.275),
     'L0_ffn_integration_weight': (0.5, 0.6),
     'L0_ffn_mu': (0.0, 0.8),
     'L1_ffn_b1': (0.0, 0.8),
     'L1_ffn_b2': (0.0, 0.8),
     'L2_xattn_fc1_b': (0.0, 0.385),
     'L2_xattn_fc2_b': (0.0, 0.1),
     'L2_xattn_ln1_g': (1.0, 0.2),
     'L2_xattn_ln1_b': (0.0, 0.1),
     'L2_xattn_ln2_g': (1.0, 0.2),
     'L2_xattn_ln2_b': (0.0, 0.1),
     'L2_xattn_ln3_g': (1.0, 0.2),
     'L2_xattn_ln3_b': (0.0, 0.1),
     'L2_ffn_norm_w': (1.0, 0.6),
     'L3_xattn_bo': (0.0, 2.0)}
    factors = {'L0_ffn_w_r1': 8.0,
     'L0_ffn_w_r2': 8.0,
     'L0_ffn_w_h1': 8.0,
     'L0_ffn_w_h2': 8.0,
     'L0_ffn_expert_w1': 8.0,
     'L0_ffn_expert_w2': 8.0,
     'L0_ffn_w_s1': 8.0,
     'L0_ffn_w_s2': 8.0,
     'L0_ffn_w_f1': 4.953,
     'L0_ffn_w_f2': 4.41,
     'L1_xattn_Wq': 8.0,
     'L1_xattn_bq': 8.0,
     'L1_xattn_Wk': 8.0,
     'L1_xattn_bk': 64.0,
     'L1_xattn_Wv': 3.554,
     'L1_xattn_bv': 8.0,
     'L1_xattn_Wo': 3.477,
     'L1_xattn_bo': 4.413,
     'L1_xattn_w1': 8.0,
     'L1_xattn_b1': 8.0,
     'L1_xattn_w2': 8.0,
     'L1_xattn_b2': 8.0,
     'L1_xattn_w3': 8.0,
     'L2_ffn_w_q': 8.0,
     'L2_ffn_keys': 8.0,
     'L2_ffn_expert_down': 8.0,
     'L2_ffn_expert_up': 8.0,
     'L3_xattn_Wq': 8.0,
     'L3_xattn_Wk': 8.0,
     'L3_xattn_Wv': 5.804,
     'L3_xattn_Wo': 5.991,
     'L3_ffn_gate_w': 8.0,
     'L3_ffn_lora_U': 5.584,
     'L3_ffn_lora_V': 5.578}
    for name, (base, spread) in spreads.items():
        noise = np.random.default_rng([zlib.crc32(name.encode()), seed]).standard_normal(out[name].shape)
        drawn = base * np.exp(spread * noise) if base else spread * noise
        out[name] = jnp.asarray(drawn.astype(out[name].dtype))
    for name, factor in factors.items():
        out[name] = (out[name] * factor).astype(out[name].dtype)
    return out
```

```python
import concourse.bass as bass
from concourse import mybir
from contextlib import ExitStack, contextmanager
import math

F32 = mybir.dt.float32
BF16 = mybir.dt.bfloat16
U8 = mybir.dt.uint8
U32 = mybir.dt.uint32
ALU = mybir.AluOpType
ACT = mybir.ActivationFunctionType
AX = mybir.AxisListType

B, S, D = 16, 128, 128
NH, HD = 16, 8
P = 128
T = 2
G = 4
J = 2
ROW_MAX, ROW_MASK = 8, 9
SCORE_SCALE = float(HD) ** -0.5
MASKED = 100000.0
NEG = -1.0e30
LN_EPS, RMS_EPS = 1e-5, 1e-6
LOG_T_MIN, LOG_T_MAX = math.log(0.1), math.log(10.0)
CH = 512
NCH = B * S // CH


@contextmanager
def cleared_semaphores(nc):
    taken = []

    def new_semaphore(name):
        taken.append(nc.alloc_semaphore(name=name))
        return taken[-1]

    yield new_semaphore
    nc.clear_and_free_semaphores(taken)
    nc.all_engine_barrier()


class Banks:

    def __init__(self, names, banks, filled, freed):
        self.place = {}
        self.per_pass = [0] * len(banks)
        for n, name in enumerate(names):
            k = n % len(banks)
            self.place[name] = (k, self.per_pass[k])
            self.per_pass[k] += 1
        self.banks, self.filled, self.freed = banks, filled, freed

    def bank(self, name):
        return self.banks[self.place[name][0]]

    def _value(self, name, i):
        k, n = self.place[name]
        return k, i * self.per_pass[k] + n + 1

    def wait_free(self, pe, name, i):
        k, value = self._value(name, i)
        pe.wait_ge(self.freed[k], value)

    def fill(self, ins, name):
        ins.then_inc(self.filled[self.place[name][0]], 1)

    def wait_filled(self, eng, name, i):
        k, value = self._value(name, i)
        eng.wait_ge(self.filled[k], value)

    def free(self, ins, name):
        ins.then_inc(self.freed[self.place[name][0]], 1)

    def wait_freed(self, eng, name, i):
        k, value = self._value(name, i)
        eng.wait_ge(self.freed[k], value + 1)


class Chain:

    def __init__(self, eng, sem, per_pass):
        self.eng, self.sem, self.per_pass = eng, sem, per_pass
        self.i, self.n = 0, 0

    def begin(self, i):
        self.i, self.n = i, 0

    def __call__(self, ins):
        self.n += 1
        ins.then_inc(self.sem, 1)
        self.eng.wait_ge(self.sem, self.i * self.per_pass + self.n)

    def end(self):
        assert self.n == self.per_pass, (self.n, self.per_pass)


def layernorm(nc, m, tag, rms_gain=None):
    x, xnT, identity = m["x"], m["xnT"], m["identity"]
    with cleared_semaphores(nc) as new_semaphore, ExitStack() as ctx:
        def sb(name, shape):
            return ctx.enter_context(nc.sbuf_tensor(f"{tag}_{name}", shape, F32))

        def sem(name):
            return new_semaphore(f"{tag}_{name}")

        stats = sb("stats", [P, B, 6])
        mean_var = sb("mean_var", [P, B, 2])
        var_eps, square = sb("var_eps", [P, B]), sb("square", [P, B])
        rstd = sb("rstd", [P, B])
        xn = [sb(f"xn{k}", [P, 4, D]) for k in range(2)]
        flipped = [ctx.enter_context(nc.psum_tensor(f"{tag}_flipped{k}", [P, 4, S], F32)) for k in range(2)]
        stats_made = sem("stats_made")
        aggregated = sem("aggregated")
        eps_added = sem("eps_added")
        rstd_made = sem("rstd_made")
        xn_made = [sem(f"xn_made{k}") for k in range(2)]
        xn_flipped = [sem(f"xn_flipped{k}") for k in range(2)]
        xnT_stored = [sem(f"xnT_stored{k}") for k in range(2)]
        block = ctx.enter_context(nc.Block())

        @block.vector
        def _(dve):
            with dve.Fori(0, B) as b:
                nc.vector.bn_stats(stats[:, b, :], x[:, b, :]).then_inc(stats_made, 1)
            dve.wait_ge(stats_made, B)
            for b in range(B):
                nc.vector.bn_aggr(mean_var[:, b, :], stats[:, b, :]).then_inc(aggregated, 1)
            dve.wait_ge(rstd_made, 1)
            with dve.Fori(0, 2) as i:
                for k in range(2):
                    dve.wait_ge(xn_flipped[k], i * 4 + 1)
                    for q in range(4):
                        b = i * 8 + k * 4 + q
                        nc.vector.tensor_scalar(xn[k][:, q, :], x[:, b, :], mean_var[:, b, 0:1],
                                                rstd[:, bass.ds(b, 1)], ALU.subtract, ALU.mult) \
                            .then_inc(xn_made[k], 1)

        @block.gpsimd
        def _(pool):
            pool.wait_ge(aggregated, B)
            nc.gpsimd.tensor_scalar(var_eps[:, :], mean_var[:, :, 1], LN_EPS, None, ALU.add) \
                .then_inc(eps_added, 1)
            pool.wait_ge(eps_added, 1)
            if rms_gain is None:
                nc.gpsimd.tensor_tensor(rstd[:, :], var_eps[:, :], m["minus_half"][:, 0:B], ALU.pow) \
                    .then_inc(rstd_made, 1)
            else:
                own = Chain(pool, eps_added, 0)
                own.n = 1
                TT = nc.gpsimd.tensor_tensor
                own(TT(rstd[:, :], var_eps[:, :], m["minus_half"][:, 0:B], ALU.pow))
                own(TT(square[:, :], rstd[:, :], rstd[:, :], ALU.mult))
                own(TT(square[:, :], square[:, :], mean_var[:, :, 1], ALU.mult))
                own(nc.gpsimd.tensor_scalar(square[:, :], square[:, :], RMS_EPS, None, ALU.add))
                own(TT(var_eps[:, :], square[:, :], m["minus_half"][:, 0:B], ALU.pow))
                TT(rstd[:, :], rstd[:, :], var_eps[:, :], ALU.mult).then_inc(rstd_made, 1)

        @block.tensor
        def _(pe):
            for k in range(2):
                pe.sem_inc(xn_flipped[k], 1)
            with pe.Fori(0, 2) as i:
                for k in range(2):
                    pe.wait_ge(xnT_stored[k], i + 1)
                    for q in range(4):
                        pe.wait_ge(xn_made[k], i * 4 + q + 1)
                        nc.tensor.transpose(flipped[k][:, q, :], xn[k][:, q, :], identity[:, :]) \
                            .then_inc(xn_flipped[k], 1)

        @block.scalar
        def _(act):
            for k in range(2):
                act.sem_inc(xnT_stored[k], 1)
            with act.Fori(0, 2) as i:
                for k in range(2):
                    act.wait_ge(xn_flipped[k], i * 4 + 5)
                    out = xnT[:, bass.ds(i * 8 + k * 4, 4), :]
                    if rms_gain is None:
                        ins = nc.scalar.copy(out, flipped[k][:, :, :])
                    else:
                        ins = nc.scalar.activation(out, flipped[k][:, :, :], ACT.Copy, scale=rms_gain[:, 0:1])
                    ins.then_inc(xnT_stored[k], 1)


def multihead(nc, m, w, tag, meanwhile, masked_keys=False, causal=False, tempered=False):
    x, xnT, ctxT, identity = m["x"], m["xnT"], m["ctxT"], m["identity"]
    layernorm(nc, m, tag + "_ln")
    with cleared_semaphores(nc) as new_semaphore, ExitStack() as ctx:
        def sb(name, shape, dt=F32):
            return ctx.enter_context(nc.sbuf_tensor(f"{tag}_{name}", shape, dt))

        def ps(name, shape):
            return ctx.enter_context(nc.psum_tensor(f"{tag}_{name}", shape, F32))

        def sem(name):
            return new_semaphore(f"{tag}_{name}")

        ctx_b = sb("ctx_b", [P, S])
        q = sb("q", [P, T, J, S])
        q_less_max = sb("q_less_max", [P, T, J, S])
        k = sb("k", [P, T, S])
        v = sb("v", [P, T, J, P])
        neg_max = sb("neg_max", [P, T, J, P])
        probs = sb("probs", [P, G, T, J, S])
        o = sb("o", [P, T, S])
        recip = sb("recip", [P, T, S])
        o_norm = sb("o_norm", [P, T, S])

        scores = [ps(f"scores{g}", [P, T, J, S]) for g in range(G)]
        q_ps = ps("q_ps", [P, T, J, S])
        v_ps = ps("v_ps", [P, T, J, P])
        k_ps = ps("k_ps", [P, 4, S])
        o_ps = ps("o_ps", [P, 4, S])

        ready = sem("ready")
        ctx_copied = sem("ctx_copied")
        q_projected, k_projected, v_projected = sem("q_projected"), sem("k_projected"), sem("v_projected")
        q_stored, k_stored, v_stored = sem("q_stored"), sem("k_stored"), sem("v_stored")
        scored, max_taken = sem("scored"), sem("max_taken")
        max_flipped, q_shifted = sem("max_flipped"), sem("q_shifted")
        shifted_scored, exp_done = sem("shifted_scored"), sem("exp_done")
        pv_done, o_stored, sums_spread = sem("pv_done"), sem("o_stored"), sem("sums_spread")
        recip_done, o_scaled, projected, added = sem("recip_done"), sem("o_scaled"), sem("projected"), sem("added")
        if masked_keys:
            key_mask = sb("key_mask", [P, B, S])
            mask_read, k_biased = sem("mask_read"), sem("k_biased")
        if tempered:
            squares = sb("squares", [P, G, T, J, S])
            q_sums, k_sums = sb("q_sums", [P, T, J]), sb("k_sums", [P, T])
            q_sum2, qk_sum = sb("q_sum2", [P, T]), sb("qk_sum", [P, T])
            zi, zi2 = sb("zi", [P, T, S]), sb("zi2", [P, T, S])
            ratio = sb("ratio", [P, T, S])
            feats = sb("feats", [P, T, 3])
            max_sum = sb("max_sum", [P, T])
            feats_t = sb("feats_t", [3, T, 8])
            h1, h2 = sb("h1", [64, NH]), sb("h2", [64, NH])
            log_t = sb("log_t", [P, NH])
            inv_2t, own = sb("inv_2t", [P, NH]), sb("own", [P, T, 8])
            row_scale = sb("row_scale", [P, T])
            q_tempered = sb("q_tempered", [P, T, J, S])
            squared, summed, z_read = sem("squared"), sem("summed"), sem("z_read")
            small, small_ps = sem("small"), sem("small_ps")
            net_act = sem("net_act")
            tempered_q, tempered_scored, temper_exp = sem("tempered_q"), sem("tempered_scored"), sem("temper_exp")
            probs_clean = sem("probs_clean")
        exp_per_batch = G
        block = ctx.enter_context(nc.Block())

        @block.sync
        def _(sp):
            meanwhile(sp)

        @block.gpsimd
        def _(pool):
            nc.gpsimd.memset(neg_max[:, :, :, :], 0.0).then_inc(ready, 1)

            def copy_context(b):
                nc.gpsimd.tensor_copy(ctx_b[:, :], ctxT[:, b, :]).then_inc(ctx_copied, 1)

            copy_context(0)
            with pool.Fori(0, B - 1) as b:
                pool.wait_ge(v_projected, b + 1)
                copy_context(b + 1)

        @block.tensor
        def _(pe):
            def project(b):
                pe.wait_ge(ctx_copied, b + 1)
                for t in range(T):
                    for j in range(J):
                        ins = nc.tensor.matmul(q_ps[:, t, j, :], w["wq"][:, t, j, :], xnT[:, b, :],
                                               start=True, stop=True)
                ins.then_inc(q_projected, 1)
                for t in range(T):
                    ins = nc.tensor.matmul(k_ps[:, t, :], w["wk"][:, t, :], ctx_b[:, :], start=True, stop=True)
                ins.then_inc(k_projected, 1)
                nc.tensor.matmul(v_ps[:, :, :, :], ctx_b[:, :], w["wv"][:, :, :, :], start=True, stop=True) \
                    .then_inc(v_projected, 1)

            def score(b):
                pe.wait_ge(q_stored, b + 1)
                pe.wait_ge(k_stored, b + 1)
                if causal:
                    for g in range(G):
                        nc.tensor.matmul(scores[g][:, :, :, :], m["ident_bf"][:, :], m["future_bf"][:, :, :],
                                         start=True, stop=False, skip_group_check=True)
                for t in range(T):
                    for j in range(J):
                        for g in range(G):
                            r = slice(32 * g, 32 * g + 32)
                            ins = nc.tensor.matmul(scores[g][:, t, j, :], q[r, t, j, :], k[r, t, :],
                                                   start=not causal, stop=True, skip_group_check=True)
                ins.then_inc(scored, 1)

            def score_shifted(rows):
                if causal:
                    for g in range(G):
                        nc.tensor.matmul(scores[g][:, :, :, :], m["ident_bf"][:, :], m["past_bf"][:, :, :],
                                         start=True, stop=False, skip_group_check=True)
                for t in range(T):
                    for g in range(G):
                        r = slice(32 * g, 32 * g + 32)
                        ins = nc.tensor.matmul(scores[g][:, t, :, :], k[r, t, :], rows[r, t, :, :],
                                               start=not causal, stop=True, skip_group_check=True)
                return ins

            def sum_keys(out, weights, terms):
                for t in range(T):
                    for j in range(J):
                        for g in range(G):
                            r = slice(32 * g, 32 * g + 32)
                            ins = nc.tensor.matmul(out[r, t, :], weights(t, j, r), terms[:, g, t, j, :],
                                                   start=(j == 0), stop=(j == J - 1))
                return ins

            def shift(b):
                pe.wait_ge(max_taken, (b + 1) * G)
                for t in range(T):
                    for j in range(J):
                        ins = nc.tensor.transpose(q_ps[:, t, j, :], neg_max[:, t, j, :], identity[:, :])
                ins.then_inc(max_flipped, 1)
                pe.wait_ge(q_shifted, b + 1)
                score_shifted(q_less_max).then_inc(shifted_scored, 1)

            def temper(b):
                pe.wait_ge(exp_done, (b + 1) * G)
                sum_keys(o_ps[:, 0:2], lambda t, j, r: m["own_cols"][:, j, r], probs)
                pe.wait_ge(squared, (b + 1) * G)
                sum_keys(o_ps[:, 2:4], lambda t, j, r: m["own_cols"][:, j, r], squares).then_inc(summed, 1)
                c = v_ps[:, 0, 0, :]
                pe.wait_ge(v_stored, b + 1)
                for t in range(T):
                    for j in range(J):
                        nc.tensor.matmul(c[:, t:t + 1], neg_max[:, t, j, :], m["ones_col"][:, :],
                                         start=(j == 0), stop=(j == J - 1))
                pe.wait_ge(small, b * 5 + 1)
                nc.tensor.matmul(c[:, 2:4], m["head_rows"][:, :], qk_sum[:, :], start=True, stop=True) \
                    .then_inc(small_ps, 1)
                pe.wait_ge(small, b * 5 + 2)
                nc.tensor.matmul(c[:, 4:6], m["spread"][:, :], max_sum[:, :], start=True, stop=True) \
                    .then_inc(small_ps, 1)
                pe.wait_ge(small, b * 5 + 3)
                for t in range(T):
                    ins = nc.tensor.matmul(c[0:3, 8 + 8 * t:16 + 8 * t], feats[:, t, :], m["head_first"][:, :],
                                           start=True, stop=True)
                ins.then_inc(small_ps, 1)
                pe.wait_ge(small, b * 5 + 4)
                nc.tensor.matmul(c[0:64, 24:40], w["w1"][:, :], feats_t[:, :, :], start=True, stop=True) \
                    .then_inc(small_ps, 1)
                pe.wait_ge(net_act, b * 3 + 1)
                nc.tensor.matmul(c[:, 40:56], w["w2"][:, :], h1[:, :], start=True, stop=True) \
                    .then_inc(small_ps, 1)
                pe.wait_ge(net_act, b * 3 + 2)
                nc.tensor.matmul(c[:, 56:72], w["w3"][:, :], h2[:, :], start=True, stop=True) \
                    .then_inc(small_ps, 1)
                pe.wait_ge(tempered_q, b + 1)
                score_shifted(q_tempered).then_inc(tempered_scored, 1)

            def finish(b):
                if tempered:
                    pe.wait_ge(probs_clean, (b + 1) * G)
                    pe.wait_ge(z_read, b + 1)
                else:
                    pe.wait_ge(exp_done, (b + 1) * G)
                    pe.wait_ge(v_stored, b + 1)
                sum_keys(o_ps[:, 0:2], lambda t, j, r: v[:, t, j, r], probs).then_inc(pv_done, 1)
                pe.wait_ge(o_stored, b + 1)
                nc.tensor.matmul(o_ps[:, 2:4, :], m["spread"][:, :], o[:, :, :], start=True, stop=True) \
                    .then_inc(sums_spread, 1)
                pe.wait_ge(o_scaled, b + 1)
                for t in range(T):
                    ins = nc.tensor.matmul(k_ps[:, 2, :], o_norm[:, t, :], w["wo"][:, t, :],
                                           start=(t == 0), stop=(t == T - 1))
                ins.then_inc(projected, 1)

            pe.wait_ge(ready, 1)
            project(0)
            score(0)
            with pe.Fori(0, B - 1) as b:
                shift(b)
                if tempered:
                    temper(b)
                    finish(b)
                    pe.wait_ge(added, b + 1)
                    project(b + 1)
                    pe.wait_ge(temper_exp, (b + 1) * G)
                    score(b + 1)
                else:
                    pe.wait_ge(v_stored, b + 1)
                    project(b + 1)
                    pe.wait_ge(exp_done, (b + 1) * G)
                    score(b + 1)
                    finish(b)
            shift(B - 1)
            if tempered:
                temper(B - 1)
            finish(B - 1)

        @block.scalar
        def _(act):
            def store_q(b):
                act.wait_ge(q_projected, b + 1)
                for t in range(T):
                    for j in range(J):
                        ins = nc.scalar.activation(q[:, t, j, :], q_ps[:, t, j, :], ACT.Identity,
                                                   bias=w["bq"][:, t, j:j + 1],
                                                   **(dict(accum_out=q_sums[:, t, j:j + 1]) if tempered else {}))
                ins.then_inc(q_stored, 1)

            def exps(b):
                act.wait_ge(shifted_scored, b + 1)
                for g in range(G):
                    nc.scalar.activation(probs[:, g], scores[g][:, :, :, :], ACT.Exp, scale=SCORE_SCALE) \
                        .then_inc(exp_done, 1)

            def temper(b):
                for g in range(G):
                    act.wait_ge(exp_done, b * G + g + 1)
                    nc.scalar.activation(squares[:, g], probs[:, g], ACT.Square).then_inc(squared, 1)
                act.wait_ge(small_ps, b * 6 + 4)
                nc.scalar.activation(h1[:, :], v_ps[0:64, 0, 0, 24:40], ACT.Gelu, bias=w["b1"][:, 0:1]) \
                    .then_inc(net_act, 1)
                act.wait_ge(small_ps, b * 6 + 5)
                nc.scalar.activation(h2[:, :], v_ps[0:64, 0, 0, 40:56], ACT.Gelu, bias=w["b2"][:, 0:1]) \
                    .then_inc(net_act, 1)
                act.wait_ge(small, b * 5 + 5)
                nc.scalar.activation(inv_2t[:, :], log_t[:, :], ACT.Exp, scale=-1.0).then_inc(net_act, 1)
                act.wait_ge(tempered_scored, b + 1)
                for g in range(G):
                    nc.scalar.activation(probs[:, g], scores[g][:, :, :, :], ACT.Exp).then_inc(temper_exp, 1)

            def store_o(b):
                act.wait_ge(pv_done, b + 1)
                nc.scalar.copy(o[:, :, :], o_ps[:, 0:2, :]).then_inc(o_stored, 1)

            store_q(0)
            with act.Fori(0, B - 1) as b:
                exps(b)
                if tempered:
                    temper(b)
                    store_o(b)
                    store_q(b + 1)
                else:
                    store_q(b + 1)
                    store_o(b)
            exps(B - 1)
            if tempered:
                temper(B - 1)
            store_o(B - 1)

        @block.vector
        def _(dve):
            if masked_keys:
                nc.vector.tensor_scalar(key_mask[:, :, :], m["mask_bytes"][:, :, :].bitcast(U8), w["mask_mult"][:, 0:1],
                                        w["mask_add"][:, 0:1], ALU.mult, ALU.add).then_inc(mask_read, 1)
                dve.wait_ge(mask_read, 1)

            def store_k(b):
                dve.wait_ge(k_projected, b + 1)
                for t in range(T):
                    if masked_keys:
                        ins = nc.vector.scalar_tensor_tensor(k[:, t, :], k_ps[:, t, :], w["bk"][:, t:t + 1],
                                                             key_mask[:, b, :], ALU.add, ALU.mult)
                    else:
                        ins = nc.vector.tensor_scalar(k[:, t, :], k_ps[:, t, :], w["bk"][:, t:t + 1], None, ALU.add)
                ins.then_inc(k_stored, 1)

            def store_v(b):
                dve.wait_ge(v_projected, b + 1)
                nc.vector.tensor_tensor(v[:, :, :, :], v_ps[:, :, :, :], w["bv"][:, :, :, :], ALU.add) \
                    .then_inc(v_stored, 1)

            def take_max(b):
                dve.wait_ge(scored, b + 1)
                for g in range(G):
                    nc.vector.tensor_reduce(max_cols(g), scores[g][:, :, :, :], AX.X, ALU.max, negate=True) \
                        .then_inc(max_taken, 1)

            def max_cols(g):
                c = neg_max[:, :, :, :].rearrange("p t j c -> p t (j c)")
                first = 32 * g + ROW_MAX
                return c[:, :, first:first + P + 17:P + 16]

            def shift(b):
                dve.wait_ge(max_flipped, b + 1)
                nc.vector.tensor_tensor(q_less_max[:, :, :, :], q[:, :, :, :], q_ps[:, :, :, :], ALU.add) \
                    .then_inc(q_shifted, 1)

            def temper(b):
                c = v_ps[:, 0, 0, :]
                dve.wait_ge(k_stored, b + 1)
                dve.wait_ge(q_stored, b + 1)
                nc.vector.tensor_reduce(k_sums[:, :], k[:, :, :], AX.X, ALU.add)
                nc.vector.tensor_reduce(q_sum2[:, :], q_sums[:, :, :], AX.X, ALU.add).then_inc(dve_step, 1)
                dve.wait_ge(dve_step, b * 8 + 1)
                nc.vector.tensor_tensor(qk_sum[:, :], q_sum2[:, :], k_sums[:, :], ALU.mult).then_inc(small, 1)
                dve.wait_ge(small_ps, b * 6 + 1)
                nc.vector.tensor_scalar(feats[:, :, 0], c[:, 2:4], SCORE_SCALE / (S * S), None, ALU.mult)
                nc.vector.tensor_copy(max_sum[:, :], c[:, 0:2]).then_inc(small, 1)
                dve.wait_ge(small_ps, b * 6 + 2)
                nc.vector.tensor_scalar(feats[:, :, 1], c[:, 4:6], -SCORE_SCALE / S, None, ALU.mult)
                dve.wait_ge(summed, b + 1)
                nc.vector.reciprocal(zi[:, :, :], o_ps[:, 0:2, :]).then_inc(dve_step, 1)
                dve.wait_ge(dve_step, b * 8 + 2)
                nc.vector.tensor_tensor(zi2[:, :, :], zi[:, :, :], zi[:, :, :], ALU.mult).then_inc(dve_step, 1)
                dve.wait_ge(dve_step, b * 8 + 3)
                nc.vector.tensor_tensor(ratio[:, :, :], zi2[:, :, :], o_ps[:, 2:4, :], ALU.mult) \
                    .then_inc(z_read, 1)
                dve.wait_ge(z_read, b + 1)
                nc.vector.tensor_scalar(zi2[:, :, :], ratio[:, :, :], 1.0 / S, 1.0 / ((S - 1) * S),
                                        ALU.subtract, ALU.mult).then_inc(dve_step, 1)
                dve.wait_ge(dve_step, b * 8 + 4)
                nc.vector.tensor_reduce(feats[:, :, 2], zi2[:, :, :], AX.X, ALU.add).then_inc(small, 1)
                dve.wait_ge(small_ps, b * 6 + 3)
                nc.vector.tensor_copy(feats_t[:, :, :], c[0:3, 8:24].rearrange("p (t n) -> p t n", t=T)) \
                    .then_inc(small, 1)
                dve.wait_ge(small_ps, b * 6 + 6)
                nc.vector.tensor_scalar(log_t[:, :], c[:, 56:72], w["b3"][:, 0:1], LOG_T_MIN, ALU.add, ALU.max) \
                    .then_inc(dve_step, 1)
                dve.wait_ge(dve_step, b * 8 + 5)
                nc.vector.tensor_scalar(log_t[:, :], log_t[:, :], LOG_T_MAX, None, ALU.min).then_inc(small, 1)
                dve.wait_ge(net_act, b * 3 + 3)
                nc.vector.scalar_tensor_tensor(own[:, :, :], inv_2t[:, :].rearrange("p (t n) -> p t n", t=T), 0.5,
                                               m["row_head"][:, :, :], ALU.mult, ALU.mult).then_inc(dve_step, 1)
                dve.wait_ge(dve_step, b * 8 + 6)
                nc.vector.tensor_reduce(row_scale[:, :], own[:, :, :], AX.X, ALU.add).then_inc(dve_step, 1)
                dve.wait_ge(dve_step, b * 8 + 7)
                for t in range(T):
                    ins = nc.vector.tensor_scalar(q_tempered[:, t], q_less_max[:, t], row_scale[:, t:t + 1], None,
                                                  ALU.mult)
                ins.then_inc(tempered_q, 1)
                for g in range(G):
                    dve.wait_ge(temper_exp, b * G + g + 1)
                    nc.vector.tensor_scalar(probs[:, g], probs[:, g], 0.0, None, ALU.max).then_inc(probs_clean, 1)

            def finish(b):
                dve.wait_ge(sums_spread, b + 1)
                if tempered:
                    nc.vector.tensor_scalar(zi[:, :, :], o_ps[:, 2:4, :], 0.5, None, ALU.max).then_inc(dve_step, 1)
                    dve.wait_ge(dve_step, b * 8 + 8)
                    nc.vector.reciprocal(recip[:, :, :], zi[:, :, :]).then_inc(recip_done, 1)
                else:
                    nc.vector.reciprocal(recip[:, :, :], o_ps[:, 2:4, :]).then_inc(recip_done, 1)
                dve.wait_ge(recip_done, b + 1)
                dve.wait_ge(o_stored, b + 1)
                nc.vector.tensor_tensor(o_norm[:, :, :], o[:, :, :], recip[:, :, :], ALU.mult).then_inc(o_scaled, 1)
                dve.wait_ge(projected, b + 1)
                nc.vector.tensor_tensor(x[:, b, :], x[:, b, :], k_ps[:, 2, :], ALU.add).then_inc(added, 1)

            if tempered:
                dve_step = sem("dve_step")
            dve.wait_ge(ready, 1)
            store_k(0)
            take_max(0)
            store_v(0)
            with dve.Fori(0, B - 1) as b:
                shift(b)
                if tempered:
                    temper(b)
                    finish(b)
                    store_k(b + 1)
                    take_max(b + 1)
                    store_v(b + 1)
                else:
                    store_k(b + 1)
                    take_max(b + 1)
                    dve.wait_ge(pv_done, b + 1)
                    store_v(b + 1)
                    finish(b)
            shift(B - 1)
            if tempered:
                temper(B - 1)
            finish(B - 1)


def refine_experts(nc, m, w, tag, meanwhile):
    E, HID, PAIRS, PARTS, ITERS, DT = 8, 64, 4, 3, 2, 0.1
    ALPHA, BETA, GATE = range(PARTS)
    ORDER = [(BETA, GATE, ALPHA), (ALPHA, GATE, BETA), (BETA, GATE, ALPHA)]
    BRANCHES = 3
    x, xnT, identity = m["x"], m["xnT"], m["identity"]
    layernorm(nc, m, tag + "_ln")
    with cleared_semaphores(nc) as new_semaphore, ExitStack() as ctx:
        def sb(name, shape, dt=F32):
            return ctx.enter_context(nc.sbuf_tensor(f"{tag}_{name}", shape, dt))

        def sem(name):
            return new_semaphore(f"{tag}_{name}")

        def ps(name):
            return ctx.enter_context(nc.psum_tensor(f"{tag}_{name}", [P, CH], F32))

        route = sb("route", [33, CH])
        logits = sb("logits", [P, 4, E])
        best = sb("best", [P, 4, 8])
        best_at = sb("best_at", [P, 4, 8], U32)
        at = sb("at", [P, 4, 2])
        gap, gap_exp, one_more = sb("gap", [P, 4]), sb("gap_exp", [P, 4]), sb("one_more", [P, 4])
        share = sb("share", [P, 4, 2])
        choice = sb("choice", [P, 4, 4, 32])
        choice_t = sb("choice_t", [P, CH])
        choice_bf = sb("choice_bf", [P, CH], BF16)
        mask = sb("mask", [P, 2, PAIRS, CH], BF16)
        weight = sb("weight", [P, 2, CH])
        xi, err, v = sb("xi", [P, CH]), sb("err", [P, CH]), sb("v", [P, CH])
        hidden = sb("hidden", [P, PAIRS + 1, CH])
        chosen = sb("chosen", [P, 2, PAIRS, CH])
        gated = [[sb(f"gated{s}{k}", [P, CH]) for k in range(PARTS)] for s in range(2)]
        abs_b, exp_b = sb("abs_b", [P, CH]), sb("exp_b", [P, CH])
        soft, push, keep = sb("soft", [P, CH]), sb("push", [P, CH]), sb("keep", [P, CH])
        v_new, move, part = sb("v_new", [P, CH]), sb("move", [P, CH]), sb("part", [P, CH])
        v_sum, move_sum, x_next = sb("v_sum", [P, CH]), sb("move_sum", [P, CH]), sb("x_next", [P, CH])
        halt_h, halt, refine = sb("halt_h", [32, CH]), sb("halt", [P, CH]), sb("refine", [P, 2, CH])
        stepped = sb("stepped", [P, CH])
        sw, sw_exp, sw_left = sb("sw", [P, 1]), sb("sw_exp", [P, 1]), sb("sw_left", [P, 1])

        names = ["route", "logits", "choice"]
        names += [f"mask{k}{p}" for k in range(2) for p in range(PAIRS)] + ["weight0", "weight1"]
        for it in range(ITERS):
            names += [f"hidden{it}{p}" for p in range(PAIRS + 1)]
            names += [f"{n}{it}" for n in ("halt_h", "refine_a", "refine_b", "halt", "refined")]
        names += ["out"]
        banks = Banks(names, [ps(f"work{k}") for k in range(2)],
                      [sem(f"work_filled{k}") for k in range(2)], [sem(f"work_freed{k}") for k in range(2)])
        ctl = [[ps(f"ctl{s}{k}") for k in range(PARTS)] for s in range(2)]
        parts_of = [2, 3]
        PER_PASS = BRANCHES * sum(parts_of)
        NB = BRANCHES * ITERS

        ready, sw_ready, sw_exped = sem("ready"), sem("sw_ready"), sem("sw_exped")
        gap_made, gap_exped, choice_made = sem("gap_made"), sem("gap_exped"), sem("choice_made")
        choice_cast = sem("choice_cast")
        x_set, chosen_made = sem("x_set"), sem("chosen_made")
        ctl_filled, ctl_act, ctl_dve = sem("ctl_filled"), sem("ctl_act"), sem("ctl_dve")
        next_made, halt_h_stored, refine_stored, halt_stored = \
            sem("next_made"), sem("halt_h_stored"), sem("refine_stored"), sem("halt_stored")
        v_made = sem("v_made")
        act_step, dve_step = sem("act_step"), sem("dve_step")
        block = ctx.enter_context(nc.Block())

        @block.sync
        def _(sp):
            meanwhile(sp)

        @block.gpsimd
        def _(pool):
            nc.gpsimd.memset(choice[:, :, :, :], 0.0).then_inc(ready, 1)
            pool.wait_ge(ready, 1)
            nc.gpsimd.memset(route[32:33, :], 1.0).then_inc(ready, 1)

        @block.tensor
        def _(pe):
            def mm(out, lhs, rhs, start=True, stop=True):
                return nc.tensor.matmul(out, lhs, rhs, start=start, stop=stop)

            for k in range(2):
                pe.sem_inc(banks.freed[k], 1)
            pe.wait_ge(ready, 2)
            with pe.Fori(0, NCH) as i:
                xn = xnT[:, bass.ds(i * 4, 4), :]
                banks.wait_free(pe, "route", i)
                banks.fill(mm(banks.bank("route")[0:32, :], w["w_r1"][:, :], xn), "route")
                banks.wait_free(pe, "logits", i)
                banks.wait_freed(pe, "route", i)
                for q in range(4):
                    ins = mm(banks.bank("logits")[:, 8 * q:8 * q + 8], route[:, S * q:S * q + S], w["w_r2"][:, :])
                banks.fill(ins, "logits")
                banks.wait_free(pe, "choice", i)
                pe.wait_ge(choice_made, i + 1)
                for q in range(4):
                    ins = nc.tensor.transpose(banks.bank("choice")[:, S * q:S * q + S],
                                              choice[:, q].rearrange("p a e -> p (a e)"), identity[:, :])
                banks.fill(ins, "choice")
                pe.wait_ge(choice_cast, i + 1)
                for k in range(2):
                    r = slice(32 * k, 32 * k + E)
                    for p in range(PAIRS):
                        banks.wait_free(pe, f"mask{k}{p}", i)
                        banks.fill(mm(banks.bank(f"mask{k}{p}")[:, :], m["pair_rows_bf"][r, p, :], choice_bf[r, :]),
                                   f"mask{k}{p}")
                for k in range(2):
                    r = slice(64 + 32 * k, 64 + 32 * k + E)
                    banks.wait_free(pe, f"weight{k}", i)
                    banks.fill(mm(banks.bank(f"weight{k}")[:, :], m["ones_sq"][r, :], choice_t[r, :]), f"weight{k}")
                done = 0
                for it in range(ITERS):
                    pe.wait_ge(x_set, i * 3 + it + 1)
                    for p in range(PAIRS + 1):
                        name = f"hidden{it}{p}"
                        banks.wait_free(pe, name, i)
                        rows = P if p < PAIRS else HID
                        ins = mm(banks.bank(name)[0:rows, :], w["w1"][:, 0, P * p:P * p + rows], xi[:, :],
                                 stop=(it == 0))
                        if it:
                            ins = mm(banks.bank(name)[0:rows, :], w["w1"][:, 1, P * p:P * p + rows], v[:, :],
                                     start=False)
                        banks.fill(ins, name)
                    for r in range(BRANCHES):
                        n = it * BRANCHES + r
                        pe.wait_ge(ctl_act, i * NB + n + 1)
                        pe.wait_ge(ctl_dve, i * NB + n + 1)
                        if r < 2:
                            pe.wait_ge(chosen_made, (i * ITERS + it) * 2 + r + 1)
                        else:
                            banks.wait_freed(pe, f"hidden{it}{PAIRS}", i)
                        for part_ in ORDER[r]:
                            if part_ == ALPHA and it == 0:
                                continue
                            c = slice(P * part_, P * part_ + P)
                            bank = ctl[n % 2][part_]
                            if r < 2:
                                rows = slice(32 * r, 32 * r + E)
                                mm(bank[:, :], w["b2"][rows, c], choice_t[rows, :], stop=False)
                                for p in range(PAIRS):
                                    ins = mm(bank[:, :], w["w2"][:, p, c], chosen[:, r, p, :], start=False,
                                             stop=(p == PAIRS - 1))
                            else:
                                ins = mm(bank[:, :], w["w_s2"][:, c], hidden[0:HID, PAIRS, :])
                            ins.then_inc(ctl_filled, 1)
                    pe.wait_ge(next_made, i * ITERS + it + 1)
                    banks.wait_free(pe, f"halt_h{it}", i)
                    banks.fill(mm(banks.bank(f"halt_h{it}")[0:32, :], w["w_h1"][:, :], x_next[:, :]), f"halt_h{it}")
                    for k, name in enumerate(("refine_a", "refine_b")):
                        banks.wait_free(pe, f"{name}{it}", i)
                        banks.fill(mm(banks.bank(f"{name}{it}")[:, :], w["w_f1"][:, P * k:P * k + P], x_next[:, :]),
                                   f"{name}{it}")
                    banks.wait_free(pe, f"halt{it}", i)
                    pe.wait_ge(halt_h_stored, i * ITERS + it + 1)
                    banks.fill(mm(banks.bank(f"halt{it}")[:, :], w["w_h2"][:, :], halt_h[:, :]), f"halt{it}")
                    banks.wait_free(pe, f"refined{it}", i)
                    pe.wait_ge(refine_stored, (i * ITERS + it + 1) * 2)
                    for k in range(2):
                        ins = mm(banks.bank(f"refined{it}")[:, :], w["w_f2"][:, k, :], refine[:, k, :],
                                 start=(k == 0), stop=(k == 1))
                    banks.fill(ins, f"refined{it}")
                banks.wait_free(pe, "out", i)
                pe.wait_ge(x_set, i * 3 + 3)
                for q in range(4):
                    ins = nc.tensor.transpose(banks.bank("out")[:, S * q:S * q + S], xi[:, S * q:S * q + S],
                                              identity[:, :])
                banks.fill(ins, "out")

        @block.scalar
        def _(act):
            chain = Chain(act, act_step, 12)
            act.sem_inc(ctl_act, 2)
            nc.scalar.activation(sw_exp[:, :], w["shared_weight"][:, :], ACT.Exp, scale=-1.0).then_inc(sw_exped, 1)
            with act.Fori(0, NCH) as i:
                chain.begin(i)
                banks.wait_filled(act, "route", i)
                banks.free(nc.scalar.activation(route[0:32, :], banks.bank("route")[0:32, :], ACT.Gelu,
                                                bias=w["b_r1"][:, 0:1]), "route")
                act.wait_ge(gap_made, i + 1)
                nc.scalar.activation(gap_exp[:, :], gap[:, :], ACT.Exp).then_inc(gap_exped, 1)
                banks.wait_filled(act, "choice", i)
                nc.scalar.copy(choice_bf[:, :], banks.bank("choice")[:, :]).then_inc(choice_cast, 1)
                banks.free(nc.scalar.copy(choice_t[:, :], banks.bank("choice")[:, :]), "choice")
                for k in range(2):
                    for p in range(PAIRS):
                        name = f"mask{k}{p}"
                        banks.wait_filled(act, name, i)
                        banks.free(nc.scalar.copy(mask[:, k, p, :], banks.bank(name)[:, :]), name)
                done = 0
                for it in range(ITERS):
                    for p in range(PAIRS + 1):
                        name = f"hidden{it}{p}"
                        rows = P if p < PAIRS else HID
                        banks.wait_filled(act, name, i)
                        banks.free(nc.scalar.activation(hidden[0:rows, p, :], banks.bank(name)[0:rows, :], ACT.Gelu,
                                                        bias=w["b1"][0:rows, p:p + 1]), name)
                    for r in range(BRANCHES):
                        n = it * BRANCHES + r
                        s = n % 2
                        for part_ in ORDER[r]:
                            if part_ == ALPHA and it == 0:
                                continue
                            done += 1
                            act.wait_ge(ctl_filled, i * PER_PASS + done)
                            bias = dict(bias=w["b_s2"][:, part_:part_ + 1]) if r == 2 else {}
                            if part_ == BETA:
                                chain(nc.scalar.activation(abs_b[:, :], ctl[s][part_][:, :], ACT.Abs, **bias))
                                chain(nc.scalar.activation(exp_b[:, :], abs_b[:, :], ACT.Exp, scale=-1.0))
                                ins = nc.scalar.activation(gated[s][part_][:, :], exp_b[:, :], ACT.Ln, bias=1.0)
                            else:
                                ins = nc.scalar.activation(gated[s][part_][:, :], ctl[s][part_][:, :], ACT.Sigmoid,
                                                           **bias)
                        ins.then_inc(ctl_act, 1)
                    banks.wait_filled(act, f"halt_h{it}", i)
                    nc.scalar.activation(halt_h[:, :], banks.bank(f"halt_h{it}")[0:32, :], ACT.Gelu,
                                         bias=w["b_h1"][:, 0:1]).then_inc(halt_h_stored, 1)
                    act.wait_ge(halt_h_stored, i * ITERS + it + 1)
                    act.sem_inc(banks.freed[banks.place[f"halt_h{it}"][0]], 1)
                    for k, name in enumerate(("refine_a", "refine_b")):
                        banks.wait_filled(act, f"{name}{it}", i)
                        nc.scalar.activation(refine[:, k, :], banks.bank(f"{name}{it}")[:, :], ACT.Gelu,
                                             bias=w["b_f1"][:, k:k + 1]).then_inc(refine_stored, 1)
                        act.wait_ge(refine_stored, (i * ITERS + it) * 2 + k + 1)
                        act.sem_inc(banks.freed[banks.place[f"{name}{it}"][0]], 1)
                    banks.wait_filled(act, f"halt{it}", i)
                    nc.scalar.activation(halt[:, :], banks.bank(f"halt{it}")[:, :], ACT.Sigmoid,
                                         bias=w["b_h2"][:, 0:1]).then_inc(halt_stored, 1)
                    act.wait_ge(halt_stored, i * ITERS + it + 1)
                    act.sem_inc(banks.freed[banks.place[f"halt{it}"][0]], 1)
                chain.end()

        @block.vector
        def _(dve):
            V = nc.vector
            pre = Chain(dve, sw_ready, 0)
            dve.sem_inc(ctl_dve, 2)
            dve.wait_ge(sw_exped, 1)
            pre(V.tensor_scalar(sw_exp[:, :], sw_exp[:, :], 1.0, None, ALU.add))
            pre(V.reciprocal(sw[:, :], sw_exp[:, :]))
            pre(V.tensor_scalar(sw_left[:, :], sw[:, :], -1.0, 1.0, ALU.mult, ALU.add))
            dve.wait_ge(ready, 2)
            chain = Chain(dve, dve_step, 40)
            with dve.Fori(0, NCH) as i:
                chain.begin(i)
                banks.wait_filled(dve, "logits", i)
                banks.free(V.tensor_copy(logits[:, :, :], banks.bank("logits")[:, 0:32]
                                         .rearrange("p (q e) -> p q e", q=4)), "logits")
                banks.wait_freed(dve, "logits", i)
                V.tensor_copy(xi[:, :].rearrange("p (q s) -> p q s", q=4), xnT[:, bass.ds(i * 4, 4), :]) \
                    .then_inc(x_set, 1)
                for q in range(4):
                    ins = V.max(best[:, q, :], logits[:, q, :])
                chain(ins)
                V.tensor_tensor(gap[:, :], best[:, :, 1], best[:, :, 0], ALU.subtract).then_inc(gap_made, 1)
                for q in range(4):
                    ins = V.max_index(best_at[:, q, :], best[:, q, :], logits[:, q, :])
                chain(ins)
                chain(V.tensor_copy(at[:, :, :], best_at[:, :, 0:2]))
                for k in range(2):
                    ins = V.tensor_tensor(choice[:, :, k, 0:E], m["iota8"][:, :, :],
                                          at[:, :, k:k + 1].broadcast_to([P, 4, E]), ALU.is_equal)
                chain(ins)
                dve.wait_ge(gap_exped, i + 1)
                chain(V.tensor_scalar(one_more[:, :], gap_exp[:, :], 1.0, None, ALU.add))
                chain(V.reciprocal(share[:, :, 0], one_more[:, :]))
                chain(V.tensor_tensor(share[:, :, 1], share[:, :, 0], gap_exp[:, :], ALU.mult))
                for k in range(2):
                    ins = V.tensor_tensor(choice[:, :, 2 + k, 0:E], choice[:, :, k, 0:E],
                                          share[:, :, k:k + 1].broadcast_to([P, 4, E]), ALU.mult)
                ins.then_inc(choice_made, 1)
                for k in range(2):
                    banks.wait_filled(dve, f"weight{k}", i)
                    banks.free(V.tensor_scalar(weight[:, k, :], banks.bank(f"weight{k}")[:, :], sw_left[:, 0:1],
                                               None, ALU.mult), f"weight{k}")
                for it in range(ITERS):
                    dve.wait_ge(x_set, i * 3 + it + 1)
                    V.tensor_scalar(err[:, :], xi[:, :], w["mu"][:, 0:1], None, ALU.subtract)
                    for k in range(2):
                        for p in range(PAIRS):
                            if k == 0:
                                banks.wait_freed(dve, f"hidden{it}{p}", i)
                            ins = V.tensor_tensor(chosen[:, k, p, :], hidden[:, p, :], mask[:, k, p, :], ALU.mult)
                        ins.then_inc(chosen_made, 1)
                    for r in range(BRANCHES):
                        n = it * BRANCHES + r
                        s = n % 2
                        dve.wait_ge(ctl_act, i * NB + n + 3)
                        beta = ctl[s][BETA][:, :]
                        if r < 2:
                            chain(V.scalar_tensor_tensor(soft[:, :], beta, 0.0, gated[s][BETA][:, :], ALU.max, ALU.add))
                        else:
                            chain(V.tensor_scalar(part[:, :], beta, w["b_s2"][:, BETA:BETA + 1], 0.0, ALU.add, ALU.max))
                            chain(V.tensor_tensor(soft[:, :], part[:, :], gated[s][BETA][:, :], ALU.add))
                        chain(V.scalar_tensor_tensor(push[:, :], soft[:, :], -1.0, err[:, :], ALU.mult, ALU.mult))
                        fresh = push
                        if it:
                            chain(V.tensor_tensor(keep[:, :], gated[s][ALPHA][:, :], v[:, :], ALU.mult))
                            chain(V.tensor_tensor(v_new[:, :], keep[:, :], push[:, :], ALU.add))
                            fresh = v_new
                        chain(V.tensor_tensor(move[:, :], gated[s][GATE][:, :], fresh[:, :], ALU.mult))
                        for total, term in ((v_sum, fresh), (move_sum, move)):
                            if r == 0:
                                ins = V.tensor_tensor(total[:, :], term[:, :], weight[:, 0, :], ALU.mult)
                            elif r == 1:
                                chain(V.tensor_tensor(part[:, :], term[:, :], weight[:, 1, :], ALU.mult))
                                ins = V.tensor_tensor(total[:, :], total[:, :], part[:, :], ALU.add)
                                if total is v_sum:
                                    chain(ins)
                            else:
                                ins = V.scalar_tensor_tensor(total[:, :], term[:, :], sw[:, 0:1], total[:, :],
                                                             ALU.mult, ALU.add)
                        ins.then_inc(ctl_dve, 1)
                        dve.wait_ge(ctl_dve, i * NB + n + 3)
                    V.scalar_tensor_tensor(x_next[:, :], move_sum[:, :], DT, xi[:, :], ALU.mult, ALU.add) \
                        .then_inc(next_made, 1)
                    if it < ITERS - 1:
                        chain(V.tensor_copy(v[:, :], v_sum[:, :]))
                    banks.wait_filled(dve, f"refined{it}", i)
                    dve.wait_ge(halt_stored, i * ITERS + it + 1)
                    banks.free(V.scalar_tensor_tensor(stepped[:, :], banks.bank(f"refined{it}")[:, :],
                                                      w["b_f2"][:, 0:1], halt[:, :], ALU.add, ALU.mult), f"refined{it}")
                    banks.wait_freed(dve, f"refined{it}", i)
                    V.scalar_tensor_tensor(xi[:, :], stepped[:, :], w["integration_weight"][:, 0:1], xi[:, :],
                                           ALU.mult, ALU.add).then_inc(x_set, 1)
                banks.wait_filled(dve, "out", i)
                xs = x[:, bass.ds(i * 4, 4), :]
                banks.free(V.tensor_tensor(xs, xs, banks.bank("out")[:, :].rearrange("p (q s) -> p q s", q=4),
                                           ALU.add), "out")
                chain.end()


def top1_experts(nc, m, w, tag, meanwhile):
    E, FT = 14, 2
    NT = E * FT
    RING = 4
    x, xnT, identity = m["x"], m["xnT"], m["identity"]
    layernorm(nc, m, tag + "_ln")
    with cleared_semaphores(nc) as new_semaphore, ExitStack() as ctx:
        def sb(name, shape, dt=F32):
            return ctx.enter_context(nc.sbuf_tensor(f"{tag}_{name}", shape, dt))

        def sem(name):
            return new_semaphore(f"{tag}_{name}")

        def ps(name):
            return ctx.enter_context(nc.psum_tensor(f"{tag}_{name}", [P, CH], F32))

        def ring(kind, names, n):
            return Banks(names, [ps(f"{kind}{k}") for k in range(n)],
                         [sem(f"{kind}_filled{k}") for k in range(n)], [sem(f"{kind}_freed{k}") for k in range(n)])

        xc = sb("xc", [P, CH])
        logits = sb("logits", [P, 4, E])
        best, best_at, at = sb("best", [P, 4, 8]), sb("best_at", [P, 4, 8], U32), sb("at", [P, 4])
        neg_best, exps, total, weight = sb("neg_best", [P, 4]), sb("exps", [P, E]), sb("total", [P, 4]), sb("weight", [P, 4])
        choice = sb("choice", [P, 4, P])
        choice_t, choice_bf = sb("choice_t", [E, CH]), sb("choice_bf", [E, CH], BF16)
        hidden = [sb(f"hidden{k}", [P, CH]) for k in range(RING)]
        chosen = [sb(f"chosen{k}", [P, CH]) for k in range(RING)]
        y_t = sb("y_t", [P, CH])
        work = ring("work", ["logits", "choice"] + [f"hidden{n}" for n in range(NT)] + ["out"], 4)
        masks = ring("mask", [f"mask{e}" for e in range(E)], 3)
        acc = ring("acc", ["acc"], 1)
        ready, xc_set, neg_made, total_made, choice_made = \
            sem("ready"), sem("xc_set"), sem("neg_made"), sem("total_made"), sem("choice_made")
        choice_cast, chosen_made, chosen_used = sem("choice_cast"), sem("chosen_made"), sem("chosen_used")
        dve_step, act_step = sem("dve_step"), sem("act_step")
        block = ctx.enter_context(nc.Block())

        @block.sync
        def _(sp):
            meanwhile(sp)

        @block.gpsimd
        def _(pool):
            nc.gpsimd.memset(choice[:, :, :], 0.0).then_inc(ready, 1)

        @block.tensor
        def _(pe):
            mm = nc.tensor.matmul
            for r in (work, masks, acc):
                for s in r.freed:
                    pe.sem_inc(s, 1)
            pe.sem_inc(chosen_used, RING)
            with pe.Fori(0, NCH) as i:
                pe.wait_ge(xc_set, i + 1)
                work.wait_free(pe, "logits", i)
                for q in range(4):
                    ins = mm(work.bank("logits")[:, E * q:E * q + E], xc[:, S * q:S * q + S], w["router_w"][:, :],
                             start=True, stop=True)
                work.fill(ins, "logits")
                work.wait_free(pe, "choice", i)
                pe.wait_ge(choice_made, i + 1)
                for q in range(4):
                    ins = nc.tensor.transpose(work.bank("choice")[:, S * q:S * q + S], choice[:, q, :], identity[:, :])
                work.fill(ins, "choice")

                def second(n):
                    pe.wait_ge(chosen_made, i * NT + n + 1 + RING)
                    mm(acc.bank("acc")[:, :], w["w2"][:, n, :], chosen[n % RING][:, :], start=False,
                       stop=(n == NT - 1)).then_inc(chosen_used, 1)

                LAG = 3
                for n in range(NT + LAG):
                    if n < NT:
                        e = n // FT
                        work.wait_free(pe, f"hidden{n}", i)
                        work.fill(mm(work.bank(f"hidden{n}")[:, :], w["w1"][:, n, :], xc[:, :], start=True, stop=True),
                                  f"hidden{n}")
                        if n % FT == 0:
                            masks.wait_free(pe, f"mask{e}", i)
                            pe.wait_ge(choice_cast, i + 1)
                            masks.fill(mm(masks.bank(f"mask{e}")[:, :], m["expert_rows_bf"][:, e, :], choice_bf[:, :],
                                          start=True, stop=True), f"mask{e}")
                        if n == 1:
                            acc.wait_free(pe, "acc", i)
                            work.wait_freed(pe, "choice", i)
                            mm(acc.bank("acc")[:, :], w["b2"][:, :], choice_t[:, :], start=True, stop=False)
                    if n >= LAG:
                        second(n - LAG)
                work.wait_free(pe, "out", i)
                acc.wait_freed(pe, "acc", i)
                for q in range(4):
                    ins = nc.tensor.transpose(work.bank("out")[:, S * q:S * q + S], y_t[:, S * q:S * q + S],
                                              identity[:, :])
                work.fill(ins, "out")

        @block.scalar
        def _(act):
            A = nc.scalar
            with act.Fori(0, NCH) as i:
                A.copy(xc[:, :].rearrange("p (q s) -> p q s", q=4), xnT[:, bass.ds(i * 4, 4), :]).then_inc(xc_set, 1)
                act.wait_ge(neg_made, i + 1)
                for q in range(4):
                    ins = A.activation(exps[:, :], logits[:, q, :], ACT.Exp, bias=neg_best[:, q:q + 1],
                                       accum_out=total[:, q:q + 1])
                    if q < 3:
                        ins.then_inc(act_step, 1)
                        act.wait_ge(act_step, i * 3 + q + 1)
                ins.then_inc(total_made, 1)
                work.wait_filled(act, "choice", i)
                A.copy(choice_bf[:, :], work.bank("choice")[0:E, :]).then_inc(choice_cast, 1)
                work.free(A.copy(choice_t[:, :], work.bank("choice")[0:E, :]), "choice")
                for n in range(NT):
                    act.wait_ge(chosen_made, i * NT + n + 1)
                    work.wait_filled(act, f"hidden{n}", i)
                    work.free(A.activation(hidden[n % RING][:, :], work.bank(f"hidden{n}")[:, :], ACT.Gelu,
                                           bias=w["b1"][:, n:n + 1]), f"hidden{n}")
                act.wait_ge(chosen_used, i * NT + NT + RING)
                acc.free(A.copy(y_t[:, :], acc.bank("acc")[:, :]), "acc")

        @block.vector
        def _(dve):
            V = nc.vector
            dve.sem_inc(chosen_made, RING)
            chain = Chain(dve, dve_step, 4)
            dve.wait_ge(ready, 1)
            with dve.Fori(0, NCH) as i:
                chain.begin(i)
                work.wait_filled(dve, "logits", i)
                work.free(V.tensor_copy(logits[:, :, :], work.bank("logits")[:, 0:4 * E]
                                        .rearrange("p (q e) -> p q e", q=4)), "logits")
                work.wait_freed(dve, "logits", i)
                V.memset(at[:, :], 0.0)
                for q in range(4):
                    ins = V.max(best[:, q, :], logits[:, q, :])
                chain(ins)
                V.tensor_scalar(neg_best[:, :], best[:, :, 0], -1.0, None, ALU.mult).then_inc(neg_made, 1)
                for q in range(4):
                    ins = V.max_index(best_at[:, q, :], best[:, q, :], logits[:, q, :])
                chain(ins)
                chain(V.tensor_copy(at[:, :], best_at[:, :, 0]))
                V.tensor_tensor(choice[:, :, 0:E], m["iota14"][:, :, :],
                                at[:, :].unsqueeze(2).broadcast_to([P, 4, E]), ALU.is_equal).then_inc(choice_made, 1)
                dve.wait_ge(total_made, i + 1)
                chain(V.reciprocal(weight[:, :], total[:, :]))
                for n in range(NT):
                    e = n // FT
                    if n % FT == 0:
                        masks.wait_filled(dve, f"mask{e}", i)
                    work.wait_freed(dve, f"hidden{n}", i)
                    dve.wait_ge(chosen_used, i * NT + n + 1)
                    V.tensor_tensor(chosen[n % RING][:, :], hidden[n % RING][:, :], masks.bank(f"mask{e}")[:, :],
                                    ALU.mult).then_inc(chosen_made, 1)
                    if n % FT == FT - 1:
                        dve.wait_ge(chosen_made, i * NT + n + 1 + RING)
                        dve.sem_inc(masks.freed[masks.place[f"mask{e}"][0]], 1)
                work.wait_filled(dve, "out", i)
                for q in range(4):
                    xb = x[:, i * 4 + q, :]
                    ins = V.scalar_tensor_tensor(xb, work.bank("out")[:, S * q:S * q + S], weight[:, q:q + 1], xb,
                                                 ALU.mult, ALU.add)
                work.free(ins, "out")
                chain.end()


def gated_lora(nc, m, w, tag, meanwhile):
    E, R = 8, 16
    x, xnT, identity = m["x"], m["xnT"], m["identity"]
    layernorm(nc, m, tag + "_ln")
    with cleared_semaphores(nc) as new_semaphore, ExitStack() as ctx:
        def sb(name, shape, dt=F32):
            return ctx.enter_context(nc.sbuf_tensor(f"{tag}_{name}", shape, dt))

        def sem(name):
            return new_semaphore(f"{tag}_{name}")

        xc = sb("xc", [P, CH])
        neg_top, exps, total, inv = sb("neg_top", [P, 4]), sb("exps", [P, 4, E]), sb("total", [P, 4]), sb("inv", [P, 4])
        gate = sb("gates", [P, 4, E])
        low = sb("low_rank", [P, 4, E, R])
        low_t = sb("low_t", [P, 4, S])
        names = ["gate", "low", "flip", "out"]
        banks = Banks(names, [ctx.enter_context(nc.psum_tensor(f"{tag}_{n}_ps", [P, CH], F32)) for n in names],
                      [sem(f"{n}_filled") for n in names], [sem(f"{n}_freed") for n in names])
        xc_set, neg_made, exps_made, low_made, dve_step = \
            sem("xc_set"), sem("neg_made"), sem("exps_made"), sem("low_made"), sem("dve_step")
        block = ctx.enter_context(nc.Block())

        @block.sync
        def _(sp):
            meanwhile(sp)

        @block.tensor
        def _(pe):
            mm = nc.tensor.matmul
            for s in banks.freed:
                pe.sem_inc(s, 1)
            with pe.Fori(0, NCH) as i:
                pe.wait_ge(xc_set, i + 1)
                banks.wait_free(pe, "gate", i)
                for q in range(4):
                    ins = mm(banks.bank("gate")[:, E * q:E * q + E], xc[:, S * q:S * q + S], w["gate"][:, :],
                             start=True, stop=True)
                banks.fill(ins, "gate")
                banks.wait_free(pe, "low", i)
                for q in range(4):
                    ins = mm(banks.bank("low")[:, S * q:S * q + S], xc[:, S * q:S * q + S], w["down"][:, :],
                             start=True, stop=True)
                banks.fill(ins, "low")
                banks.wait_free(pe, "flip", i)
                pe.wait_ge(low_made, i + 1)
                for q in range(4):
                    ins = nc.tensor.transpose(banks.bank("flip")[:, S * q:S * q + S],
                                              low[:, q].rearrange("p e r -> p (e r)"), identity[:, :])
                banks.fill(ins, "flip")
                banks.wait_free(pe, "out", i)
                banks.wait_freed(pe, "flip", i)
                for q in range(4):
                    o = banks.bank("out")[:, S * q:S * q + S]
                    mm(o, xc[:, S * q:S * q + S], w["weight"][:, :], start=True, stop=False)
                    ins = mm(o, low_t[:, q, :], w["up"][:, :], start=False, stop=True)
                banks.fill(ins, "out")

        @block.scalar
        def _(act):
            A = nc.scalar
            with act.Fori(0, NCH) as i:
                A.copy(xc[:, :].rearrange("p (q s) -> p q s", q=4), xnT[:, bass.ds(i * 4, 4), :]).then_inc(xc_set, 1)
                act.wait_ge(neg_made, i + 1)
                banks.wait_filled(act, "gate", i)
                for q in range(4):
                    ins = A.activation(exps[:, q, :], banks.bank("gate")[:, E * q:E * q + E], ACT.Exp,
                                       bias=neg_top[:, q:q + 1], accum_out=total[:, q:q + 1])
                ins.then_inc(exps_made, 1)
                banks.wait_filled(act, "flip", i)
                banks.free(A.copy(low_t[:, :, :], banks.bank("flip")[:, :].rearrange("p (q s) -> p q s", q=4)), "flip")
                banks.wait_filled(act, "out", i)

        @block.vector
        def _(dve):
            V = nc.vector
            chain = Chain(dve, dve_step, 2)
            with dve.Fori(0, NCH) as i:
                chain.begin(i)
                banks.wait_filled(dve, "gate", i)
                V.tensor_reduce(neg_top[:, :], banks.bank("gate")[:, 0:4 * E].rearrange("p (q e) -> p q e", q=4),
                                AX.X, ALU.max, negate=True).then_inc(neg_made, 1)
                dve.wait_ge(exps_made, i + 1)
                dve.sem_inc(banks.freed[banks.place["gate"][0]], 1)
                chain(V.reciprocal(inv[:, :], total[:, :]))
                chain(V.scalar_tensor_tensor(gate[:, :, :], exps[:, :, :], 1.0 / R,
                                             inv[:, :].unsqueeze(2).broadcast_to([P, 4, E]), ALU.mult, ALU.mult))
                banks.wait_filled(dve, "low", i)
                V.tensor_tensor(low[:, :, :, :].rearrange("p q e r -> p (q e) r"),
                                banks.bank("low")[:, :].rearrange("p (q r) -> p q r", r=R),
                                gate[:, :, :].rearrange("p q e -> p (q e)").unsqueeze(2).broadcast_to([P, 4 * E, R]),
                                ALU.mult).then_inc(low_made, 1)
                dve.wait_ge(low_made, i + 1)
                dve.sem_inc(banks.freed[banks.place["low"][0]], 1)
                banks.wait_filled(dve, "out", i)
                xs = x[:, bass.ds(i * 4, 4), :]
                banks.free(V.tensor_tensor(xs, xs, banks.bank("out")[:, :].rearrange("p (q s) -> p q s", q=4),
                                           ALU.add), "out")
                chain.end()


def two_attentions(nc, m, w, tag, meanwhile):
    x, xnT, ctxT, identity = m["x"], m["xnT"], m["ctxT"], m["identity"]
    layernorm(nc, m, tag + "_ln")
    with cleared_semaphores(nc) as new_semaphore, ExitStack() as ctx:
        def sb(name, shape, dt=F32):
            return ctx.enter_context(nc.sbuf_tensor(f"{tag}_{name}_sb", shape, dt))

        def sem(name):
            return new_semaphore(f"{tag}_{name}")

        Q4 = [P, 4, S]
        xc, ctx_c = sb("xc", Q4), sb("ctx_c", Q4)
        res = [sb("res0", Q4), sb("res1", Q4), sb("res2", Q4)]
        qT, kT, v = sb("qT", Q4), sb("kT", Q4), sb("v", Q4)
        sT = sb("sT", Q4)
        masked, probs, probsT = sb("masked", Q4), sb("probs", Q4), sb("probsT", Q4)
        neg = sb("neg", Q4)
        nonzero, length, length_all = sb("nonzero", [1, 4, S]), sb("length", [1, 4]), sb("length_all", [P, 4])
        neg_max, sums, inv = sb("neg_max", [P, 4]), sb("sums", [P, 4]), sb("inv", [P, 4])
        y, z = sb("y", Q4), sb("z", Q4)
        stats, mean_var = sb("stats", [P, 4, 6]), sb("mean_var", [P, 4, 2])
        var_eps, rstd = sb("var_eps", [P, 4]), sb("rstd", [P, 4])
        hid = sb("hid", Q4)

        names = ["res0"]
        for a in range(2):
            names += [f"{n}{a}" for n in ("q", "k", "v", "scores", "length", "flip", "pv", "xT")]
        names += ["hid", "fc"]
        NB = 7
        banks = Banks(names, [ctx.enter_context(nc.psum_tensor(f"{tag}_bank{k}", Q4, F32)) for k in range(NB)],
                      [sem(f"bank{k}_filled") for k in range(NB)], [sem(f"bank{k}_freed") for k in range(NB)])
        inputs_set, length_made, neg_made, probs_made = sem("inputs_set"), sem("length_made"), sem("neg_made"), sem("probs_made")
        eps_added, rstd_made, stage_made = sem("eps_added"), sem("rstd_made"), sem("stage_made")
        dve_step = sem("dve_step")
        block = ctx.enter_context(nc.Block())

        @block.sync
        def _(sp):
            meanwhile(sp)

        @block.gpsimd
        def _(pool):
            with pool.Fori(0, NCH) as i:
                for n in range(3):
                    pool.wait_ge(eps_added, i * 3 + n + 1)
                    nc.gpsimd.tensor_tensor(rstd[:, :], var_eps[:, :], m["minus_half"][:, 0:4], ALU.pow) \
                        .then_inc(rstd_made, 1)

        @block.tensor
        def _(pe):
            for s in banks.freed:
                pe.sem_inc(s, 1)

            def each(name, i, products):
                banks.wait_free(pe, name, i)
                for out, lhs, rhs in products:
                    ins = nc.tensor.matmul(out, lhs, rhs, start=True, stop=True)
                banks.fill(ins, name)

            def flip(name, i, source):
                banks.wait_free(pe, name, i)
                for q in range(4):
                    ins = nc.tensor.transpose(banks.bank(name)[:, q, :], source[:, q, :], identity[:, :])
                banks.fill(ins, name)

            with pe.Fori(0, NCH) as i:
                pe.wait_ge(inputs_set, i + 1)
                flip("res0", i, xc)
                for a in range(2):
                    b = lambda n: banks.bank(f"{n}{a}")
                    q_in = sT if a else xc
                    kv_in = ctx_c if a else xc
                    if a:
                        banks.wait_freed(pe, "xT0", i)
                    each(f"q{a}", i, [(b("q")[:, :, :], w[f"Wq{a + 1}"][:, :], q_in[:, :, :])])
                    each(f"k{a}", i, [(b("k")[:, :, :], w[f"Wk{a + 1}"][:, :], kv_in[:, :, :])])
                    each(f"v{a}", i, [(b("v")[:, q, :], kv_in[:, q, :], w[f"Wv{a + 1}"][:, :]) for q in range(4)])
                    banks.wait_freed(pe, f"q{a}", i)
                    banks.wait_freed(pe, f"k{a}", i)
                    each(f"scores{a}", i, [(b("scores")[:, q, :], qT[:, q, :], kT[:, q, :]) for q in range(4)])
                    pe.wait_ge(length_made, i * 2 + a + 1)
                    each(f"length{a}", i, [(b("length")[:, 0, 0:4], m["ones_sq"][0:1, :], length[:, :])])
                    pe.wait_ge(probs_made, i * 2 + a + 1)
                    flip(f"flip{a}", i, probs)
                    banks.wait_freed(pe, f"flip{a}", i)
                    banks.wait_freed(pe, f"v{a}", i)
                    each(f"pv{a}", i, [(b("pv")[:, q, :], probsT[:, q, :], v[:, q, :]) for q in range(4)])
                    pe.wait_ge(stage_made, i * 3 + a + 1)
                    flip(f"xT{a}", i, res[a + 1])
                banks.wait_freed(pe, "xT1", i)
                each("hid", i, [(banks.bank("hid")[:, :, :], w["fc1_w"][:, :], sT[:, :, :])])
                banks.wait_freed(pe, "hid", i)
                each("fc", i, [(banks.bank("fc")[:, q, :], hid[:, q, :], w["fc2_w"][:, :]) for q in range(4)])

        @block.scalar
        def _(act):
            A = nc.scalar

            def store(name, i, out):
                banks.wait_filled(act, name, i)
                banks.free(A.copy(out[:, :, :], banks.bank(name)[:, :, :]), name)

            with act.Fori(0, NCH) as i:
                A.copy(xc[:, :, :], xnT[:, bass.ds(i * 4, 4), :])
                A.copy(ctx_c[:, :, :], ctxT[:, bass.ds(i * 4, 4), :]).then_inc(inputs_set, 1)
                store("res0", i, res[0])
                for a in range(2):
                    store(f"q{a}", i, qT)
                    store(f"k{a}", i, kT)
                    act.wait_ge(neg_made, i * 2 + a + 1)
                    for q in range(4):
                        ins = A.activation(probs[:, q, :], masked[:, q, :], ACT.Exp, bias=neg_max[:, q:q + 1],
                                           scale=SCORE_SCALE, accum_out=sums[:, q:q + 1])
                    ins.then_inc(probs_made, 1)
                    store(f"flip{a}", i, probsT)
                    store(f"xT{a}", i, sT)
                banks.wait_filled(act, "hid", i)
                banks.free(A.activation(hid[:, :, :], banks.bank("hid")[:, :, :], ACT.Relu, bias=w["fc1_b"][:, 0:1]),
                           "hid")

        @block.vector
        def _(dve):
            V = nc.vector
            chain = Chain(dve, dve_step, 23)

            def wide(row):
                return row[:, :].unsqueeze(1).broadcast_to(Q4)

            def norm(i, n, out):
                for q in range(4):
                    ins = V.bn_stats(stats[:, q, :], z[:, q, :])
                chain(ins)
                V.memset(var_eps[:, :], LN_EPS)
                for q in range(4):
                    ins = V.bn_aggr(mean_var[:, q, :], stats[:, q, :])
                chain(ins)
                V.tensor_tensor(var_eps[:, :], var_eps[:, :], mean_var[:, :, 1], ALU.add).then_inc(eps_added, 1)
                dve.wait_ge(rstd_made, i * 3 + n + 1)
                for q in range(4):
                    ins = V.tensor_scalar(y[:, q, :], z[:, q, :], mean_var[:, q, 0:1], rstd[:, q:q + 1],
                                          ALU.subtract, ALU.mult)
                chain(ins)
                chain(V.tensor_tensor(z[:, :, :], y[:, :, :], wide(w[f"ln{n + 1}_g"]), ALU.mult))
                V.tensor_tensor(out[:, :, :], z[:, :, :], wide(w[f"ln{n + 1}_b"]), ALU.add).then_inc(stage_made, 1)
                dve.wait_ge(stage_made, i * 3 + n + 1)

            with dve.Fori(0, NCH) as i:
                chain.begin(i)
                banks.wait_freed(dve, "res0", i)
                for a in range(2):
                    name = f"v{a}"
                    banks.wait_filled(dve, name, i)
                    banks.free(V.tensor_copy(v[:, :, :], banks.bank(name)[:, :, :]), name)
                    name = f"scores{a}"
                    banks.wait_filled(dve, name, i)
                    chain(V.tensor_scalar(nonzero[:, :, :], banks.bank(name)[0:1, :, :], 0.0, None, ALU.not_equal))
                    V.tensor_reduce(length[:, :], nonzero[:, :, :], AX.X, ALU.add).then_inc(length_made, 1)
                    banks.wait_filled(dve, f"length{a}", i)
                    banks.free(V.tensor_copy(length_all[:, :], banks.bank(f"length{a}")[:, 0, 0:4]), f"length{a}")
                    banks.wait_freed(dve, f"length{a}", i)
                    for q in range(4):
                        ins = V.tensor_scalar(neg[:, q, :], m["iota128"][:, :], length_all[:, q:q + 1], NEG,
                                              ALU.is_ge, ALU.mult)
                    chain(ins)
                    if a == 0:
                        chain(V.tensor_tensor(neg[:, :, :], neg[:, :, :], wide(m["future_f32"]), ALU.min))
                    banks.free(V.tensor_tensor(masked[:, :, :], neg[:, :, :], banks.bank(name)[:, :, :], ALU.add), name)
                    banks.wait_freed(dve, name, i)
                    chain(V.tensor_reduce(inv[:, :], masked[:, :, :], AX.X, ALU.max, negate=True))
                    V.tensor_scalar(neg_max[:, :], inv[:, :], SCORE_SCALE, None, ALU.mult).then_inc(neg_made, 1)
                    dve.wait_ge(probs_made, i * 2 + a + 1)
                    dve.wait_ge(neg_made, i * 2 + a + 1)
                    chain(V.reciprocal(inv[:, :], sums[:, :]))
                    banks.wait_filled(dve, f"pv{a}", i)
                    for q in range(4):
                        ins = V.scalar_tensor_tensor(z[:, q, :], banks.bank(f"pv{a}")[:, q, :], inv[:, q:q + 1],
                                                     res[a][:, q, :], ALU.mult, ALU.add)
                    banks.free(ins, f"pv{a}")
                    banks.wait_freed(dve, f"pv{a}", i)
                    norm(i, a, res[a + 1])
                banks.wait_filled(dve, "fc", i)
                banks.free(V.tensor_tensor(y[:, :, :], banks.bank("fc")[:, :, :], res[2][:, :, :], ALU.add), "fc")
                banks.wait_freed(dve, "fc", i)
                chain(V.tensor_tensor(z[:, :, :], y[:, :, :], wide(w["fc2_b"]), ALU.add))
                norm(i, 2, y)
                xs = x[:, bass.ds(i * 4, 4), :]
                chain(V.tensor_tensor(xs, xs, y[:, :, :], ALU.add))
                chain.end()


def product_keys(nc, m, w, tag, meanwhile):
    H, K, DK = 8, 32, 128
    E = K * K
    ET = E // P
    x, xnT, identity = m["x"], m["xnT"], m["identity"]
    layernorm(nc, m, tag + "_ln", rms_gain=w["norm_w"])
    with cleared_semaphores(nc) as new_semaphore, ExitStack() as ctx:
        def sb(name, shape, dt=F32):
            return ctx.enter_context(nc.sbuf_tensor(f"{tag}_{name}_sb", shape, dt))

        def sem(name):
            return new_semaphore(f"{tag}_{name}")

        def ps(name, shape):
            return ctx.enter_context(nc.psum_tensor(f"{tag}_{name}", shape, F32))

        RING = 3
        fold = sb("fold", [P, H, 2, K])
        xb = sb("xb", [P, S])
        sim = sb("sim", [P, H, 2, K])
        top = sb("top", [P, H, 2, 8])
        pairs = sb("pairs", [P, H, 8, 8])
        best = sb("best", [P, H, 8])
        least = sb("least", [P, H])
        sums = [sb(f"sums{k}", [P, K, K]) for k in range(RING)]
        kept = [sb(f"kept{k}", [P, E]) for k in range(RING)]
        hid, given = sb("hid", [P, ET, S]), sb("given", [P, ET, S])
        sim_ps, hid_ps, given_ps, out_ps = ps("sim_ps", [P, 512]), ps("hid_ps", [P, ET, S]), ps("given_ps", [P, ET, S]), \
            ps("out_ps", [P, 512])
        fold_made, fold_stored, xb_set, scored, sim_stored, sums_made, kept_made, kept_flipped = [
            sem(n) for n in ("fold_made", "fold_stored", "xb_set", "scored", "sim_stored", "sums_made", "kept_made",
                             "kept_flipped")]
        hid_made, hid_stored, given_made, out_made, added, least_made = [
            sem(n) for n in ("hid_made", "hid_stored", "given_made", "out_made", "added", "least_made")]
        dve_step = sem("dve_step")
        block = ctx.enter_context(nc.Block())

        @block.sync
        def _(sp):
            meanwhile(sp)

        @block.tensor
        def _(pe):
            mm = nc.tensor.matmul
            for h in range(H):
                for j in range(2):
                    ins = mm(sim_ps[:, (2 * h + j) * K:(2 * h + j) * K + K], w["w_q"][:, 2 * h + j, :],
                             w["keys"][:, 2 * h + j, :], start=True, stop=True)
            ins.then_inc(fold_made, 1)
            pe.wait_ge(fold_stored, 1)
            pe.sem_inc(kept_flipped, RING)
            pe.sem_inc(added, 1)
            with pe.Fori(0, B) as b:
                pe.wait_ge(xb_set, b + 1)
                mm(sim_ps[:, :], xb[:, :], fold[:, :, :, :], start=True, stop=True).then_inc(scored, 1)
                for e in range(ET):
                    ins = mm(hid_ps[:, e, :], w["down"][:, e, :], xb[:, :], start=True, stop=True)
                ins.then_inc(hid_made, 1)
                for h in range(H):
                    pe.wait_ge(kept_made, b * H + h + 1 + RING)
                    for e in range(ET):
                        ins = mm(given_ps[:, e, :], kept[h % RING][:, P * e:P * e + P], identity[:, :],
                                 start=(h == 0 and e % 4 == 0), stop=(h == H - 1), skip_group_check=True)
                    ins.then_inc(kept_flipped, 1)
                pe.wait_ge(given_made, b + 1)
                pe.wait_ge(added, b + 1)
                for e in range(ET):
                    ins = mm(out_ps[:, 0:D], given[:, e, :], w["up"][:, e, :], start=(e == 0), stop=(e == ET - 1))
                ins.then_inc(out_made, 1)

        @block.scalar
        def _(act):
            A = nc.scalar
            act.wait_ge(fold_made, 1)
            A.copy(fold[:, :, :, :].rearrange("p h j k -> p (h j k)"), sim_ps[:, :]).then_inc(fold_stored, 1)
            with act.Fori(0, B) as b:
                A.copy(xb[:, :], xnT[:, b, :]).then_inc(xb_set, 1)
                act.wait_ge(hid_made, b + 1)
                for k in range(2):
                    ins = A.activation(hid[:, 4 * k:4 * k + 4, :], hid_ps[:, 4 * k:4 * k + 4, :], ACT.Gelu)
                ins.then_inc(hid_stored, 1)
                act.wait_ge(out_made, b + 1)

        @block.gpsimd
        def _(pool):
            pool.sem_inc(sums_made, RING)
            with pool.Fori(0, B) as b:
                for h in range(H):
                    if h == 0:
                        pool.wait_ge(sim_stored, b + 1)
                    pool.wait_ge(kept_made, b * H + h + 1)
                    nc.gpsimd.tensor_tensor(sums[h % RING][:, :, :],
                                            sim[:, h, 0, :].unsqueeze(2).broadcast_to([P, K, K]),
                                            sim[:, h, 1, :].unsqueeze(1).broadcast_to([P, K, K]), ALU.add) \
                        .then_inc(sums_made, 1)

        @block.vector
        def _(dve):
            V = nc.vector
            chain = Chain(dve, dve_step, 4)
            dve.sem_inc(kept_made, RING)
            with dve.Fori(0, B) as b:
                chain.begin(b)
                dve.wait_ge(scored, b + 1)
                V.tensor_copy(sim[:, :, :, :].rearrange("p h j k -> p (h j k)"), sim_ps[:, :]).then_inc(sim_stored, 1)
                dve.wait_ge(sim_stored, b + 1)
                V.memset(least[:, :], 0.0)
                for h in range(H):
                    for j in range(2):
                        ins = V.max(top[:, h, j, :], sim[:, h, j, :])
                chain(ins)
                chain(V.tensor_tensor(pairs[:, :, :, :], top[:, :, 0, :].unsqueeze(3).broadcast_to([P, H, 8, 8]),
                                      top[:, :, 1, :].unsqueeze(2).broadcast_to([P, H, 8, 8]), ALU.add))
                V.memset(least[:, :], 0.0)
                for h in range(H):
                    ins = V.max(best[:, h, :], pairs[:, h, :, :])
                chain(ins)
                chain(V.tensor_scalar(least[:, :], best[:, :, 7], 0.0, None, ALU.max))
                for h in range(H):
                    k = h % RING
                    dve.wait_ge(sums_made, b * H + h + 1 + RING)
                    dve.wait_ge(kept_flipped, b * H + h + 1)
                    flat = sums[k][:, :, :].rearrange("p a c -> p (a c)")
                    V.scalar_tensor_tensor(kept[k][:, :], flat, least[:, h:h + 1], flat, ALU.is_ge, ALU.mult) \
                        .then_inc(kept_made, 1)
                dve.wait_ge(hid_stored, b + 1)
                dve.wait_ge(kept_flipped, b * H + H + RING)
                for k in range(2):
                    s = slice(4 * k, 4 * k + 4)
                    ins = V.tensor_tensor(given[:, s, :], hid[:, s, :], given_ps[:, s, :], ALU.mult)
                ins.then_inc(given_made, 1)
                dve.wait_ge(out_made, b + 1)
                V.tensor_tensor(x[:, b, :], x[:, b, :], out_ps[:, 0:D], ALU.add).then_inc(added, 1)
                chain.end()


def bf16(constant):
    import numpy as np
    bits = np.ascontiguousarray(constant, np.float32).view(np.uint32) >> 16
    return np.ascontiguousarray(bits.astype(np.uint16)).view(np.float32)


def _layout(a):
    import numpy as np
    f = np.float32
    out = {}
    p = np.arange(P)
    out["identity"] = np.eye(P, dtype=f)
    out["ident_bf"] = bf16(np.eye(P))
    neg = np.where(p[None, :] > p[:, None], NEG, 0.0)
    out["future_bf"] = bf16(np.broadcast_to(neg[:, None], (P, 4, P)))
    out["past_bf"] = bf16(np.broadcast_to(neg.T[:, None], (P, 4, P)))
    out["minus_half"] = np.full((P, B), -0.5, f)
    out["own_cols"] = np.broadcast_to(((p[None, :] // 16) % 2 == np.arange(2)[:, None])[None], (P, J, P)).astype(f)
    out["spread"] = (p[:, None] == 16 * (p[None, :] // 16) + ROW_MAX).astype(f)
    out["head_rows"] = (p[:, None] // 16 == p[None, :] // 16).astype(f)
    out["head_first"] = (p[:, None] == 16 * np.arange(8)[None, :]).astype(f)
    out["row_head"] = np.broadcast_to((p[:, None] // 16 == np.arange(8)[None, :])[:, None], (P, T, 8)).astype(f)
    out["ones_col"] = np.ones((P, 1), f)
    out["x"] = a["x"].transpose(1, 0, 2)
    out["ctxT"] = a["ctx_1024"].transpose(2, 0, 1)
    out["mask_bytes"] = np.broadcast_to(a["mask_BxS2_bk0"].view(np.uint32)[None], (P, B, S // 4))

    def heads(w):
        z = np.zeros(w.shape[:-1] + (NH, 16), f)
        z[..., :HD] = w.reshape(w.shape[:-1] + (NH, HD))
        return z.reshape(w.shape[:-1] + (T, P))

    def by_j(w):
        z = np.zeros(w.shape[:-1] + (J, P), f)
        for j in range(J):
            z[..., j, (p // 16) % 2 == j] = w[..., (p // 16) % 2 == j]
        return z

    for tag, wq, wk, wv, wo, bq, bk, bv, bo in (
        ("l0", a["L0_xattn_wq"], a["L0_xattn_wk"], a["L0_xattn_wv"], a["L0_xattn_wo"],
         a["L0_xattn_bq"], a["L0_xattn_bk"], a["L0_xattn_bv"], a["L0_xattn_bo"]),
        ("l1", a["L1_xattn_Wq"].T, a["L1_xattn_Wk"].T, a["L1_xattn_Wv"].T, a["L1_xattn_Wo"].T,
         a["L1_xattn_bq"], a["L1_xattn_bk"], a["L1_xattn_bv"], a["L1_xattn_bo"]),
        ("l3", a["L3_xattn_Wq"].T, a["L3_xattn_Wk"].T, a["L3_xattn_Wv"].T, a["L3_xattn_Wo"].T,
         np.zeros(P, f), np.zeros(P, f), np.zeros(P, f), a["L3_xattn_bo"]),
    ):
        out[tag + "_wq"] = by_j(heads(wq))
        out[tag + "_wk"] = heads(wk)
        out[tag + "_wv"] = by_j(heads(wv))
        out[tag + "_wo"] = heads(wo.T).transpose(2, 1, 0)
        out[tag + "_wo"][ROW_MAX, 0, :] = bo
        q, k, v = heads(bq), heads(bk), heads(bv)
        k[:, p % 16 == ROW_MAX] = 1
        v[:, p % 16 == ROW_MAX] = 1
        if tag == "l0":
            q[:, p % 16 == ROW_MASK] = 1
            k[:, p % 16 == ROW_MASK] = 1
        out[tag + "_bq"] = by_j(q).transpose(2, 0, 1)
        out[tag + "_bk"] = k.T
        out[tag + "_bv"] = np.broadcast_to(by_j(v)[None], (P, T, J, P))
    full = MASKED / SCORE_SCALE
    out["l0_mask_mult"] = np.where(p % 16 == ROW_MAX, 0, np.where(p % 16 == ROW_MASK, full, 1))[:, None].astype(f)
    out["l0_mask_add"] = np.where(p % 16 == ROW_MAX, 1, np.where(p % 16 == ROW_MASK, -full, 0))[:, None].astype(f)
    out["l1_w1"] = a["L1_xattn_w1"].T
    out["l1_b1"] = a["L1_xattn_b1"][:, None]
    out["l1_w2"] = np.concatenate([a["L1_xattn_w2"].T, np.zeros((64, 64), f)], axis=1)
    out["l1_b2"] = a["L1_xattn_b2"][:, None]
    out["l1_w3"] = np.broadcast_to(a["L1_xattn_w3"].T, (64, P))
    out["l1_b3"] = np.broadcast_to(a["L1_xattn_b3"][None], (P, 1))
    _layout_ffn(a, out)
    return pack(out)


GROUPS = ("l0", "l0f", "l1", "l1f", "l2", "l2f", "l3", "l3f")
ALONE = ("x", "ctxT")


def group_of(name):
    tag = name.split("_")[0]
    return tag if tag in GROUPS else "common"


def pack(arrays):
    import numpy as np
    packed, where, width = {}, {}, {}
    for name, v in arrays.items():
        if v.dtype != np.float32 or name in ALONE:
            packed[name] = np.ascontiguousarray(v)
            continue
        g = group_of(name)
        flat = np.zeros((P, v[0].size), np.float32)
        flat[:v.shape[0]] = v.reshape(v.shape[0], -1)
        where[name] = (g, width.get(g, 0), v.shape)
        width[g] = width.get(g, 0) + flat.shape[1]
        packed.setdefault(g, []).append(flat)
    return {n: np.concatenate(v, axis=1) if isinstance(v, list) else v for n, v in packed.items()}, where


def _layout_ffn(a, out):
    import numpy as np
    f = np.float32
    p = np.arange(P)
    col = lambda v: v.reshape(-1, P).T if v.size >= P else v[:, None]
    E = 8
    g = lambda n: a["L0_ffn_" + n]
    out["iota8"] = np.broadcast_to(np.arange(E, dtype=f), (P, 4, E))
    out["ones_sq"] = np.ones((P, P), f)
    rows = np.arange(4)[:, None] * 2 + p[None, :] // 64
    e32 = (p % 32)[:, None, None]
    out["pair_rows_bf"] = bf16(rows[None] == e32)
    out["l0f_w_r1"] = g("w_r1")
    out["l0f_b_r1"] = g("b_r1")[:, None]
    out["l0f_w_r2"] = np.concatenate([g("w_r2"), g("b_r2")[None]], 0)
    w1 = np.concatenate([g("expert_w1").transpose(1, 0, 2).reshape(256, 512), g("w_s1")], 1)
    out["l0f_w1"] = w1.reshape(2, P, 576).transpose(1, 0, 2)
    b1 = np.zeros((P, 5), f)
    b1[:, :4] = g("expert_b1").reshape(4, P).T
    b1[:64, 4] = g("b_s1")
    out["l0f_b1"] = b1
    out["l0f_w2"] = g("expert_w2").reshape(4, P, 384).transpose(1, 0, 2)
    b2 = np.zeros((4, 32, 384), f)
    b2[:, :E] = g("expert_b2")
    out["l0f_b2"] = b2.reshape(P, 384)
    out["l0f_w_s2"] = g("w_s2")
    out["l0f_b_s2"] = g("b_s2").reshape(3, P).T
    out["l0f_shared_weight"] = np.broadcast_to(g("shared_weight").reshape(1, 1), (P, 1))
    out["l0f_w_h1"] = g("w_h1")
    out["l0f_b_h1"] = g("b_h1")[:, None]
    out["l0f_w_h2"] = np.broadcast_to(g("w_h2"), (32, P))
    out["l0f_b_h2"] = np.broadcast_to(g("b_h2")[None], (P, 1))
    out["l0f_w_f1"] = g("w_f1")
    out["l0f_b_f1"] = g("b_f1").reshape(2, P).T
    out["l0f_w_f2"] = g("w_f2").reshape(2, P, P).transpose(1, 0, 2)
    out["l0f_b_f2"] = g("b_f2")[:, None]
    out["l0f_integration_weight"] = g("integration_weight")[:, None]
    out["l0f_mu"] = g("mu")[:, None]
    out["iota14"] = np.broadcast_to(np.arange(14, dtype=f), (P, 4, 14))
    out["expert_rows_bf"] = bf16(np.broadcast_to(np.eye(14)[:, :, None], (14, 14, P)))
    out["l1f_router_w"] = a["L1_ffn_router_w"]
    out["l1f_w1"] = a["L1_ffn_w1"].transpose(1, 0, 2).reshape(P, 28, P)
    out["l1f_b1"] = a["L1_ffn_b1"].reshape(28, P).T
    out["l1f_w2"] = a["L1_ffn_w2"].reshape(28, P, P).transpose(1, 0, 2)
    out["l1f_b2"] = a["L1_ffn_b2"]
    out["l3f_weight"] = a["L3_ffn_weight"].T
    out["l3f_gate"] = a["L3_ffn_gate_w"].T
    out["l3f_down"] = a["L3_ffn_lora_U"].reshape(P, P).T
    out["l3f_up"] = a["L3_ffn_lora_V"].transpose(0, 2, 1).reshape(P, P)
    out["iota128"] = np.broadcast_to(np.arange(P, dtype=f), (P, P))
    out["future_f32"] = np.where(p[None, :] > p[:, None], NEG, 0.0).astype(f)
    for n in ("Wq1", "Wk1", "Wv1", "Wq2", "Wk2", "Wv2", "fc1_w", "fc2_w"):
        out["l2_" + n] = a["L2_xattn_" + n]
    out["l2_fc1_b"] = a["L2_xattn_fc1_b"][:, None]
    for n in ("fc2_b", "ln1_g", "ln1_b", "ln2_g", "ln2_b", "ln3_g", "ln3_b"):
        out["l2_" + n] = np.broadcast_to(a["L2_xattn_" + n], (P, P))
    out["l2f_norm_w"] = a["L2_ffn_norm_w"][:, None]
    out["l2f_w_q"] = a["L2_ffn_w_q"].reshape(16, P, P).transpose(1, 0, 2)
    out["l2f_keys"] = a["L2_ffn_keys"].transpose(3, 0, 2, 1).reshape(P, 16, 32)
    out["l2f_down"] = a["L2_ffn_expert_down"].T.reshape(P, 8, P)
    out["l2f_up"] = a["L2_ffn_expert_up"].reshape(8, P, P).transpose(1, 0, 2)


LAYERS = ("l0_xattn", "l0_ffn", "l1_xattn", "l1_ffn", "l2_xattn", "l2_ffn", "l3_xattn", "l3_ffn")
IN_PLACE_OF = {"l2f": "l0f", "l3": "l0"}


def build(nc, dram, where, out, layers=LAYERS):
    with ExitStack() as ctx:
        m, group, loaded = {}, {}, {}
        for n, d in dram.items():
            if n in IN_PLACE_OF:
                continue
            shape = list(d.shape)
            for late, early in IN_PLACE_OF.items():
                if n == early:
                    shape[1] = max(shape[1], dram[late].shape[1])
            group[n] = ctx.enter_context(nc.sbuf_tensor(n + "_in", shape, d.dtype))
        for late, early in IN_PLACE_OF.items():
            group[late] = group[early]
        for n, d in dram.items():
            loaded[n] = ctx.enter_context(nc.semaphore(n + "_loaded"))
            if n not in GROUPS and n != "common":
                m[n] = group[n]
        by_group = {g: {} for g in GROUPS + ("common",)}
        for name, (g, first, shape) in where.items():
            size = 1
            for s in shape[1:]:
                size *= s
            ap = group[g][0:shape[0], first:first + size]
            if name.endswith("_bf"):
                ap, shape = ap.bitcast(BF16), shape[:-1] + (2 * shape[-1],)
            if len(shape) > 2:
                axes = "abcd"[:len(shape) - 1]
                ap = ap.rearrange(f"p ({' '.join(axes)}) -> p {' '.join(axes)}", **dict(zip(axes, shape[1:])))
            if g == "common":
                m[name] = ap
            else:
                by_group[g][name[len(g) + 1:]] = ap
        m["xnT"] = ctx.enter_context(nc.sbuf_tensor("xnT", [P, B, S], F32))
        stored = ctx.enter_context(nc.semaphore("stored"))

        def load(sp, *names):
            for n in names:
                index = (slice(None), slice(0, dram[n].shape[1])) + tuple(slice(None) for _ in dram[n].shape[2:])
                partitions = slice(0, dram[n].shape[0])
                sp.dma_start(group[n][(partitions,) + index[1:]], dram[n]).then_inc(loaded[n], 16)

        def wait(sp, *names):
            for n in names:
                sp.wait_ge(loaded[n], 16)

        with nc.Block() as block:
            @block.sync
            def _(sp):
                load(sp, "x", "common", "l0", "ctxT", *[n for n in m if n in dram and n not in ALONE])
                wait(sp, "x", "common")
                wait(sp, "l0", "ctxT", *[n for n in m if n in dram and n not in ALONE])
                load(sp, "l0f", "l1", "l1f", "l2", "l3f")
        run = [
            ("l0_xattn", multihead, "l0", dict(masked_keys=True), lambda sp: wait(sp, "l0f")),
            ("l0_ffn", refine_experts, "l0f", {}, lambda sp: (load(sp, "l3"), wait(sp, "l1"))),
            ("l1_xattn", multihead, "l1", dict(tempered=True), lambda sp: (load(sp, "l2f"), wait(sp, "l1f"))),
            ("l1_ffn", top1_experts, "l1f", {}, lambda sp: wait(sp, "l2")),
            ("l2_xattn", two_attentions, "l2", {}, lambda sp: wait(sp, "l2f")),
            ("l2_ffn", product_keys, "l2f", {}, lambda sp: wait(sp, "l3")),
            ("l3_xattn", multihead, "l3", dict(causal=True), lambda sp: wait(sp, "l3f")),
            ("l3_ffn", gated_lora, "l3f", {}, lambda sp: None),
        ]
        if layers != LAYERS:
            first = [r[2] for r in run if r[0] == layers[0]][0]
            with nc.Block() as block:
                @block.sync
                def _(sp):
                    if first in IN_PLACE_OF:
                        wait(sp, IN_PLACE_OF[first])
                        load(sp, first)
                    wait(sp, first)
        for name, layer, tag, options, meanwhile in run:
            if name in layers:
                layer(nc, m, by_group[tag], tag, meanwhile if layers == LAYERS else (lambda sp: None), **options)
        with nc.Block() as block:
            @block.sync
            def _(sp):
                sp.dma_start(out, m["x"][:, :, :]).then_inc(stored, 16)
                sp.wait_ge(stored, 16)


def kernel(**inputs):
    import numpy as np
    import concourse.bacc as bacc
    from concourse.bass_utils import run_bass_kernel_spmd

    nc = bacc.Bacc("TRN2", target_bir_lowering=False, num_devices=1)
    arrays, where = _layout({k: np.asarray(v) for k, v in inputs.items()})
    dram = {n: nc.dram_tensor(f"in_{n}", list(v.shape), mybir.dt.from_np(v.dtype), kind="ExternalInput").ap()
            for n, v in arrays.items()}
    out = nc.dram_tensor("out_x", [P, B, D], F32, kind="ExternalOutput").ap()
    build(nc, dram, where, out)
    r = run_bass_kernel_spmd(nc, [{f"in_{n}": v for n, v in arrays.items()}], core_ids=[0])
    return np.ascontiguousarray(r.results[0]["out_x"].transpose(1, 0, 2))
```

```python
import concourse.bass as bass
from concourse import mybir
from contextlib import ExitStack, contextmanager
import math

F32 = mybir.dt.float32
BF16 = mybir.dt.bfloat16
U8 = mybir.dt.uint8
U32 = mybir.dt.uint32
ALU = mybir.AluOpType
ACT = mybir.ActivationFunctionType
AX = mybir.AxisListType

B, S, D = 16, 128, 128
NH, HD = 16, 8
P = 128
T = 2
G = 4
J = 2
ROW_MAX, ROW_MASK = 8, 12
SCORE_SCALE = float(HD) ** -0.5
MASKED = 100000.0
NEG = -1.0e30
LN_EPS, RMS_EPS = 1e-5, 1e-6
LOG_T_MIN, LOG_T_MAX = math.log(0.1), math.log(10.0)
CH = 512
NCH = B * S // CH


@contextmanager
def cleared_semaphores(nc):
    taken = []

    def new_semaphore(name):
        taken.append(nc.alloc_semaphore(name=name))
        return taken[-1]

    yield new_semaphore
    nc.clear_and_free_semaphores(taken)
    nc.all_engine_barrier()


class Banks:

    def __init__(self, names, banks, filled, freed):
        self.place = {}
        self.per_pass = [0] * len(banks)
        for n, name in enumerate(names):
            k = n % len(banks)
            self.place[name] = (k, self.per_pass[k])
            self.per_pass[k] += 1
        self.banks, self.filled, self.freed = banks, filled, freed

    def bank(self, name):
        return self.banks[self.place[name][0]]

    def _value(self, name, i):
        k, n = self.place[name]
        return k, i * self.per_pass[k] + n + 1

    def wait_free(self, pe, name, i):
        k, value = self._value(name, i)
        pe.wait_ge(self.freed[k], value)

    def fill(self, ins, name):
        ins.then_inc(self.filled[self.place[name][0]], 1)

    def wait_filled(self, eng, name, i):
        k, value = self._value(name, i)
        eng.wait_ge(self.filled[k], value)

    def free(self, ins, name):
        ins.then_inc(self.freed[self.place[name][0]], 1)

    def wait_freed(self, eng, name, i):
        k, value = self._value(name, i)
        eng.wait_ge(self.freed[k], value + 1)


class Chain:

    def __init__(self, eng, sem, per_pass):
        self.eng, self.sem, self.per_pass = eng, sem, per_pass
        self.i, self.n = 0, 0

    def begin(self, i):
        self.i, self.n = i, 0

    def __call__(self, ins):
        self.n += 1
        ins.then_inc(self.sem, 1)
        self.eng.wait_ge(self.sem, self.i * self.per_pass + self.n)

    def end(self):
        assert self.n == self.per_pass, (self.n, self.per_pass)


def layernorm(nc, m, tag, rms_gain=None):
    x, xnT, identity = m["x"], m["xnT"], m["identity"]
    with cleared_semaphores(nc) as new_semaphore, ExitStack() as ctx:
        def sb(name, shape):
            return ctx.enter_context(nc.sbuf_tensor(f"{tag}_{name}", shape, F32))

        def sem(name):
            return new_semaphore(f"{tag}_{name}")

        stats = sb("stats", [P, B, 6])
        mean_var = sb("mean_var", [P, B, 2])
        var_eps, square = sb("var_eps", [P, B]), sb("square", [P, B])
        rstd = sb("rstd", [P, B])
        xn = [sb(f"xn{k}", [P, 4, D]) for k in range(2)]
        flipped = [ctx.enter_context(nc.psum_tensor(f"{tag}_flipped{k}", [P, 4, S], F32)) for k in range(2)]
        stats_made = sem("stats_made")
        aggregated = sem("aggregated")
        eps_added = sem("eps_added")
        rstd_made = sem("rstd_made")
        xn_made = [sem(f"xn_made{k}") for k in range(2)]
        xn_flipped = [sem(f"xn_flipped{k}") for k in range(2)]
        xnT_stored = [sem(f"xnT_stored{k}") for k in range(2)]
        block = ctx.enter_context(nc.Block())

        @block.vector
        def _(dve):
            with dve.Fori(0, B) as b:
                nc.vector.bn_stats(stats[:, b, :], x[:, b, :]).then_inc(stats_made, 1)
            dve.wait_ge(stats_made, B)
            for b in range(B):
                nc.vector.bn_aggr(mean_var[:, b, :], stats[:, b, :]).then_inc(aggregated, 1)
            dve.wait_ge(rstd_made, 1)
            with dve.Fori(0, 2) as i:
                for k in range(2):
                    dve.wait_ge(xn_flipped[k], i * 4 + 1)
                    for q in range(4):
                        b = i * 8 + k * 4 + q
                        nc.vector.tensor_scalar(xn[k][:, q, :], x[:, b, :], mean_var[:, b, 0:1],
                                                rstd[:, bass.ds(b, 1)], ALU.subtract, ALU.mult) \
                            .then_inc(xn_made[k], 1)

        @block.gpsimd
        def _(pool):
            pool.wait_ge(aggregated, B)
            nc.gpsimd.tensor_scalar(var_eps[:, :], mean_var[:, :, 1], LN_EPS, None, ALU.add) \
                .then_inc(eps_added, 1)
            pool.wait_ge(eps_added, 1)
            if rms_gain is None:
                nc.gpsimd.tensor_tensor(rstd[:, :], var_eps[:, :], m["minus_half"][:, 0:B], ALU.pow) \
                    .then_inc(rstd_made, 1)
            else:
                own = Chain(pool, eps_added, 0)
                own.n = 1
                TT = nc.gpsimd.tensor_tensor
                own(TT(rstd[:, :], var_eps[:, :], m["minus_half"][:, 0:B], ALU.pow))
                own(TT(square[:, :], rstd[:, :], rstd[:, :], ALU.mult))
                own(TT(square[:, :], square[:, :], mean_var[:, :, 1], ALU.mult))
                own(nc.gpsimd.tensor_scalar(square[:, :], square[:, :], RMS_EPS, None, ALU.add))
                own(TT(var_eps[:, :], square[:, :], m["minus_half"][:, 0:B], ALU.pow))
                TT(rstd[:, :], rstd[:, :], var_eps[:, :], ALU.mult).then_inc(rstd_made, 1)

        @block.tensor
        def _(pe):
            for k in range(2):
                pe.sem_inc(xn_flipped[k], 1)
            with pe.Fori(0, 2) as i:
                for k in range(2):
                    pe.wait_ge(xnT_stored[k], i + 1)
                    for q in range(4):
                        pe.wait_ge(xn_made[k], i * 4 + q + 1)
                        nc.tensor.transpose(flipped[k][:, q, :], xn[k][:, q, :], identity[:, :]) \
                            .then_inc(xn_flipped[k], 1)

        @block.scalar
        def _(act):
            for k in range(2):
                act.sem_inc(xnT_stored[k], 1)
            with act.Fori(0, 2) as i:
                for k in range(2):
                    act.wait_ge(xn_flipped[k], i * 4 + 5)
                    out = xnT[:, bass.ds(i * 8 + k * 4, 4), :]
                    if rms_gain is None:
                        ins = nc.scalar.copy(out, flipped[k][:, :, :])
                    else:
                        ins = nc.scalar.activation(out, flipped[k][:, :, :], ACT.Copy, scale=rms_gain[:, 0:1])
                    ins.then_inc(xnT_stored[k], 1)


def multihead(nc, m, w, tag, meanwhile, masked_keys=False, causal=False, tempered=False):
    layernorm(nc, m, tag + "_ln")
    with ExitStack() as ctx:
        def sb(name, shape):
            m[name] = ctx.enter_context(nc.sbuf_tensor(f"{tag}_{name}", shape, F32))

        sb("q_all", [P, B, T, J, S])
        sb("k_all", [P, B, T, S])
        if tempered:
            for name in ("max_all", "z_all", "z2_all"):
                sb(name, [P, B, G, T, J])
            sb("q_sums", [P, B, T, J])
            sb("k_sums", [P, B, T])
            sb("temper", [P, B, T, J])
        take_maxima(nc, m, w, tag + "_max", masked_keys, causal, tempered)
        if tempered:
            temperatures(nc, m, w, tag + "_net")
        attend(nc, m, w, tag + "_out", meanwhile, causal, tempered)


def take_maxima(nc, m, w, tag, masked_keys, causal, tempered):
    xnT, ctxT, q_all, k_all = m["xnT"], m["ctxT"], m["q_all"], m["k_all"]
    with cleared_semaphores(nc) as new_semaphore, ExitStack() as ctx:
        def sb(name, shape):
            return ctx.enter_context(nc.sbuf_tensor(f"{tag}_{name}", shape, F32))

        def ps(name, shape):
            return ctx.enter_context(nc.psum_tensor(f"{tag}_{name}", shape, F32))

        def sem(name):
            return new_semaphore(f"{tag}_{name}")

        q = [sb(f"q{r}", [P, T, J, S]) for r in range(2)]
        k = [sb(f"k{r}", [P, T, S]) for r in range(2)]
        neg_max = [sb(f"neg_max{r}", [P, P]) for r in range(2)]
        scores = [ps(f"scores{g}", [P, T, J, S]) for g in range(G)]
        q_ps, k_ps = ps("q_ps", [P, 4, S]), ps("k_ps", [P, 4, S])
        flip_ps = ps("flip_ps", [P, 4, S])

        ready = sem("ready")
        q_projected, k_projected = sem("q_projected"), sem("k_projected")
        q_stored, k_stored, k_kept = sem("q_stored"), sem("k_stored"), sem("k_kept")
        scored, max_taken, max_flipped, q_shifted = sem("scored"), sem("max_taken"), sem("max_flipped"), sem("q_shifted")
        if masked_keys:
            key_mask = sb("key_mask", [P, B, S])
            mask_made = sem("mask_made")
        if tempered:
            exps = [sb(f"exps{g}", [P, T, J, S]) for g in range(G)]
            squares = [sb(f"squares{g}", [P, T, J, S]) for g in range(G)]
            bias = sb("bias", [P, T, J])
            exp_done, squared, squares_summed, max_kept = sem("exp_done"), sem("squared"), sem("squares_summed"), sem("max_kept")
        else:
            bias = w["bq"]
        block = ctx.enter_context(nc.Block())

        @block.gpsimd
        def _(pool):
            for r in range(2):
                nc.gpsimd.memset(neg_max[r][:, :], 0.0).then_inc(ready, 1)
            if tempered:
                nc.gpsimd.tensor_scalar(bias[:, :, :], w["bq"][:, :, :], SCORE_SCALE, None, ALU.mult).then_inc(ready, 1)
            with pool.Fori(0, B // 2) as i:
                for r in range(2):
                    b = i * 2 + r
                    pool.wait_ge(k_stored, b + 1)
                    nc.gpsimd.tensor_copy(k_all[:, b, :, :], k[r][:, :, :]).then_inc(k_kept, 1)
                    if tempered:
                        for g in range(G):
                            pool.wait_ge(exp_done, b * G + g + 1)
                            pool.wait_ge(squares_summed, b * G + g + 1)
                            nc.gpsimd.tensor_tensor(squares[g][:, :, :, :], exps[g][:, :, :, :], exps[g][:, :, :, :],
                                                    ALU.mult).then_inc(squared, 1)
                        columns = neg_max[r][:, :].rearrange("p (g c) -> p g c", g=G)[:, :, ROW_MAX:ROW_MAX + T * J]
                        nc.gpsimd.tensor_copy(m["max_all"][:, b].rearrange("p g t j -> p g (t j)"), columns) \
                            .then_inc(max_kept, 1)

        @block.tensor
        def _(pe):
            def project(b):
                for t in range(T):
                    ins = nc.tensor.matmul(q_ps[:, t, :], w["wq"][:, t, :], xnT[:, b, :], start=True, stop=True)
                ins.then_inc(q_projected, 1)
                for t in range(T):
                    ins = nc.tensor.matmul(k_ps[:, t, :], w["wk"][:, t, :], ctxT[:, b, :], start=True, stop=True)
                ins.then_inc(k_projected, 1)

            def flip(b, r):
                pe.wait_ge(max_taken, (b + 1) * G)
                nc.tensor.transpose(flip_ps[:, 0, :], neg_max[r][:, :], m["identity"][:, :]).then_inc(max_flipped, 1)

            def score(b, r, first=False):
                pe.wait_ge(q_stored, b + 1)
                pe.wait_ge(k_stored, b + 1)
                for pair in ((0, 1), (2, 3)) if tempered else (range(G),):
                    for g in pair:
                        if not first:
                            pe.wait_ge(exp_done if tempered else max_taken, (b - 1) * G + g + 1)
                        if causal:
                            nc.tensor.matmul(scores[g][:, :, :, :], m["ident_bf"][:, :], m["future_bf"][:, :, :],
                                             start=True, stop=False, skip_group_check=True)
                    for t in range(T):
                        for j in range(J):
                            for g in pair:
                                rows = slice(32 * g, 32 * g + 32)
                                ins = nc.tensor.matmul(scores[g][:, t, j, :], q[r][rows, t, j, :], k[r][rows, t, :],
                                                       start=not causal, stop=True, skip_group_check=True)
                                if (t, j) == (T - 1, J - 1):
                                    ins.then_inc(scored, 1)

            project(0)
            pe.wait_ge(q_stored, 1)
            pe.wait_ge(k_stored, 1)
            project(1)
            score(0, 0, first=True)
            with pe.Fori(0, B // 2 - 1) as i:
                for r in (1, 0):
                    b = i * 2 + (1 if r else 2)
                    pe.wait_ge(q_stored, b + 1)
                    pe.wait_ge(k_stored, b + 1)
                    project(b + 1)
                    pe.wait_ge(ready, 2)
                    flip(b - 1, 1 - r)
                    score(b, r)
            flip(B - 2, 0)
            score(B - 1, 1)
            flip(B - 1, 1)

        @block.scalar
        def _(act):
            def store_q(b, r):
                act.wait_ge(q_projected, b + 1)
                for t in range(T):
                    for j in range(J):
                        ins = nc.scalar.activation(q[r][:, t, j, :], q_ps[:, t, :], ACT.Identity,
                                                   bias=bias[:, t, j:j + 1], scale=w["q_gain"][:, j:j + 1],
                                                   **(dict(accum_out=m["q_sums"][:, b, t, j:j + 1]) if tempered else {}))
                ins.then_inc(q_stored, 1)
                if not masked_keys:
                    act.wait_ge(k_projected, b + 1)
                    for t in range(T):
                        ins = nc.scalar.activation(k[r][:, t, :], k_ps[:, t, :], ACT.Identity, bias=w["bk"][:, t:t + 1],
                                                   **(dict(accum_out=m["k_sums"][:, b, t:t + 1]) if tempered else {}))
                    ins.then_inc(k_stored, 1)

            def exponentials(b, r):
                for g in range(G):
                    act.wait_ge(max_taken, b * G + g + 1)
                    act.wait_ge(squared, b * G + g + 1)
                    for t in range(T):
                        for j in range(J):
                            column = 32 * g + ROW_MAX + 2 * t + j
                            ins = nc.scalar.activation(exps[g][:, t, j, :], scores[g][:, t, j, :], ACT.Exp,
                                                       bias=neg_max[r][:, column:column + 1],
                                                       accum_out=m["z_all"][:, b, g, t, j:j + 1])
                    ins.then_inc(exp_done, 1)

            if tempered:
                act.sem_inc(squared, G)
                act.wait_ge(ready, 3)
            store_q(0, 0)
            store_q(1, 1)
            with act.Fori(0, B // 2 - 1) as i:
                for r in range(2):
                    b = i * 2 + r
                    if tempered:
                        exponentials(b, r)
                    act.wait_ge(q_shifted, b + 1)
                    act.wait_ge(k_kept, b + 1)
                    store_q(b + 2, r)
            if tempered:
                exponentials(B - 2, 0)
                exponentials(B - 1, 1)

        @block.vector
        def _(dve):
            def store_k(b, r):
                dve.wait_ge(k_projected, b + 1)
                for t in range(T):
                    ins = nc.vector.scalar_tensor_tensor(k[r][:, t, :], k_ps[:, t, :], w["bk"][:, t:t + 1],
                                                         key_mask[:, b, :], ALU.add, ALU.mult)
                ins.then_inc(k_stored, 1)

            def sum_squares(b, g):
                dve.wait_ge(squared, (b + 1) * G + g + 1)
                nc.vector.tensor_reduce(m["z2_all"][:, b, g], squares[g][:, :, :, :], AX.X, ALU.add) \
                    .then_inc(squares_summed, 1)

            def maxima(b, r, sums=True):
                for g in range(G):
                    dve.wait_ge(scored, b * G + g + 1)
                    column = 32 * g + ROW_MAX
                    out = neg_max[r][:, column:column + T * J].rearrange("p (t j) -> p t j", t=T)
                    nc.vector.tensor_reduce(out, scores[g][:, :, :, :], AX.X, ALU.max, negate=True) \
                        .then_inc(max_taken, 1)
                    if tempered and sums:
                        sum_squares(b - 1, g)

            def shift(b, r):
                dve.wait_ge(max_flipped, b + 1)
                for t in range(T):
                    for j in range(J):
                        ins = nc.vector.scalar_tensor_tensor(q_all[:, b, t, j, :], flip_ps[:, 0, :],
                                                             m["max_row"][:, 2 * t + j:2 * t + j + 1], q[r][:, t, j, :],
                                                             ALU.mult, ALU.add)
                ins.then_inc(q_shifted, 1)

            if masked_keys:
                nc.vector.tensor_scalar(key_mask[:, :, :], m["mask_bytes"][:, :, :].bitcast(U8), w["mask_mult"][:, 0:1],
                                        w["mask_add"][:, 0:1], ALU.mult, ALU.add).then_inc(mask_made, 1)
                dve.wait_ge(mask_made, 1)
                store_k(0, 0)
                store_k(1, 1)
            if tempered:
                dve.sem_inc(squares_summed, G)
                dve.sem_inc(max_kept, 1)
            dve.wait_ge(ready, 2)
            maxima(0, 0, sums=False)
            with dve.Fori(0, B // 2 - 1) as i:
                for r in range(2):
                    b = i * 2 + r
                    if masked_keys:
                        dve.wait_ge(k_kept, b + 1)
                        store_k(b + 2, r)
                    shift(b, r)
                    if tempered:
                        dve.wait_ge(max_kept, b + 1)
                    maxima(b + 1, 1 - r)
            shift(B - 2, 0)
            if tempered:
                dve.wait_ge(max_kept, B - 1)
            maxima(B - 1, 1)
            if tempered:
                for g in range(G):
                    sum_squares(B - 1, g)
            shift(B - 1, 1)


def temperatures(nc, m, w, tag):
    with cleared_semaphores(nc) as new_semaphore, ExitStack() as ctx:
        def sb(name, shape):
            return ctx.enter_context(nc.sbuf_tensor(f"{tag}_{name}", shape, F32))

        def ps(name, shape):
            return ctx.enter_context(nc.psum_tensor(f"{tag}_{name}", shape, F32))

        C = B * NH
        q_sum, qk_sum = sb("q_sum", [P, B, T]), sb("qk_sum", [P, B, T])
        qk_heads = sb("qk_heads", [P, B, G, T, J])
        zi, zi2, ratio, excess = (sb(n, [P, B, NH]) for n in ("zi", "zi2", "ratio", "excess"))
        feats, h1, h2 = sb("feats", [3, C]), sb("h1", [64, C]), sb("h2", [64, C])
        log_t, clipped, inv_t = sb("log_t", [P, C]), sb("clipped", [P, C]), sb("inv_t", [P, B, G, T * J])
        own = sb("own", [P, B, G, T * J])
        feats_ps, h1_ps, h2_ps, log_ps = (ps(n, [P, C]) for n in ("feats_ps", "h1_ps", "h2_ps", "log_ps"))
        step, qk_made, variance_made = (new_semaphore(f"{tag}_{n}") for n in ("step", "qk_made", "variance_made"))
        multiplied, moved = new_semaphore(f"{tag}_multiplied"), new_semaphore(f"{tag}_moved")
        block = ctx.enter_context(nc.Block())

        @block.tensor
        def _(pe):
            def product(out, weights, terms, **group):
                return nc.tensor.matmul(out, weights, terms, **(group or dict(start=True, stop=True)))

            product(feats_ps[0:3, :], m["feature_row"][:, 1, :], m["max_all"].rearrange("p b g t j -> p (b g t j)"),
                    start=True, stop=False)
            pe.wait_ge(qk_made, 1)
            product(feats_ps[0:3, :], m["feature_row"][:, 0, :], qk_heads.rearrange("p b g t j -> p (b g t j)"),
                    start=False, stop=False)
            pe.wait_ge(variance_made, 1)
            product(feats_ps[0:3, :], m["feature_row"][:, 2, :], excess.rearrange("p b n -> p (b n)"),
                    start=False, stop=True).then_inc(multiplied, 1)
            pe.wait_ge(moved, 1)
            product(h1_ps[0:64, :], w["w1"][:, :], feats[:, :]).then_inc(multiplied, 1)
            pe.wait_ge(moved, 2)
            product(h2_ps[:, :], w["w2"][:, :], h1[:, :]).then_inc(multiplied, 1)
            pe.wait_ge(moved, 3)
            product(log_ps[:, :], w["w3"][:, :], h2[:, :]).then_inc(multiplied, 1)

        @block.scalar
        def _(act):
            act.wait_ge(multiplied, 1)
            nc.scalar.copy(feats[:, :], feats_ps[0:3, :]).then_inc(moved, 1)
            act.wait_ge(multiplied, 2)
            nc.scalar.activation(h1[:, :], h1_ps[0:64, :], ACT.Gelu, bias=w["b1"][:, 0:1]).then_inc(moved, 1)
            act.wait_ge(multiplied, 3)
            nc.scalar.activation(h2[:, :], h2_ps[0:64, :], ACT.Gelu, bias=w["b2"][:, 0:1]).then_inc(moved, 1)
            act.wait_ge(moved, 4)
            nc.scalar.activation(inv_t.rearrange("p b g c -> p (b g c)"), clipped[:, :], ACT.Exp, scale=-1.0) \
                .then_inc(moved, 1)

        @block.vector
        def _(dve):
            own_step = Chain(dve, step, 0)
            V = nc.vector
            own_step(V.tensor_reduce(q_sum[:, :, :], m["q_sums"][:, :, :, :], AX.X, ALU.add))
            own_step(V.tensor_tensor(qk_sum[:, :, :], q_sum[:, :, :], m["k_sums"][:, :, :], ALU.mult))
            for g in range(G):
                ins = V.tensor_tensor(qk_heads[:, :, g], qk_sum[:, :, :, None].to_broadcast([P, B, T, J]),
                                      m["head_mask"][:, g, None, None, :].to_broadcast([P, B, T, J]), ALU.mult)
            ins.then_inc(qk_made, 1)
            z = m["z_all"].rearrange("p b g t j -> p b (g t j)")
            own_step(V.reciprocal(zi[:, :, :], z))
            own_step(V.tensor_tensor(zi2[:, :, :], zi[:, :, :], zi[:, :, :], ALU.mult))
            own_step(V.tensor_tensor(ratio[:, :, :], zi2[:, :, :], m["z2_all"].rearrange("p b g t j -> p b (g t j)"),
                                     ALU.mult))
            V.tensor_scalar(excess[:, :, :], ratio[:, :, :], 1.0 / S, 1.0 / ((S - 1) * S), ALU.subtract, ALU.mult) \
                .then_inc(variance_made, 1)
            dve.wait_ge(multiplied, 4)
            own_step(V.tensor_scalar(log_t[:, :], log_ps[:, :], w["b3"][:, 0:1], LOG_T_MIN, ALU.add, ALU.max))
            V.tensor_scalar(clipped[:, :], log_t[:, :], LOG_T_MAX, None, ALU.min).then_inc(moved, 1)
            dve.wait_ge(moved, 5)
            for g in range(G):
                ins = V.tensor_scalar(own[:, :, g], inv_t[:, :, g], m["group_mask"][:, g:g + 1], 0.5 / SCORE_SCALE,
                                      ALU.mult, ALU.mult)
            own_step(ins)
            own_step(V.tensor_reduce(m["temper"].rearrange("p b t j -> p b (t j)"),
                                     own.rearrange("p b g c -> p b c g"), AX.X, ALU.add))


def attend(nc, m, w, tag, meanwhile, causal, tempered):
    x, ctxT, q_all, k_all = m["x"], m["ctxT"], m["q_all"], m["k_all"]
    with cleared_semaphores(nc) as new_semaphore, ExitStack() as ctx:
        def sb(name, shape):
            return ctx.enter_context(nc.sbuf_tensor(f"{tag}_{name}", shape, F32))

        def ps(name, shape):
            return ctx.enter_context(nc.psum_tensor(f"{tag}_{name}", shape, F32))

        def sem(name):
            return new_semaphore(f"{tag}_{name}")

        ctx_b = [sb(f"ctx_b{r}", [P, S]) for r in range(2)]
        q = [sb(f"q{r}", [P, T, J, S]) for r in range(2)]
        k = [sb(f"k{r}", [P, T, S]) for r in range(2)]
        v = [sb(f"v{r}", [P, T, J, P]) for r in range(2)]
        probs = [sb(f"probs{r}", [P, G, T, J, S]) for r in range(2)]
        o, recip, o_norm = sb("o", [P, T, S]), sb("recip", [P, T, S]), sb("o_norm", [P, T, S])
        scores = [ps(f"scores{g}", [P, T, J, S]) for g in range(G)]
        v_ps, out_ps = ps("v_ps", [P, 4, P]), ps("out_ps", [P, 4, P])
        o_ps = ps("o_ps", [P, 4, S])

        ready, operands, v_projected, v_stored = sem("ready"), sem("operands"), sem("v_projected"), sem("v_stored")
        scored, exp_done, pv_done, o_stored = sem("scored"), sem("exp_done"), sem("pv_done"), sem("o_stored")
        sums_spread, own, o_scaled = sem("sums_spread"), sem("own"), sem("o_scaled")
        projected, added = sem("projected"), sem("added")
        block = ctx.enter_context(nc.Block())

        @block.sync
        def _(sp):
            meanwhile(sp)

        @block.gpsimd
        def _(pool):
            def fetch(b, r):
                if tempered:
                    nc.gpsimd.tensor_tensor(q[r].rearrange("p t j s -> p (t j) s"),
                                            q_all[:, b].rearrange("p t j s -> p (t j) s"),
                                            m["temper"][:, b].rearrange("p t j -> p (t j)")[:, :, None]
                                            .to_broadcast([P, T * J, S]), ALU.mult)
                else:
                    nc.gpsimd.tensor_copy(q[r][:, :, :, :], q_all[:, b, :, :, :])
                nc.gpsimd.tensor_copy(k[r][:, :, :], k_all[:, b, :, :])
                nc.gpsimd.tensor_copy(ctx_b[r][:, :], ctxT[:, b, :]).then_inc(operands, 1)

            for r in range(2):
                fetch(r, r)
                nc.gpsimd.memset(v[r][:, :, :, :], 0.0).then_inc(ready, 1)
            with pool.Fori(0, B // 2 - 1) as i:
                for r in range(2):
                    b = i * 2 + r
                    pool.wait_ge(scored, (b + 1) * G)
                    pool.wait_ge(v_projected, b + 1)
                    fetch(b + 2, r)

        @block.tensor
        def _(pe):
            def project_v(b, r):
                pe.wait_ge(operands, b + 1)
                nc.tensor.matmul(v_ps[:, 0:T, :], ctx_b[r][:, :], w["wv"][:, :, :], start=True, stop=True) \
                    .then_inc(v_projected, 1)

            def score(b, r, first=False):
                pe.wait_ge(operands, b + 1)
                for pair in ((0, 1), (2, 3)):
                    for g in pair:
                        if not first:
                            pe.wait_ge(exp_done, (b - 1) * G + g + 1)
                        if causal:
                            nc.tensor.matmul(scores[g][:, :, :, :], m["ident_bf"][:, :], m["past_bf"][:, :, :],
                                             start=True, stop=False, skip_group_check=True)
                    for t in range(T):
                        for g in pair:
                            rows = slice(32 * g, 32 * g + 32)
                            ins = nc.tensor.matmul(scores[g][:, t, :, :], k[r][rows, t, :], q[r][rows, t, :, :],
                                                   start=not causal, stop=True, skip_group_check=True)
                            if t == T - 1:
                                ins.then_inc(scored, 1)

            def weigh(b, r):
                pe.wait_ge(exp_done, (b + 1) * G)
                pe.wait_ge(v_stored, b + 1)
                pe.wait_ge(o_scaled, b + 1)
                for t in range(T):
                    for j in range(J):
                        for g in range(G):
                            rows = slice(32 * g, 32 * g + 32)
                            ins = nc.tensor.matmul(o_ps[rows, t, :], v[r][:, t, j, rows], probs[r][:, g, t, j, :],
                                                   start=(j == 0), stop=(j == J - 1))
                ins.then_inc(pv_done, 1)

            def spread(b):
                pe.wait_ge(o_stored, b + 1)
                nc.tensor.matmul(o_ps[:, 2:4, :], m["spread"][:, :], o[:, :, :], start=True, stop=True) \
                    .then_inc(sums_spread, 1)

            def project_out(b):
                pe.wait_ge(o_scaled, b + 2)
                pe.wait_ge(added, b + 1)
                for t in range(T):
                    ins = nc.tensor.matmul(out_ps[:, 0, :], o_norm[:, t, :], w["wo"][:, t, :],
                                           start=(t == 0), stop=(t == T - 1))
                ins.then_inc(projected, 1)

            pe.sem_inc(o_scaled, 1)
            pe.sem_inc(added, 1)
            project_v(0, 0)
            score(0, 0, first=True)
            score(1, 1)
            with pe.Fori(0, B // 2 - 1) as i:
                for r in range(2):
                    b = i * 2 + r
                    weigh(b, r)
                    project_v(b + 1, 1 - r)
                    spread(b)
                    score(b + 2, r)
                    project_out(b)
            weigh(B - 2, 0)
            project_v(B - 1, 1)
            spread(B - 2)
            project_out(B - 2)
            weigh(B - 1, 1)
            spread(B - 1)
            project_out(B - 1)

        @block.scalar
        def _(act):
            def exponentials(b, r):
                for g in range(G):
                    act.wait_ge(scored, b * G + g + 1)
                    nc.scalar.activation(probs[r][:, g], scores[g][:, :, :, :], ACT.Exp,
                                         scale=1.0 if tempered else SCORE_SCALE).then_inc(exp_done, 1)

            exponentials(0, 0)
            exponentials(1, 1)
            with act.Fori(0, B // 2 - 1) as i:
                for r in range(2):
                    act.wait_ge(pv_done, i * 2 + r + 1)
                    exponentials(i * 2 + r + 2, r)

        @block.vector
        def _(dve):
            steps = Chain(dve, own, 3 if tempered else 1)

            def store_v(b, r):
                dve.wait_ge(v_projected, b + 1)
                for j in range(J):
                    def head_j(a):
                        return a.rearrange("p t (g h c) -> p t g h c", g=G, h=J)[:, :, :, j, :]
                    ins = nc.vector.tensor_tensor(head_j(v[r][:, :, j, :]), head_j(v_ps[:, 0:T, :]),
                                                  head_j(w["bv"][:, :, :]), ALU.add)
                ins.then_inc(v_stored, 1)

            def store_o(b):
                dve.wait_ge(pv_done, b + 1)
                if tempered:
                    steps(nc.vector.tensor_scalar(recip[:, :, :], o_ps[:, 0:2, :], 0.0, None, ALU.max))
                    ins = nc.vector.scalar_tensor_tensor(o[:, :, :], o_ps[:, 0:2, :], 0.0, recip[:, :, :],
                                                         ALU.min, ALU.add)
                else:
                    ins = nc.vector.tensor_copy(o[:, :, :], o_ps[:, 0:2, :])
                ins.then_inc(o_stored, 1)

            def normalise(b):
                dve.wait_ge(o_stored, b + 1)
                dve.wait_ge(sums_spread, b + 1)
                if tempered:
                    steps(nc.vector.tensor_scalar(o_norm[:, :, :], o_ps[:, 2:4, :], 0.5, None, ALU.max))
                    steps(nc.vector.reciprocal(recip[:, :, :], o_norm[:, :, :]))
                else:
                    steps(nc.vector.reciprocal(recip[:, :, :], o_ps[:, 2:4, :]))
                nc.vector.tensor_tensor(o_norm[:, :, :], o[:, :, :], recip[:, :, :], ALU.mult).then_inc(o_scaled, 1)

            def add(b):
                dve.wait_ge(projected, b + 1)
                nc.vector.tensor_tensor(x[:, b, :], x[:, b, :], out_ps[:, 0, :], ALU.add).then_inc(added, 1)

            dve.wait_ge(ready, 2)
            store_v(0, 0)
            with dve.Fori(0, B // 2 - 1) as i:
                for r in range(2):
                    b = i * 2 + r
                    steps.begin(b)
                    store_o(b)
                    store_v(b + 1, 1 - r)
                    normalise(b)
                    steps.end()
                    add(b)
            for b in (B - 2, B - 1):
                steps.begin(b)
                store_o(b)
                if b == B - 2:
                    store_v(B - 1, 1)
                normalise(b)
                steps.end()
                add(b)


def refine_experts(nc, m, w, tag, meanwhile):
    E, HID, PAIRS, PARTS, ITERS, DT = 8, 64, 4, 3, 2, 0.1
    ALPHA, BETA, GATE = range(PARTS)
    ORDER = [(BETA, GATE, ALPHA), (ALPHA, GATE, BETA), (BETA, GATE, ALPHA)]
    BRANCHES = 3
    x, xnT, identity = m["x"], m["xnT"], m["identity"]
    layernorm(nc, m, tag + "_ln")
    with cleared_semaphores(nc) as new_semaphore, ExitStack() as ctx:
        def sb(name, shape, dt=F32):
            return ctx.enter_context(nc.sbuf_tensor(f"{tag}_{name}", shape, dt))

        def sem(name):
            return new_semaphore(f"{tag}_{name}")

        def ps(name):
            return ctx.enter_context(nc.psum_tensor(f"{tag}_{name}", [P, CH], F32))

        route = sb("route", [33, CH])
        logits = sb("logits", [P, 4, E])
        best = sb("best", [P, 4, 8])
        best_at = sb("best_at", [P, 4, 8], U32)
        at = sb("at", [P, 4, 2])
        gap, gap_exp, one_more = sb("gap", [P, 4]), sb("gap_exp", [P, 4]), sb("one_more", [P, 4])
        share = sb("share", [P, 4, 2])
        choice = sb("choice", [P, 4, 4, 32])
        choice_t = sb("choice_t", [P, CH])
        choice_bf = sb("choice_bf", [P, CH], BF16)
        mask = sb("mask", [P, 2, PAIRS, CH], BF16)
        weight = sb("weight", [P, 2, CH])
        xi, err, v = sb("xi", [P, CH]), sb("err", [P, CH]), sb("v", [P, CH])
        hidden = sb("hidden", [P, PAIRS + 1, CH])
        chosen = sb("chosen", [P, 2, PAIRS, CH])
        gated = [[sb(f"gated{s}{k}", [P, CH]) for k in range(PARTS)] for s in range(2)]
        abs_b, exp_b = sb("abs_b", [P, CH]), sb("exp_b", [P, CH])
        soft, push, keep = sb("soft", [P, CH]), sb("push", [P, CH]), sb("keep", [P, CH])
        v_new, move, part = sb("v_new", [P, CH]), sb("move", [P, CH]), sb("part", [P, CH])
        v_sum, move_sum, x_next = sb("v_sum", [P, CH]), sb("move_sum", [P, CH]), sb("x_next", [P, CH])
        halt_h, halt, refine = sb("halt_h", [32, CH]), sb("halt", [P, CH]), sb("refine", [P, 2, CH])
        stepped = sb("stepped", [P, CH])
        sw, sw_exp, sw_left = sb("sw", [P, 1]), sb("sw_exp", [P, 1]), sb("sw_left", [P, 1])

        names = ["route", "logits", "choice"]
        names += [f"mask{k}{p}" for k in range(2) for p in range(PAIRS)] + ["weight0", "weight1"]
        for it in range(ITERS):
            names += [f"hidden{it}{p}" for p in range(PAIRS + 1)]
            names += [f"{n}{it}" for n in ("halt_h", "refine_a", "refine_b", "halt", "refined")]
        names += ["out"]
        banks = Banks(names, [ps(f"work{k}") for k in range(2)],
                      [sem(f"work_filled{k}") for k in range(2)], [sem(f"work_freed{k}") for k in range(2)])
        ctl = [[ps(f"ctl{s}{k}") for k in range(PARTS)] for s in range(2)]
        parts_of = [2, 3]
        PER_PASS = BRANCHES * sum(parts_of)
        NB = BRANCHES * ITERS

        ready, sw_ready, sw_exped = sem("ready"), sem("sw_ready"), sem("sw_exped")
        gap_made, gap_exped, choice_made = sem("gap_made"), sem("gap_exped"), sem("choice_made")
        choice_cast = sem("choice_cast")
        x_set, chosen_made = sem("x_set"), sem("chosen_made")
        ctl_filled, ctl_act, ctl_dve = sem("ctl_filled"), sem("ctl_act"), sem("ctl_dve")
        next_made, halt_h_stored, refine_stored, halt_stored = \
            sem("next_made"), sem("halt_h_stored"), sem("refine_stored"), sem("halt_stored")
        v_made = sem("v_made")
        act_step, dve_step = sem("act_step"), sem("dve_step")
        block = ctx.enter_context(nc.Block())

        @block.sync
        def _(sp):
            meanwhile(sp)

        @block.gpsimd
        def _(pool):
            nc.gpsimd.memset(choice[:, :, :, :], 0.0).then_inc(ready, 1)
            pool.wait_ge(ready, 1)
            nc.gpsimd.memset(route[32:33, :], 1.0).then_inc(ready, 1)

        @block.tensor
        def _(pe):
            def mm(out, lhs, rhs, start=True, stop=True):
                return nc.tensor.matmul(out, lhs, rhs, start=start, stop=stop)

            for k in range(2):
                pe.sem_inc(banks.freed[k], 1)
            pe.wait_ge(ready, 2)
            with pe.Fori(0, NCH) as i:
                xn = xnT[:, bass.ds(i * 4, 4), :]
                banks.wait_free(pe, "route", i)
                banks.fill(mm(banks.bank("route")[0:32, :], w["w_r1"][:, :], xn), "route")
                banks.wait_free(pe, "logits", i)
                banks.wait_freed(pe, "route", i)
                for q in range(4):
                    ins = mm(banks.bank("logits")[:, 8 * q:8 * q + 8], route[:, S * q:S * q + S], w["w_r2"][:, :])
                banks.fill(ins, "logits")
                banks.wait_free(pe, "choice", i)
                pe.wait_ge(choice_made, i + 1)
                for q in range(4):
                    ins = nc.tensor.transpose(banks.bank("choice")[:, S * q:S * q + S],
                                              choice[:, q].rearrange("p a e -> p (a e)"), identity[:, :])
                banks.fill(ins, "choice")
                pe.wait_ge(choice_cast, i + 1)
                for k in range(2):
                    r = slice(32 * k, 32 * k + E)
                    for p in range(PAIRS):
                        banks.wait_free(pe, f"mask{k}{p}", i)
                        banks.fill(mm(banks.bank(f"mask{k}{p}")[:, :], m["pair_rows_bf"][r, p, :], choice_bf[r, :]),
                                   f"mask{k}{p}")
                for k in range(2):
                    r = slice(64 + 32 * k, 64 + 32 * k + E)
                    banks.wait_free(pe, f"weight{k}", i)
                    banks.fill(mm(banks.bank(f"weight{k}")[:, :], m["ones_sq"][r, :], choice_t[r, :]), f"weight{k}")
                done = 0
                for it in range(ITERS):
                    pe.wait_ge(x_set, i * 3 + it + 1)
                    for p in range(PAIRS + 1):
                        name = f"hidden{it}{p}"
                        banks.wait_free(pe, name, i)
                        rows = P if p < PAIRS else HID
                        ins = mm(banks.bank(name)[0:rows, :], w["w1"][:, 0, P * p:P * p + rows], xi[:, :],
                                 stop=(it == 0))
                        if it:
                            ins = mm(banks.bank(name)[0:rows, :], w["w1"][:, 1, P * p:P * p + rows], v[:, :],
                                     start=False)
                        banks.fill(ins, name)
                    for r in range(BRANCHES):
                        n = it * BRANCHES + r
                        pe.wait_ge(ctl_act, i * NB + n + 1)
                        pe.wait_ge(ctl_dve, i * NB + n + 1)
                        if r < 2:
                            pe.wait_ge(chosen_made, (i * ITERS + it) * 2 + r + 1)
                        else:
                            banks.wait_freed(pe, f"hidden{it}{PAIRS}", i)
                        for part_ in ORDER[r]:
                            if part_ == ALPHA and it == 0:
                                continue
                            c = slice(P * part_, P * part_ + P)
                            bank = ctl[n % 2][part_]
                            if r < 2:
                                rows = slice(32 * r, 32 * r + E)
                                mm(bank[:, :], w["b2"][rows, c], choice_t[rows, :], stop=False)
                                for p in range(PAIRS):
                                    ins = mm(bank[:, :], w["w2"][:, p, c], chosen[:, r, p, :], start=False,
                                             stop=(p == PAIRS - 1))
                            else:
                                ins = mm(bank[:, :], w["w_s2"][:, c], hidden[0:HID, PAIRS, :])
                            ins.then_inc(ctl_filled, 1)
                    pe.wait_ge(next_made, i * ITERS + it + 1)
                    banks.wait_free(pe, f"halt_h{it}", i)
                    banks.fill(mm(banks.bank(f"halt_h{it}")[0:32, :], w["w_h1"][:, :], x_next[:, :]), f"halt_h{it}")
                    for k, name in enumerate(("refine_a", "refine_b")):
                        banks.wait_free(pe, f"{name}{it}", i)
                        banks.fill(mm(banks.bank(f"{name}{it}")[:, :], w["w_f1"][:, P * k:P * k + P], x_next[:, :]),
                                   f"{name}{it}")
                    banks.wait_free(pe, f"halt{it}", i)
                    pe.wait_ge(halt_h_stored, i * ITERS + it + 1)
                    banks.fill(mm(banks.bank(f"halt{it}")[:, :], w["w_h2"][:, :], halt_h[:, :]), f"halt{it}")
                    banks.wait_free(pe, f"refined{it}", i)
                    pe.wait_ge(refine_stored, (i * ITERS + it + 1) * 2)
                    for k in range(2):
                        ins = mm(banks.bank(f"refined{it}")[:, :], w["w_f2"][:, k, :], refine[:, k, :],
                                 start=(k == 0), stop=(k == 1))
                    banks.fill(ins, f"refined{it}")
                banks.wait_free(pe, "out", i)
                pe.wait_ge(x_set, i * 3 + 3)
                for q in range(4):
                    ins = nc.tensor.transpose(banks.bank("out")[:, S * q:S * q + S], xi[:, S * q:S * q + S],
                                              identity[:, :])
                banks.fill(ins, "out")

        @block.scalar
        def _(act):
            chain = Chain(act, act_step, 12)
            act.sem_inc(ctl_act, 2)
            nc.scalar.activation(sw_exp[:, :], w["shared_weight"][:, :], ACT.Exp, scale=-1.0).then_inc(sw_exped, 1)
            with act.Fori(0, NCH) as i:
                chain.begin(i)
                banks.wait_filled(act, "route", i)
                banks.free(nc.scalar.activation(route[0:32, :], banks.bank("route")[0:32, :], ACT.Gelu,
                                                bias=w["b_r1"][:, 0:1]), "route")
                act.wait_ge(gap_made, i + 1)
                nc.scalar.activation(gap_exp[:, :], gap[:, :], ACT.Exp).then_inc(gap_exped, 1)
                banks.wait_filled(act, "choice", i)
                nc.scalar.copy(choice_bf[:, :], banks.bank("choice")[:, :]).then_inc(choice_cast, 1)
                banks.free(nc.scalar.copy(choice_t[:, :], banks.bank("choice")[:, :]), "choice")
                for k in range(2):
                    for p in range(PAIRS):
                        name = f"mask{k}{p}"
                        banks.wait_filled(act, name, i)
                        banks.free(nc.scalar.copy(mask[:, k, p, :], banks.bank(name)[:, :]), name)
                done = 0
                for it in range(ITERS):
                    for p in range(PAIRS + 1):
                        name = f"hidden{it}{p}"
                        rows = P if p < PAIRS else HID
                        banks.wait_filled(act, name, i)
                        banks.free(nc.scalar.activation(hidden[0:rows, p, :], banks.bank(name)[0:rows, :], ACT.Gelu,
                                                        bias=w["b1"][0:rows, p:p + 1]), name)
                    for r in range(BRANCHES):
                        n = it * BRANCHES + r
                        s = n % 2
                        for part_ in ORDER[r]:
                            if part_ == ALPHA and it == 0:
                                continue
                            done += 1
                            act.wait_ge(ctl_filled, i * PER_PASS + done)
                            bias = dict(bias=w["b_s2"][:, part_:part_ + 1]) if r == 2 else {}
                            if part_ == BETA:
                                chain(nc.scalar.activation(abs_b[:, :], ctl[s][part_][:, :], ACT.Abs, **bias))
                                chain(nc.scalar.activation(exp_b[:, :], abs_b[:, :], ACT.Exp, scale=-1.0))
                                ins = nc.scalar.activation(gated[s][part_][:, :], exp_b[:, :], ACT.Ln, bias=1.0)
                            else:
                                ins = nc.scalar.activation(gated[s][part_][:, :], ctl[s][part_][:, :], ACT.Sigmoid,
                                                           **bias)
                        ins.then_inc(ctl_act, 1)
                    banks.wait_filled(act, f"halt_h{it}", i)
                    nc.scalar.activation(halt_h[:, :], banks.bank(f"halt_h{it}")[0:32, :], ACT.Gelu,
                                         bias=w["b_h1"][:, 0:1]).then_inc(halt_h_stored, 1)
                    act.wait_ge(halt_h_stored, i * ITERS + it + 1)
                    act.sem_inc(banks.freed[banks.place[f"halt_h{it}"][0]], 1)
                    for k, name in enumerate(("refine_a", "refine_b")):
                        banks.wait_filled(act, f"{name}{it}", i)
                        nc.scalar.activation(refine[:, k, :], banks.bank(f"{name}{it}")[:, :], ACT.Gelu,
                                             bias=w["b_f1"][:, k:k + 1]).then_inc(refine_stored, 1)
                        act.wait_ge(refine_stored, (i * ITERS + it) * 2 + k + 1)
                        act.sem_inc(banks.freed[banks.place[f"{name}{it}"][0]], 1)
                    banks.wait_filled(act, f"halt{it}", i)
                    nc.scalar.activation(halt[:, :], banks.bank(f"halt{it}")[:, :], ACT.Sigmoid,
                                         bias=w["b_h2"][:, 0:1]).then_inc(halt_stored, 1)
                    act.wait_ge(halt_stored, i * ITERS + it + 1)
                    act.sem_inc(banks.freed[banks.place[f"halt{it}"][0]], 1)
                chain.end()

        @block.vector
        def _(dve):
            V = nc.vector
            pre = Chain(dve, sw_ready, 0)
            dve.sem_inc(ctl_dve, 2)
            dve.wait_ge(sw_exped, 1)
            pre(V.tensor_scalar(sw_exp[:, :], sw_exp[:, :], 1.0, None, ALU.add))
            pre(V.reciprocal(sw[:, :], sw_exp[:, :]))
            pre(V.tensor_scalar(sw_left[:, :], sw[:, :], -1.0, 1.0, ALU.mult, ALU.add))
            dve.wait_ge(ready, 2)
            chain = Chain(dve, dve_step, 40)
            with dve.Fori(0, NCH) as i:
                chain.begin(i)
                banks.wait_filled(dve, "logits", i)
                banks.free(V.tensor_copy(logits[:, :, :], banks.bank("logits")[:, 0:32]
                                         .rearrange("p (q e) -> p q e", q=4)), "logits")
                banks.wait_freed(dve, "logits", i)
                V.tensor_copy(xi[:, :].rearrange("p (q s) -> p q s", q=4), xnT[:, bass.ds(i * 4, 4), :]) \
                    .then_inc(x_set, 1)
                for q in range(4):
                    ins = V.max(best[:, q, :], logits[:, q, :])
                chain(ins)
                V.tensor_tensor(gap[:, :], best[:, :, 1], best[:, :, 0], ALU.subtract).then_inc(gap_made, 1)
                for q in range(4):
                    ins = V.max_index(best_at[:, q, :], best[:, q, :], logits[:, q, :])
                chain(ins)
                chain(V.tensor_copy(at[:, :, :], best_at[:, :, 0:2]))
                for k in range(2):
                    ins = V.tensor_tensor(choice[:, :, k, 0:E], m["iota8"][:, :, :],
                                          at[:, :, k:k + 1].broadcast_to([P, 4, E]), ALU.is_equal)
                chain(ins)
                dve.wait_ge(gap_exped, i + 1)
                chain(V.tensor_scalar(one_more[:, :], gap_exp[:, :], 1.0, None, ALU.add))
                chain(V.reciprocal(share[:, :, 0], one_more[:, :]))
                chain(V.tensor_tensor(share[:, :, 1], share[:, :, 0], gap_exp[:, :], ALU.mult))
                for k in range(2):
                    ins = V.tensor_tensor(choice[:, :, 2 + k, 0:E], choice[:, :, k, 0:E],
                                          share[:, :, k:k + 1].broadcast_to([P, 4, E]), ALU.mult)
                ins.then_inc(choice_made, 1)
                for k in range(2):
                    banks.wait_filled(dve, f"weight{k}", i)
                    banks.free(V.tensor_scalar(weight[:, k, :], banks.bank(f"weight{k}")[:, :], sw_left[:, 0:1],
                                               None, ALU.mult), f"weight{k}")
                for it in range(ITERS):
                    dve.wait_ge(x_set, i * 3 + it + 1)
                    V.tensor_scalar(err[:, :], xi[:, :], w["mu"][:, 0:1], None, ALU.subtract)
                    for k in range(2):
                        for p in range(PAIRS):
                            if k == 0:
                                banks.wait_freed(dve, f"hidden{it}{p}", i)
                            ins = V.tensor_tensor(chosen[:, k, p, :], hidden[:, p, :], mask[:, k, p, :], ALU.mult)
                        ins.then_inc(chosen_made, 1)
                    for r in range(BRANCHES):
                        n = it * BRANCHES + r
                        s = n % 2
                        dve.wait_ge(ctl_act, i * NB + n + 3)
                        beta = ctl[s][BETA][:, :]
                        if r < 2:
                            chain(V.scalar_tensor_tensor(soft[:, :], beta, 0.0, gated[s][BETA][:, :], ALU.max, ALU.add))
                        else:
                            chain(V.tensor_scalar(part[:, :], beta, w["b_s2"][:, BETA:BETA + 1], 0.0, ALU.add, ALU.max))
                            chain(V.tensor_tensor(soft[:, :], part[:, :], gated[s][BETA][:, :], ALU.add))
                        chain(V.scalar_tensor_tensor(push[:, :], soft[:, :], -1.0, err[:, :], ALU.mult, ALU.mult))
                        fresh = push
                        if it:
                            chain(V.tensor_tensor(keep[:, :], gated[s][ALPHA][:, :], v[:, :], ALU.mult))
                            chain(V.tensor_tensor(v_new[:, :], keep[:, :], push[:, :], ALU.add))
                            fresh = v_new
                        chain(V.tensor_tensor(move[:, :], gated[s][GATE][:, :], fresh[:, :], ALU.mult))
                        for total, term in ((v_sum, fresh), (move_sum, move)):
                            if r == 0:
                                ins = V.tensor_tensor(total[:, :], term[:, :], weight[:, 0, :], ALU.mult)
                            elif r == 1:
                                chain(V.tensor_tensor(part[:, :], term[:, :], weight[:, 1, :], ALU.mult))
                                ins = V.tensor_tensor(total[:, :], total[:, :], part[:, :], ALU.add)
                                if total is v_sum:
                                    chain(ins)
                            else:
                                ins = V.scalar_tensor_tensor(total[:, :], term[:, :], sw[:, 0:1], total[:, :],
                                                             ALU.mult, ALU.add)
                        ins.then_inc(ctl_dve, 1)
                        dve.wait_ge(ctl_dve, i * NB + n + 3)
                    V.scalar_tensor_tensor(x_next[:, :], move_sum[:, :], DT, xi[:, :], ALU.mult, ALU.add) \
                        .then_inc(next_made, 1)
                    if it < ITERS - 1:
                        chain(V.tensor_copy(v[:, :], v_sum[:, :]))
                    banks.wait_filled(dve, f"refined{it}", i)
                    dve.wait_ge(halt_stored, i * ITERS + it + 1)
                    banks.free(V.scalar_tensor_tensor(stepped[:, :], banks.bank(f"refined{it}")[:, :],
                                                      w["b_f2"][:, 0:1], halt[:, :], ALU.add, ALU.mult), f"refined{it}")
                    banks.wait_freed(dve, f"refined{it}", i)
                    V.scalar_tensor_tensor(xi[:, :], stepped[:, :], w["integration_weight"][:, 0:1], xi[:, :],
                                           ALU.mult, ALU.add).then_inc(x_set, 1)
                banks.wait_filled(dve, "out", i)
                xs = x[:, bass.ds(i * 4, 4), :]
                banks.free(V.tensor_tensor(xs, xs, banks.bank("out")[:, :].rearrange("p (q s) -> p q s", q=4),
                                           ALU.add), "out")
                chain.end()


def top1_experts(nc, m, w, tag, meanwhile):
    E, FT = 14, 2
    NT = E * FT
    RING = 4
    x, xnT, identity = m["x"], m["xnT"], m["identity"]
    layernorm(nc, m, tag + "_ln")
    with cleared_semaphores(nc) as new_semaphore, ExitStack() as ctx:
        def sb(name, shape, dt=F32):
            return ctx.enter_context(nc.sbuf_tensor(f"{tag}_{name}", shape, dt))

        def sem(name):
            return new_semaphore(f"{tag}_{name}")

        def ps(name):
            return ctx.enter_context(nc.psum_tensor(f"{tag}_{name}", [P, CH], F32))

        def ring(kind, names, n):
            return Banks(names, [ps(f"{kind}{k}") for k in range(n)],
                         [sem(f"{kind}_filled{k}") for k in range(n)], [sem(f"{kind}_freed{k}") for k in range(n)])

        xc = sb("xc", [P, CH])
        logits = sb("logits", [P, 4, E])
        best, best_at, at = sb("best", [P, 4, 8]), sb("best_at", [P, 4, 8], U32), sb("at", [P, 4])
        neg_best, exps, total, weight = sb("neg_best", [P, 4]), sb("exps", [P, E]), sb("total", [P, 4]), sb("weight", [P, 4])
        choice = sb("choice", [P, 4, P])
        choice_t, choice_bf = sb("choice_t", [E, CH]), sb("choice_bf", [E, CH], BF16)
        hidden = [sb(f"hidden{k}", [P, CH]) for k in range(RING)]
        chosen = [sb(f"chosen{k}", [P, CH]) for k in range(RING)]
        y_t = sb("y_t", [P, CH])
        work = ring("work", ["logits", "choice"] + [f"hidden{n}" for n in range(NT)] + ["out"], 4)
        masks = ring("mask", [f"mask{e}" for e in range(E)], 3)
        acc = ring("acc", ["acc"], 1)
        ready, xc_set, neg_made, total_made, choice_made = \
            sem("ready"), sem("xc_set"), sem("neg_made"), sem("total_made"), sem("choice_made")
        choice_cast, chosen_made, chosen_used = sem("choice_cast"), sem("chosen_made"), sem("chosen_used")
        dve_step, act_step = sem("dve_step"), sem("act_step")
        block = ctx.enter_context(nc.Block())

        @block.sync
        def _(sp):
            meanwhile(sp)

        @block.gpsimd
        def _(pool):
            nc.gpsimd.memset(choice[:, :, :], 0.0).then_inc(ready, 1)

        @block.tensor
        def _(pe):
            mm = nc.tensor.matmul
            for r in (work, masks, acc):
                for s in r.freed:
                    pe.sem_inc(s, 1)
            pe.sem_inc(chosen_used, RING)
            with pe.Fori(0, NCH) as i:
                pe.wait_ge(xc_set, i + 1)
                work.wait_free(pe, "logits", i)
                for q in range(4):
                    ins = mm(work.bank("logits")[:, E * q:E * q + E], xc[:, S * q:S * q + S], w["router_w"][:, :],
                             start=True, stop=True)
                work.fill(ins, "logits")
                work.wait_free(pe, "choice", i)
                pe.wait_ge(choice_made, i + 1)
                for q in range(4):
                    ins = nc.tensor.transpose(work.bank("choice")[:, S * q:S * q + S], choice[:, q, :], identity[:, :])
                work.fill(ins, "choice")

                def second(n):
                    pe.wait_ge(chosen_made, i * NT + n + 1 + RING)
                    mm(acc.bank("acc")[:, :], w["w2"][:, n, :], chosen[n % RING][:, :], start=False,
                       stop=(n == NT - 1)).then_inc(chosen_used, 1)

                LAG = 3
                for n in range(NT + LAG):
                    if n < NT:
                        e = n // FT
                        work.wait_free(pe, f"hidden{n}", i)
                        work.fill(mm(work.bank(f"hidden{n}")[:, :], w["w1"][:, n, :], xc[:, :], start=True, stop=True),
                                  f"hidden{n}")
                        if n % FT == 0:
                            masks.wait_free(pe, f"mask{e}", i)
                            pe.wait_ge(choice_cast, i + 1)
                            masks.fill(mm(masks.bank(f"mask{e}")[:, :], m["expert_rows_bf"][:, e, :], choice_bf[:, :],
                                          start=True, stop=True), f"mask{e}")
                        if n == 1:
                            acc.wait_free(pe, "acc", i)
                            work.wait_freed(pe, "choice", i)
                            mm(acc.bank("acc")[:, :], w["b2"][:, :], choice_t[:, :], start=True, stop=False)
                    if n >= LAG:
                        second(n - LAG)
                work.wait_free(pe, "out", i)
                acc.wait_freed(pe, "acc", i)
                for q in range(4):
                    ins = nc.tensor.transpose(work.bank("out")[:, S * q:S * q + S], y_t[:, S * q:S * q + S],
                                              identity[:, :])
                work.fill(ins, "out")

        @block.scalar
        def _(act):
            A = nc.scalar
            with act.Fori(0, NCH) as i:
                A.copy(xc[:, :].rearrange("p (q s) -> p q s", q=4), xnT[:, bass.ds(i * 4, 4), :]).then_inc(xc_set, 1)
                act.wait_ge(neg_made, i + 1)
                for q in range(4):
                    ins = A.activation(exps[:, :], logits[:, q, :], ACT.Exp, bias=neg_best[:, q:q + 1],
                                       accum_out=total[:, q:q + 1])
                    if q < 3:
                        ins.then_inc(act_step, 1)
                        act.wait_ge(act_step, i * 3 + q + 1)
                ins.then_inc(total_made, 1)
                work.wait_filled(act, "choice", i)
                A.copy(choice_bf[:, :], work.bank("choice")[0:E, :]).then_inc(choice_cast, 1)
                work.free(A.copy(choice_t[:, :], work.bank("choice")[0:E, :]), "choice")
                for n in range(NT):
                    act.wait_ge(chosen_made, i * NT + n + 1)
                    work.wait_filled(act, f"hidden{n}", i)
                    work.free(A.activation(hidden[n % RING][:, :], work.bank(f"hidden{n}")[:, :], ACT.Gelu,
                                           bias=w["b1"][:, n:n + 1]), f"hidden{n}")
                act.wait_ge(chosen_used, i * NT + NT + RING)
                acc.free(A.copy(y_t[:, :], acc.bank("acc")[:, :]), "acc")

        @block.vector
        def _(dve):
            V = nc.vector
            dve.sem_inc(chosen_made, RING)
            chain = Chain(dve, dve_step, 4)
            dve.wait_ge(ready, 1)
            with dve.Fori(0, NCH) as i:
                chain.begin(i)
                work.wait_filled(dve, "logits", i)
                work.free(V.tensor_copy(logits[:, :, :], work.bank("logits")[:, 0:4 * E]
                                        .rearrange("p (q e) -> p q e", q=4)), "logits")
                work.wait_freed(dve, "logits", i)
                V.memset(at[:, :], 0.0)
                for q in range(4):
                    ins = V.max(best[:, q, :], logits[:, q, :])
                chain(ins)
                V.tensor_scalar(neg_best[:, :], best[:, :, 0], -1.0, None, ALU.mult).then_inc(neg_made, 1)
                for q in range(4):
                    ins = V.max_index(best_at[:, q, :], best[:, q, :], logits[:, q, :])
                chain(ins)
                chain(V.tensor_copy(at[:, :], best_at[:, :, 0]))
                V.tensor_tensor(choice[:, :, 0:E], m["iota14"][:, :, :],
                                at[:, :].unsqueeze(2).broadcast_to([P, 4, E]), ALU.is_equal).then_inc(choice_made, 1)
                dve.wait_ge(total_made, i + 1)
                chain(V.reciprocal(weight[:, :], total[:, :]))
                for n in range(NT):
                    e = n // FT
                    if n % FT == 0:
                        masks.wait_filled(dve, f"mask{e}", i)
                    work.wait_freed(dve, f"hidden{n}", i)
                    dve.wait_ge(chosen_used, i * NT + n + 1)
                    V.tensor_tensor(chosen[n % RING][:, :], hidden[n % RING][:, :], masks.bank(f"mask{e}")[:, :],
                                    ALU.mult).then_inc(chosen_made, 1)
                    if n % FT == FT - 1:
                        dve.wait_ge(chosen_made, i * NT + n + 1 + RING)
                        dve.sem_inc(masks.freed[masks.place[f"mask{e}"][0]], 1)
                work.wait_filled(dve, "out", i)
                for q in range(4):
                    xb = x[:, i * 4 + q, :]
                    ins = V.scalar_tensor_tensor(xb, work.bank("out")[:, S * q:S * q + S], weight[:, q:q + 1], xb,
                                                 ALU.mult, ALU.add)
                work.free(ins, "out")
                chain.end()


def gated_lora(nc, m, w, tag, meanwhile):
    E, R = 8, 16
    x, xnT, identity = m["x"], m["xnT"], m["identity"]
    layernorm(nc, m, tag + "_ln")
    with cleared_semaphores(nc) as new_semaphore, ExitStack() as ctx:
        def sb(name, shape, dt=F32):
            return ctx.enter_context(nc.sbuf_tensor(f"{tag}_{name}", shape, dt))

        def sem(name):
            return new_semaphore(f"{tag}_{name}")

        xc = sb("xc", [P, CH])
        neg_top, exps, total, inv = sb("neg_top", [P, 4]), sb("exps", [P, 4, E]), sb("total", [P, 4]), sb("inv", [P, 4])
        gate = sb("gates", [P, 4, E])
        low = sb("low_rank", [P, 4, E, R])
        low_t = sb("low_t", [P, 4, S])
        names = ["gate", "low", "flip", "out"]
        banks = Banks(names, [ctx.enter_context(nc.psum_tensor(f"{tag}_{n}_ps", [P, CH], F32)) for n in names],
                      [sem(f"{n}_filled") for n in names], [sem(f"{n}_freed") for n in names])
        xc_set, neg_made, exps_made, low_made, dve_step = \
            sem("xc_set"), sem("neg_made"), sem("exps_made"), sem("low_made"), sem("dve_step")
        block = ctx.enter_context(nc.Block())

        @block.sync
        def _(sp):
            meanwhile(sp)

        @block.tensor
        def _(pe):
            mm = nc.tensor.matmul
            for s in banks.freed:
                pe.sem_inc(s, 1)
            with pe.Fori(0, NCH) as i:
                pe.wait_ge(xc_set, i + 1)
                banks.wait_free(pe, "gate", i)
                for q in range(4):
                    ins = mm(banks.bank("gate")[:, E * q:E * q + E], xc[:, S * q:S * q + S], w["gate"][:, :],
                             start=True, stop=True)
                banks.fill(ins, "gate")
                banks.wait_free(pe, "low", i)
                for q in range(4):
                    ins = mm(banks.bank("low")[:, S * q:S * q + S], xc[:, S * q:S * q + S], w["down"][:, :],
                             start=True, stop=True)
                banks.fill(ins, "low")
                banks.wait_free(pe, "flip", i)
                pe.wait_ge(low_made, i + 1)
                for q in range(4):
                    ins = nc.tensor.transpose(banks.bank("flip")[:, S * q:S * q + S],
                                              low[:, q].rearrange("p e r -> p (e r)"), identity[:, :])
                banks.fill(ins, "flip")
                banks.wait_free(pe, "out", i)
                banks.wait_freed(pe, "flip", i)
                for q in range(4):
                    o = banks.bank("out")[:, S * q:S * q + S]
                    mm(o, xc[:, S * q:S * q + S], w["weight"][:, :], start=True, stop=False)
                    ins = mm(o, low_t[:, q, :], w["up"][:, :], start=False, stop=True)
                banks.fill(ins, "out")

        @block.scalar
        def _(act):
            A = nc.scalar
            with act.Fori(0, NCH) as i:
                A.copy(xc[:, :].rearrange("p (q s) -> p q s", q=4), xnT[:, bass.ds(i * 4, 4), :]).then_inc(xc_set, 1)
                act.wait_ge(neg_made, i + 1)
                banks.wait_filled(act, "gate", i)
                for q in range(4):
                    ins = A.activation(exps[:, q, :], banks.bank("gate")[:, E * q:E * q + E], ACT.Exp,
                                       bias=neg_top[:, q:q + 1], accum_out=total[:, q:q + 1])
                ins.then_inc(exps_made, 1)
                banks.wait_filled(act, "flip", i)
                banks.free(A.copy(low_t[:, :, :], banks.bank("flip")[:, :].rearrange("p (q s) -> p q s", q=4)), "flip")
                banks.wait_filled(act, "out", i)

        @block.vector
        def _(dve):
            V = nc.vector
            chain = Chain(dve, dve_step, 2)
            with dve.Fori(0, NCH) as i:
                chain.begin(i)
                banks.wait_filled(dve, "gate", i)
                V.tensor_reduce(neg_top[:, :], banks.bank("gate")[:, 0:4 * E].rearrange("p (q e) -> p q e", q=4),
                                AX.X, ALU.max, negate=True).then_inc(neg_made, 1)
                dve.wait_ge(exps_made, i + 1)
                dve.sem_inc(banks.freed[banks.place["gate"][0]], 1)
                chain(V.reciprocal(inv[:, :], total[:, :]))
                chain(V.scalar_tensor_tensor(gate[:, :, :], exps[:, :, :], 1.0 / R,
                                             inv[:, :].unsqueeze(2).broadcast_to([P, 4, E]), ALU.mult, ALU.mult))
                banks.wait_filled(dve, "low", i)
                V.tensor_tensor(low[:, :, :, :].rearrange("p q e r -> p (q e) r"),
                                banks.bank("low")[:, :].rearrange("p (q r) -> p q r", r=R),
                                gate[:, :, :].rearrange("p q e -> p (q e)").unsqueeze(2).broadcast_to([P, 4 * E, R]),
                                ALU.mult).then_inc(low_made, 1)
                dve.wait_ge(low_made, i + 1)
                dve.sem_inc(banks.freed[banks.place["low"][0]], 1)
                banks.wait_filled(dve, "out", i)
                xs = x[:, bass.ds(i * 4, 4), :]
                banks.free(V.tensor_tensor(xs, xs, banks.bank("out")[:, :].rearrange("p (q s) -> p q s", q=4),
                                           ALU.add), "out")
                chain.end()


def two_attentions(nc, m, w, tag, meanwhile):
    x, xnT, ctxT, identity = m["x"], m["xnT"], m["ctxT"], m["identity"]
    layernorm(nc, m, tag + "_ln")
    with cleared_semaphores(nc) as new_semaphore, ExitStack() as ctx:
        def sb(name, shape, dt=F32):
            return ctx.enter_context(nc.sbuf_tensor(f"{tag}_{name}_sb", shape, dt))

        def sem(name):
            return new_semaphore(f"{tag}_{name}")

        Q4 = [P, 4, S]
        xc, ctx_c = sb("xc", Q4), sb("ctx_c", Q4)
        res = [sb("res0", Q4), sb("res1", Q4), sb("res2", Q4)]
        qT, kT, v = sb("qT", Q4), sb("kT", Q4), sb("v", Q4)
        sT = sb("sT", Q4)
        masked, probs, probsT = sb("masked", Q4), sb("probs", Q4), sb("probsT", Q4)
        neg = sb("neg", Q4)
        nonzero, length, length_all = sb("nonzero", [1, 4, S]), sb("length", [1, 4]), sb("length_all", [P, 4])
        neg_max, sums, inv = sb("neg_max", [P, 4]), sb("sums", [P, 4]), sb("inv", [P, 4])
        y, z = sb("y", Q4), sb("z", Q4)
        stats, mean_var = sb("stats", [P, 4, 6]), sb("mean_var", [P, 4, 2])
        var_eps, rstd = sb("var_eps", [P, 4]), sb("rstd", [P, 4])
        hid = sb("hid", Q4)

        names = ["res0"]
        for a in range(2):
            names += [f"{n}{a}" for n in ("q", "k", "v", "scores", "length", "flip", "pv", "xT")]
        names += ["hid", "fc"]
        NB = 7
        banks = Banks(names, [ctx.enter_context(nc.psum_tensor(f"{tag}_bank{k}", Q4, F32)) for k in range(NB)],
                      [sem(f"bank{k}_filled") for k in range(NB)], [sem(f"bank{k}_freed") for k in range(NB)])
        inputs_set, length_made, neg_made, probs_made = sem("inputs_set"), sem("length_made"), sem("neg_made"), sem("probs_made")
        eps_added, rstd_made, stage_made = sem("eps_added"), sem("rstd_made"), sem("stage_made")
        dve_step = sem("dve_step")
        block = ctx.enter_context(nc.Block())

        @block.sync
        def _(sp):
            meanwhile(sp)

        @block.gpsimd
        def _(pool):
            with pool.Fori(0, NCH) as i:
                for n in range(3):
                    pool.wait_ge(eps_added, i * 3 + n + 1)
                    nc.gpsimd.tensor_tensor(rstd[:, :], var_eps[:, :], m["minus_half"][:, 0:4], ALU.pow) \
                        .then_inc(rstd_made, 1)

        @block.tensor
        def _(pe):
            for s in banks.freed:
                pe.sem_inc(s, 1)

            def each(name, i, products):
                banks.wait_free(pe, name, i)
                for out, lhs, rhs in products:
                    ins = nc.tensor.matmul(out, lhs, rhs, start=True, stop=True)
                banks.fill(ins, name)

            def flip(name, i, source):
                banks.wait_free(pe, name, i)
                for q in range(4):
                    ins = nc.tensor.transpose(banks.bank(name)[:, q, :], source[:, q, :], identity[:, :])
                banks.fill(ins, name)

            with pe.Fori(0, NCH) as i:
                pe.wait_ge(inputs_set, i + 1)
                flip("res0", i, xc)
                for a in range(2):
                    b = lambda n: banks.bank(f"{n}{a}")
                    q_in = sT if a else xc
                    kv_in = ctx_c if a else xc
                    if a:
                        banks.wait_freed(pe, "xT0", i)
                    each(f"q{a}", i, [(b("q")[:, :, :], w[f"Wq{a + 1}"][:, :], q_in[:, :, :])])
                    each(f"k{a}", i, [(b("k")[:, :, :], w[f"Wk{a + 1}"][:, :], kv_in[:, :, :])])
                    each(f"v{a}", i, [(b("v")[:, q, :], kv_in[:, q, :], w[f"Wv{a + 1}"][:, :]) for q in range(4)])
                    banks.wait_freed(pe, f"q{a}", i)
                    banks.wait_freed(pe, f"k{a}", i)
                    each(f"scores{a}", i, [(b("scores")[:, q, :], qT[:, q, :], kT[:, q, :]) for q in range(4)])
                    pe.wait_ge(length_made, i * 2 + a + 1)
                    each(f"length{a}", i, [(b("length")[:, 0, 0:4], m["ones_sq"][0:1, :], length[:, :])])
                    pe.wait_ge(probs_made, i * 2 + a + 1)
                    flip(f"flip{a}", i, probs)
                    banks.wait_freed(pe, f"flip{a}", i)
                    banks.wait_freed(pe, f"v{a}", i)
                    each(f"pv{a}", i, [(b("pv")[:, q, :], probsT[:, q, :], v[:, q, :]) for q in range(4)])
                    pe.wait_ge(stage_made, i * 3 + a + 1)
                    flip(f"xT{a}", i, res[a + 1])
                banks.wait_freed(pe, "xT1", i)
                each("hid", i, [(banks.bank("hid")[:, :, :], w["fc1_w"][:, :], sT[:, :, :])])
                banks.wait_freed(pe, "hid", i)
                each("fc", i, [(banks.bank("fc")[:, q, :], hid[:, q, :], w["fc2_w"][:, :]) for q in range(4)])

        @block.scalar
        def _(act):
            A = nc.scalar

            def store(name, i, out):
                banks.wait_filled(act, name, i)
                banks.free(A.copy(out[:, :, :], banks.bank(name)[:, :, :]), name)

            with act.Fori(0, NCH) as i:
                A.copy(xc[:, :, :], xnT[:, bass.ds(i * 4, 4), :])
                A.copy(ctx_c[:, :, :], ctxT[:, bass.ds(i * 4, 4), :]).then_inc(inputs_set, 1)
                store("res0", i, res[0])
                for a in range(2):
                    store(f"q{a}", i, qT)
                    store(f"k{a}", i, kT)
                    act.wait_ge(neg_made, i * 2 + a + 1)
                    for q in range(4):
                        ins = A.activation(probs[:, q, :], masked[:, q, :], ACT.Exp, bias=neg_max[:, q:q + 1],
                                           scale=SCORE_SCALE, accum_out=sums[:, q:q + 1])
                    ins.then_inc(probs_made, 1)
                    store(f"flip{a}", i, probsT)
                    store(f"xT{a}", i, sT)
                banks.wait_filled(act, "hid", i)
                banks.free(A.activation(hid[:, :, :], banks.bank("hid")[:, :, :], ACT.Relu, bias=w["fc1_b"][:, 0:1]),
                           "hid")

        @block.vector
        def _(dve):
            V = nc.vector
            chain = Chain(dve, dve_step, 23)

            def wide(row):
                return row[:, :].unsqueeze(1).broadcast_to(Q4)

            def norm(i, n, out):
                for q in range(4):
                    ins = V.bn_stats(stats[:, q, :], z[:, q, :])
                chain(ins)
                V.memset(var_eps[:, :], LN_EPS)
                for q in range(4):
                    ins = V.bn_aggr(mean_var[:, q, :], stats[:, q, :])
                chain(ins)
                V.tensor_tensor(var_eps[:, :], var_eps[:, :], mean_var[:, :, 1], ALU.add).then_inc(eps_added, 1)
                dve.wait_ge(rstd_made, i * 3 + n + 1)
                for q in range(4):
                    ins = V.tensor_scalar(y[:, q, :], z[:, q, :], mean_var[:, q, 0:1], rstd[:, q:q + 1],
                                          ALU.subtract, ALU.mult)
                chain(ins)
                chain(V.tensor_tensor(z[:, :, :], y[:, :, :], wide(w[f"ln{n + 1}_g"]), ALU.mult))
                V.tensor_tensor(out[:, :, :], z[:, :, :], wide(w[f"ln{n + 1}_b"]), ALU.add).then_inc(stage_made, 1)
                dve.wait_ge(stage_made, i * 3 + n + 1)

            with dve.Fori(0, NCH) as i:
                chain.begin(i)
                banks.wait_freed(dve, "res0", i)
                for a in range(2):
                    name = f"v{a}"
                    banks.wait_filled(dve, name, i)
                    banks.free(V.tensor_copy(v[:, :, :], banks.bank(name)[:, :, :]), name)
                    name = f"scores{a}"
                    banks.wait_filled(dve, name, i)
                    chain(V.tensor_scalar(nonzero[:, :, :], banks.bank(name)[0:1, :, :], 0.0, None, ALU.not_equal))
                    V.tensor_reduce(length[:, :], nonzero[:, :, :], AX.X, ALU.add).then_inc(length_made, 1)
                    banks.wait_filled(dve, f"length{a}", i)
                    banks.free(V.tensor_copy(length_all[:, :], banks.bank(f"length{a}")[:, 0, 0:4]), f"length{a}")
                    banks.wait_freed(dve, f"length{a}", i)
                    for q in range(4):
                        ins = V.tensor_scalar(neg[:, q, :], m["iota128"][:, :], length_all[:, q:q + 1], NEG,
                                              ALU.is_ge, ALU.mult)
                    chain(ins)
                    if a == 0:
                        chain(V.tensor_tensor(neg[:, :, :], neg[:, :, :], wide(m["future_f32"]), ALU.min))
                    banks.free(V.tensor_tensor(masked[:, :, :], neg[:, :, :], banks.bank(name)[:, :, :], ALU.add), name)
                    banks.wait_freed(dve, name, i)
                    chain(V.tensor_reduce(inv[:, :], masked[:, :, :], AX.X, ALU.max, negate=True))
                    V.tensor_scalar(neg_max[:, :], inv[:, :], SCORE_SCALE, None, ALU.mult).then_inc(neg_made, 1)
                    dve.wait_ge(probs_made, i * 2 + a + 1)
                    dve.wait_ge(neg_made, i * 2 + a + 1)
                    chain(V.reciprocal(inv[:, :], sums[:, :]))
                    banks.wait_filled(dve, f"pv{a}", i)
                    for q in range(4):
                        ins = V.scalar_tensor_tensor(z[:, q, :], banks.bank(f"pv{a}")[:, q, :], inv[:, q:q + 1],
                                                     res[a][:, q, :], ALU.mult, ALU.add)
                    banks.free(ins, f"pv{a}")
                    banks.wait_freed(dve, f"pv{a}", i)
                    norm(i, a, res[a + 1])
                banks.wait_filled(dve, "fc", i)
                banks.free(V.tensor_tensor(y[:, :, :], banks.bank("fc")[:, :, :], res[2][:, :, :], ALU.add), "fc")
                banks.wait_freed(dve, "fc", i)
                chain(V.tensor_tensor(z[:, :, :], y[:, :, :], wide(w["fc2_b"]), ALU.add))
                norm(i, 2, y)
                xs = x[:, bass.ds(i * 4, 4), :]
                chain(V.tensor_tensor(xs, xs, y[:, :, :], ALU.add))
                chain.end()


def product_keys(nc, m, w, tag, meanwhile):
    H, K, DK = 8, 32, 128
    E = K * K
    ET = E // P
    x, xnT, identity = m["x"], m["xnT"], m["identity"]
    layernorm(nc, m, tag + "_ln", rms_gain=w["norm_w"])
    with cleared_semaphores(nc) as new_semaphore, ExitStack() as ctx:
        def sb(name, shape, dt=F32):
            return ctx.enter_context(nc.sbuf_tensor(f"{tag}_{name}_sb", shape, dt))

        def sem(name):
            return new_semaphore(f"{tag}_{name}")

        def ps(name, shape):
            return ctx.enter_context(nc.psum_tensor(f"{tag}_{name}", shape, F32))

        RING = 3
        fold = sb("fold", [P, H, 2, K])
        xb = sb("xb", [P, S])
        sim = sb("sim", [P, H, 2, K])
        top = sb("top", [P, H, 2, 8])
        pairs = sb("pairs", [P, H, 8, 8])
        best = sb("best", [P, H, 8])
        least = sb("least", [P, H])
        sums = [sb(f"sums{k}", [P, K, K]) for k in range(RING)]
        kept = [sb(f"kept{k}", [P, E]) for k in range(RING)]
        hid, given = sb("hid", [P, ET, S]), sb("given", [P, ET, S])
        sim_ps, hid_ps, given_ps, out_ps = ps("sim_ps", [P, 512]), ps("hid_ps", [P, ET, S]), ps("given_ps", [P, ET, S]), \
            ps("out_ps", [P, 512])
        fold_made, fold_stored, xb_set, scored, sim_stored, sums_made, kept_made, kept_flipped = [
            sem(n) for n in ("fold_made", "fold_stored", "xb_set", "scored", "sim_stored", "sums_made", "kept_made",
                             "kept_flipped")]
        hid_made, hid_stored, given_made, out_made, added, least_made = [
            sem(n) for n in ("hid_made", "hid_stored", "given_made", "out_made", "added", "least_made")]
        dve_step = sem("dve_step")
        block = ctx.enter_context(nc.Block())

        @block.sync
        def _(sp):
            meanwhile(sp)

        @block.tensor
        def _(pe):
            mm = nc.tensor.matmul
            for h in range(H):
                for j in range(2):
                    ins = mm(sim_ps[:, (2 * h + j) * K:(2 * h + j) * K + K], w["w_q"][:, 2 * h + j, :],
                             w["keys"][:, 2 * h + j, :], start=True, stop=True)
            ins.then_inc(fold_made, 1)
            pe.wait_ge(fold_stored, 1)
            pe.sem_inc(kept_flipped, RING)
            pe.sem_inc(added, 1)
            with pe.Fori(0, B) as b:
                pe.wait_ge(xb_set, b + 1)
                mm(sim_ps[:, :], xb[:, :], fold[:, :, :, :], start=True, stop=True).then_inc(scored, 1)
                for e in range(ET):
                    ins = mm(hid_ps[:, e, :], w["down"][:, e, :], xb[:, :], start=True, stop=True)
                ins.then_inc(hid_made, 1)
                for h in range(H):
                    pe.wait_ge(kept_made, b * H + h + 1 + RING)
                    for e in range(ET):
                        ins = mm(given_ps[:, e, :], kept[h % RING][:, P * e:P * e + P], identity[:, :],
                                 start=(h == 0 and e % 4 == 0), stop=(h == H - 1), skip_group_check=True)
                    ins.then_inc(kept_flipped, 1)
                pe.wait_ge(given_made, b + 1)
                pe.wait_ge(added, b + 1)
                for e in range(ET):
                    ins = mm(out_ps[:, 0:D], given[:, e, :], w["up"][:, e, :], start=(e == 0), stop=(e == ET - 1))
                ins.then_inc(out_made, 1)

        @block.scalar
        def _(act):
            A = nc.scalar
            act.wait_ge(fold_made, 1)
            A.copy(fold[:, :, :, :].rearrange("p h j k -> p (h j k)"), sim_ps[:, :]).then_inc(fold_stored, 1)
            with act.Fori(0, B) as b:
                A.copy(xb[:, :], xnT[:, b, :]).then_inc(xb_set, 1)
                act.wait_ge(hid_made, b + 1)
                for k in range(2):
                    ins = A.activation(hid[:, 4 * k:4 * k + 4, :], hid_ps[:, 4 * k:4 * k + 4, :], ACT.Gelu)
                ins.then_inc(hid_stored, 1)
                act.wait_ge(out_made, b + 1)

        @block.gpsimd
        def _(pool):
            pool.sem_inc(sums_made, RING)
            with pool.Fori(0, B) as b:
                for h in range(H):
                    if h == 0:
                        pool.wait_ge(sim_stored, b + 1)
                    pool.wait_ge(kept_made, b * H + h + 1)
                    nc.gpsimd.tensor_tensor(sums[h % RING][:, :, :],
                                            sim[:, h, 0, :].unsqueeze(2).broadcast_to([P, K, K]),
                                            sim[:, h, 1, :].unsqueeze(1).broadcast_to([P, K, K]), ALU.add) \
                        .then_inc(sums_made, 1)

        @block.vector
        def _(dve):
            V = nc.vector
            chain = Chain(dve, dve_step, 4)
            dve.sem_inc(kept_made, RING)
            with dve.Fori(0, B) as b:
                chain.begin(b)
                dve.wait_ge(scored, b + 1)
                V.tensor_copy(sim[:, :, :, :].rearrange("p h j k -> p (h j k)"), sim_ps[:, :]).then_inc(sim_stored, 1)
                dve.wait_ge(sim_stored, b + 1)
                V.memset(least[:, :], 0.0)
                for h in range(H):
                    for j in range(2):
                        ins = V.max(top[:, h, j, :], sim[:, h, j, :])
                chain(ins)
                chain(V.tensor_tensor(pairs[:, :, :, :], top[:, :, 0, :].unsqueeze(3).broadcast_to([P, H, 8, 8]),
                                      top[:, :, 1, :].unsqueeze(2).broadcast_to([P, H, 8, 8]), ALU.add))
                V.memset(least[:, :], 0.0)
                for h in range(H):
                    ins = V.max(best[:, h, :], pairs[:, h, :, :])
                chain(ins)
                chain(V.tensor_scalar(least[:, :], best[:, :, 7], 0.0, None, ALU.max))
                for h in range(H):
                    k = h % RING
                    dve.wait_ge(sums_made, b * H + h + 1 + RING)
                    dve.wait_ge(kept_flipped, b * H + h + 1)
                    flat = sums[k][:, :, :].rearrange("p a c -> p (a c)")
                    V.scalar_tensor_tensor(kept[k][:, :], flat, least[:, h:h + 1], flat, ALU.is_ge, ALU.mult) \
                        .then_inc(kept_made, 1)
                dve.wait_ge(hid_stored, b + 1)
                dve.wait_ge(kept_flipped, b * H + H + RING)
                for k in range(2):
                    s = slice(4 * k, 4 * k + 4)
                    ins = V.tensor_tensor(given[:, s, :], hid[:, s, :], given_ps[:, s, :], ALU.mult)
                ins.then_inc(given_made, 1)
                dve.wait_ge(out_made, b + 1)
                V.tensor_tensor(x[:, b, :], x[:, b, :], out_ps[:, 0:D], ALU.add).then_inc(added, 1)
                chain.end()


def bf16(constant):
    import numpy as np
    bits = np.ascontiguousarray(constant, np.float32).view(np.uint32) >> 16
    return np.ascontiguousarray(bits.astype(np.uint16)).view(np.float32)


def _layout(a):
    import numpy as np
    f = np.float32
    out = {}
    p = np.arange(P)
    out["identity"] = np.eye(P, dtype=f)
    out["ident_bf"] = bf16(np.eye(P))
    neg = np.where(p[None, :] > p[:, None], NEG, 0.0)
    out["future_bf"] = bf16(np.broadcast_to(neg[:, None], (P, 4, P)))
    out["past_bf"] = bf16(np.broadcast_to(neg.T[:, None], (P, 4, P)))
    out["minus_half"] = np.full((P, B), -0.5, f)
    out["spread"] = (p[:, None] == 16 * (p[None, :] // 16) + ROW_MAX).astype(f)
    out["max_row"] = (p[:, None] % 32 == ROW_MAX + np.arange(T * J)[None]).astype(f)
    out["group_mask"] = (p[:, None] // 32 == np.arange(G)[None]).astype(f)
    out["head_mask"] = (p[:, None] // 16 == np.arange(8)[None]).reshape(P, G, J).astype(f)
    means = np.zeros((P, 3, 3), f)
    means[:, 0, 0], means[:, 1, 1], means[:, 2, 2] = 1.0 / (S * S), -1.0 / S, 1.0
    out["feature_row"] = means
    out["x"] = a["x"].transpose(1, 0, 2)
    out["ctxT"] = a["ctx_1024"].transpose(2, 0, 1)
    out["mask_bytes"] = np.broadcast_to(a["mask_BxS2_bk0"].view(np.uint32)[None], (P, B, S // 4))

    def heads(w):
        z = np.zeros(w.shape[:-1] + (NH, 16), f)
        z[..., :HD] = w.reshape(w.shape[:-1] + (NH, HD))
        return z.reshape(w.shape[:-1] + (T, P))

    def by_j(w):
        z = np.zeros(w.shape[:-1] + (J, P), f)
        for j in range(J):
            z[..., j, (p // 16) % 2 == j] = w[..., (p // 16) % 2 == j]
        return z

    for tag, wq, wk, wv, wo, bq, bk, bv, bo in (
        ("l0", a["L0_xattn_wq"], a["L0_xattn_wk"], a["L0_xattn_wv"], a["L0_xattn_wo"],
         a["L0_xattn_bq"], a["L0_xattn_bk"], a["L0_xattn_bv"], a["L0_xattn_bo"]),
        ("l1", a["L1_xattn_Wq"].T, a["L1_xattn_Wk"].T, a["L1_xattn_Wv"].T, a["L1_xattn_Wo"].T,
         a["L1_xattn_bq"], a["L1_xattn_bk"], a["L1_xattn_bv"], a["L1_xattn_bo"]),
        ("l3", a["L3_xattn_Wq"].T, a["L3_xattn_Wk"].T, a["L3_xattn_Wv"].T, a["L3_xattn_Wo"].T,
         np.zeros(P, f), np.zeros(P, f), np.zeros(P, f), a["L3_xattn_bo"]),
    ):
        out[tag + "_wq"] = heads(wq)
        out[tag + "_wk"] = heads(wk)
        out[tag + "_wv"] = heads(wv)
        out[tag + "_wo"] = heads(wo.T).transpose(2, 1, 0)
        out[tag + "_wo"][ROW_MAX, 0, :] = bo
        q, k, v = heads(bq), heads(bk), heads(bv)
        k[:, (p % 16 >= ROW_MAX) & (p % 16 < ROW_MASK)] = 1
        v[:, p % 16 == ROW_MAX] = 1
        if tag == "l0":
            q[:, p % 16 == ROW_MASK] = 1
            k[:, p % 16 == ROW_MASK] = 1
        out[tag + "_bq"] = by_j(q).transpose(2, 0, 1)
        out[tag + "_bk"] = k.T
        out[tag + "_bv"] = np.broadcast_to(v[None], (P, T, P))
        own = ((p[:, None] // 16) % 2 == np.arange(J)[None]).astype(f)
        out[tag + "_q_gain"] = own * f(SCORE_SCALE) if tag == "l1" else own
    full = MASKED / SCORE_SCALE
    of_max, of_mask = (p % 16 >= ROW_MAX) & (p % 16 < ROW_MASK), p % 16 == ROW_MASK
    out["l0_mask_mult"] = np.where(of_max, 0, np.where(of_mask, full, 1))[:, None].astype(f)
    out["l0_mask_add"] = np.where(of_max, 1, np.where(of_mask, -full, 0))[:, None].astype(f)
    out["l1_w1"] = a["L1_xattn_w1"].T
    out["l1_b1"] = a["L1_xattn_b1"][:, None]
    out["l1_w2"] = np.concatenate([a["L1_xattn_w2"].T, np.zeros((64, 64), f)], axis=1)
    out["l1_b2"] = a["L1_xattn_b2"][:, None]
    out["l1_w3"] = np.broadcast_to(a["L1_xattn_w3"].T, (64, P))
    out["l1_b3"] = np.broadcast_to(a["L1_xattn_b3"][None], (P, 1))
    _layout_ffn(a, out)
    return pack(out)


GROUPS = ("l0", "l0f", "l1", "l1f", "l2", "l2f", "l3", "l3f")
ALONE = ("x", "ctxT")


def group_of(name):
    tag = name.split("_")[0]
    return tag if tag in GROUPS else "common"


def pack(arrays):
    import numpy as np
    packed, where, width = {}, {}, {}
    for name, v in arrays.items():
        if v.dtype != np.float32 or name in ALONE:
            packed[name] = np.ascontiguousarray(v)
            continue
        g = group_of(name)
        flat = np.zeros((P, v[0].size), np.float32)
        flat[:v.shape[0]] = v.reshape(v.shape[0], -1)
        where[name] = (g, width.get(g, 0), v.shape)
        width[g] = width.get(g, 0) + flat.shape[1]
        packed.setdefault(g, []).append(flat)
    return {n: np.concatenate(v, axis=1) if isinstance(v, list) else v for n, v in packed.items()}, where


def _layout_ffn(a, out):
    import numpy as np
    f = np.float32
    p = np.arange(P)
    col = lambda v: v.reshape(-1, P).T if v.size >= P else v[:, None]
    E = 8
    g = lambda n: a["L0_ffn_" + n]
    out["iota8"] = np.broadcast_to(np.arange(E, dtype=f), (P, 4, E))
    out["ones_sq"] = np.ones((P, P), f)
    rows = np.arange(4)[:, None] * 2 + p[None, :] // 64
    e32 = (p % 32)[:, None, None]
    out["pair_rows_bf"] = bf16(rows[None] == e32)
    out["l0f_w_r1"] = g("w_r1")
    out["l0f_b_r1"] = g("b_r1")[:, None]
    out["l0f_w_r2"] = np.concatenate([g("w_r2"), g("b_r2")[None]], 0)
    w1 = np.concatenate([g("expert_w1").transpose(1, 0, 2).reshape(256, 512), g("w_s1")], 1)
    out["l0f_w1"] = w1.reshape(2, P, 576).transpose(1, 0, 2)
    b1 = np.zeros((P, 5), f)
    b1[:, :4] = g("expert_b1").reshape(4, P).T
    b1[:64, 4] = g("b_s1")
    out["l0f_b1"] = b1
    out["l0f_w2"] = g("expert_w2").reshape(4, P, 384).transpose(1, 0, 2)
    b2 = np.zeros((4, 32, 384), f)
    b2[:, :E] = g("expert_b2")
    out["l0f_b2"] = b2.reshape(P, 384)
    out["l0f_w_s2"] = g("w_s2")
    out["l0f_b_s2"] = g("b_s2").reshape(3, P).T
    out["l0f_shared_weight"] = np.broadcast_to(g("shared_weight").reshape(1, 1), (P, 1))
    out["l0f_w_h1"] = g("w_h1")
    out["l0f_b_h1"] = g("b_h1")[:, None]
    out["l0f_w_h2"] = np.broadcast_to(g("w_h2"), (32, P))
    out["l0f_b_h2"] = np.broadcast_to(g("b_h2")[None], (P, 1))
    out["l0f_w_f1"] = g("w_f1")
    out["l0f_b_f1"] = g("b_f1").reshape(2, P).T
    out["l0f_w_f2"] = g("w_f2").reshape(2, P, P).transpose(1, 0, 2)
    out["l0f_b_f2"] = g("b_f2")[:, None]
    out["l0f_integration_weight"] = g("integration_weight")[:, None]
    out["l0f_mu"] = g("mu")[:, None]
    out["iota14"] = np.broadcast_to(np.arange(14, dtype=f), (P, 4, 14))
    out["expert_rows_bf"] = bf16(np.broadcast_to(np.eye(14)[:, :, None], (14, 14, P)))
    out["l1f_router_w"] = a["L1_ffn_router_w"]
    out["l1f_w1"] = a["L1_ffn_w1"].transpose(1, 0, 2).reshape(P, 28, P)
    out["l1f_b1"] = a["L1_ffn_b1"].reshape(28, P).T
    out["l1f_w2"] = a["L1_ffn_w2"].reshape(28, P, P).transpose(1, 0, 2)
    out["l1f_b2"] = a["L1_ffn_b2"]
    out["l3f_weight"] = a["L3_ffn_weight"].T
    out["l3f_gate"] = a["L3_ffn_gate_w"].T
    out["l3f_down"] = a["L3_ffn_lora_U"].reshape(P, P).T
    out["l3f_up"] = a["L3_ffn_lora_V"].transpose(0, 2, 1).reshape(P, P)
    out["iota128"] = np.broadcast_to(np.arange(P, dtype=f), (P, P))
    out["future_f32"] = np.where(p[None, :] > p[:, None], NEG, 0.0).astype(f)
    for n in ("Wq1", "Wk1", "Wv1", "Wq2", "Wk2", "Wv2", "fc1_w", "fc2_w"):
        out["l2_" + n] = a["L2_xattn_" + n]
    out["l2_fc1_b"] = a["L2_xattn_fc1_b"][:, None]
    for n in ("fc2_b", "ln1_g", "ln1_b", "ln2_g", "ln2_b", "ln3_g", "ln3_b"):
        out["l2_" + n] = np.broadcast_to(a["L2_xattn_" + n], (P, P))
    out["l2f_norm_w"] = a["L2_ffn_norm_w"][:, None]
    out["l2f_w_q"] = a["L2_ffn_w_q"].reshape(16, P, P).transpose(1, 0, 2)
    out["l2f_keys"] = a["L2_ffn_keys"].transpose(3, 0, 2, 1).reshape(P, 16, 32)
    out["l2f_down"] = a["L2_ffn_expert_down"].T.reshape(P, 8, P)
    out["l2f_up"] = a["L2_ffn_expert_up"].reshape(8, P, P).transpose(1, 0, 2)


LAYERS = ("l0_xattn", "l0_ffn", "l1_xattn", "l1_ffn", "l2_xattn", "l2_ffn", "l3_xattn", "l3_ffn")
IN_PLACE_OF = {"l2f": "l0f", "l3": "l0"}


def build(nc, dram, where, out, layers=LAYERS):
    with ExitStack() as ctx:
        m, group, loaded = {}, {}, {}
        for n, d in dram.items():
            if n in IN_PLACE_OF:
                continue
            shape = list(d.shape)
            for late, early in IN_PLACE_OF.items():
                if n == early:
                    shape[1] = max(shape[1], dram[late].shape[1])
            group[n] = ctx.enter_context(nc.sbuf_tensor(n + "_in", shape, d.dtype))
        for late, early in IN_PLACE_OF.items():
            group[late] = group[early]
        for n, d in dram.items():
            loaded[n] = ctx.enter_context(nc.semaphore(n + "_loaded"))
            if n not in GROUPS and n != "common":
                m[n] = group[n]
        by_group = {g: {} for g in GROUPS + ("common",)}
        for name, (g, first, shape) in where.items():
            size = 1
            for s in shape[1:]:
                size *= s
            ap = group[g][0:shape[0], first:first + size]
            if name.endswith("_bf"):
                ap, shape = ap.bitcast(BF16), shape[:-1] + (2 * shape[-1],)
            if len(shape) > 2:
                axes = "abcd"[:len(shape) - 1]
                ap = ap.rearrange(f"p ({' '.join(axes)}) -> p {' '.join(axes)}", **dict(zip(axes, shape[1:])))
            if g == "common":
                m[name] = ap
            else:
                by_group[g][name[len(g) + 1:]] = ap
        m["xnT"] = ctx.enter_context(nc.sbuf_tensor("xnT", [P, B, S], F32))
        stored = ctx.enter_context(nc.semaphore("stored"))

        def load(sp, *names):
            for n in names:
                index = (slice(None), slice(0, dram[n].shape[1])) + tuple(slice(None) for _ in dram[n].shape[2:])
                partitions = slice(0, dram[n].shape[0])
                sp.dma_start(group[n][(partitions,) + index[1:]], dram[n]).then_inc(loaded[n], 16)

        def wait(sp, *names):
            for n in names:
                sp.wait_ge(loaded[n], 16)

        with nc.Block() as block:
            @block.sync
            def _(sp):
                load(sp, "x", "common", "l0", "ctxT", *[n for n in m if n in dram and n not in ALONE])
                wait(sp, "x", "common")
                wait(sp, "l0", "ctxT", *[n for n in m if n in dram and n not in ALONE])
                load(sp, "l0f", "l1", "l1f", "l2", "l3f")
        run = [
            ("l0_xattn", multihead, "l0", dict(masked_keys=True), lambda sp: wait(sp, "l0f")),
            ("l0_ffn", refine_experts, "l0f", {}, lambda sp: (load(sp, "l3"), wait(sp, "l1"))),
            ("l1_xattn", multihead, "l1", dict(tempered=True), lambda sp: (load(sp, "l2f"), wait(sp, "l1f"))),
            ("l1_ffn", top1_experts, "l1f", {}, lambda sp: wait(sp, "l2")),
            ("l2_xattn", two_attentions, "l2", {}, lambda sp: wait(sp, "l2f")),
            ("l2_ffn", product_keys, "l2f", {}, lambda sp: wait(sp, "l3")),
            ("l3_xattn", multihead, "l3", dict(causal=True), lambda sp: wait(sp, "l3f")),
            ("l3_ffn", gated_lora, "l3f", {}, lambda sp: None),
        ]
        if layers != LAYERS:
            first = [r[2] for r in run if r[0] == layers[0]][0]
            with nc.Block() as block:
                @block.sync
                def _(sp):
                    if first in IN_PLACE_OF:
                        wait(sp, IN_PLACE_OF[first])
                        load(sp, first)
                    wait(sp, first)
        for name, layer, tag, options, meanwhile in run:
            if name in layers:
                layer(nc, m, by_group[tag], tag, meanwhile if layers == LAYERS else (lambda sp: None), **options)
        with nc.Block() as block:
            @block.sync
            def _(sp):
                sp.dma_start(out, m["x"][:, :, :]).then_inc(stored, 16)
                sp.wait_ge(stored, 16)


def kernel(**inputs):
    import numpy as np
    import concourse.bacc as bacc
    from concourse.bass_utils import run_bass_kernel_spmd

    nc = bacc.Bacc("TRN2", target_bir_lowering=False, num_devices=1)
    arrays, where = _layout({k: np.asarray(v) for k, v in inputs.items()})
    dram = {n: nc.dram_tensor(f"in_{n}", list(v.shape), mybir.dt.from_np(v.dtype), kind="ExternalInput").ap()
            for n, v in arrays.items()}
    out = nc.dram_tensor("out_x", [P, B, D], F32, kind="ExternalOutput").ap()
    build(nc, dram, where, out)
    r = run_bass_kernel_spmd(nc, [{f"in_{n}": v for n, v in arrays.items()}], core_ids=[0])
    return np.ascontiguousarray(r.results[0]["out_x"].transpose(1, 0, 2))
```

```python
import concourse.bass as bass
from concourse import mybir
from contextlib import ExitStack, contextmanager
import math

F32 = mybir.dt.float32
BF16 = mybir.dt.bfloat16
U8 = mybir.dt.uint8
U32 = mybir.dt.uint32
ALU = mybir.AluOpType
ACT = mybir.ActivationFunctionType
AX = mybir.AxisListType

B, S, D = 16, 128, 128
NH, HD = 16, 8
P = 128
T = 2
HT = 8
QUADS = 4
G = 4
J = 2
ROW_MAX, ROW_MASK = 8, 10
SCORE_SCALE = float(HD) ** -0.5
MASKED = 100000.0
NEG = -1.0e30
LN_EPS, RMS_EPS = 1e-5, 1e-6
LOG_T_MIN, LOG_T_MAX = math.log(0.1), math.log(10.0)
CH = 512
NCH = B * S // CH


@contextmanager
def cleared_semaphores(nc):
    taken = []

    def new_semaphore(name):
        taken.append(nc.alloc_semaphore(name=name))
        return taken[-1]

    yield new_semaphore
    nc.clear_and_free_semaphores(taken)
    nc.all_engine_barrier()


class Banks:

    def __init__(self, names, banks, filled, freed):
        self.place = {}
        self.per_pass = [0] * len(banks)
        for n, name in enumerate(names):
            k = n % len(banks)
            self.place[name] = (k, self.per_pass[k])
            self.per_pass[k] += 1
        self.banks, self.filled, self.freed = banks, filled, freed

    def bank(self, name):
        return self.banks[self.place[name][0]]

    def _value(self, name, i):
        k, n = self.place[name]
        return k, i * self.per_pass[k] + n + 1

    def wait_free(self, pe, name, i):
        k, value = self._value(name, i)
        pe.wait_ge(self.freed[k], value)

    def fill(self, ins, name):
        ins.then_inc(self.filled[self.place[name][0]], 1)

    def wait_filled(self, eng, name, i):
        k, value = self._value(name, i)
        eng.wait_ge(self.filled[k], value)

    def free(self, ins, name):
        ins.then_inc(self.freed[self.place[name][0]], 1)

    def wait_freed(self, eng, name, i):
        k, value = self._value(name, i)
        eng.wait_ge(self.freed[k], value + 1)


class Chain:

    def __init__(self, eng, sem, per_pass):
        self.eng, self.sem, self.per_pass = eng, sem, per_pass
        self.i, self.n = 0, 0

    def begin(self, i):
        self.i, self.n = i, 0

    def __call__(self, ins):
        self.n += 1
        ins.then_inc(self.sem, 1)
        self.eng.wait_ge(self.sem, self.i * self.per_pass + self.n)

    def end(self):
        assert self.n == self.per_pass, (self.n, self.per_pass)


def layernorm(nc, m, tag, rms_gain=None):
    x, xnT, identity = m["x"], m["xnT"], m["identity"]
    with cleared_semaphores(nc) as new_semaphore, ExitStack() as ctx:
        def sb(name, shape):
            return ctx.enter_context(nc.sbuf_tensor(f"{tag}_{name}", shape, F32))

        def sem(name):
            return new_semaphore(f"{tag}_{name}")

        stats = sb("stats", [P, B, 6])
        mean_var = sb("mean_var", [P, B, 2])
        var_eps, square = sb("var_eps", [P, B]), sb("square", [P, B])
        rstd = sb("rstd", [P, B])
        xn = [sb(f"xn{k}", [P, 4, D]) for k in range(2)]
        flipped = [ctx.enter_context(nc.psum_tensor(f"{tag}_flipped{k}", [P, 4, S], F32)) for k in range(2)]
        stats_made = sem("stats_made")
        aggregated = sem("aggregated")
        pool_step = sem("pool_step")
        rstd_made = sem("rstd_made")
        xn_made = [sem(f"xn_made{k}") for k in range(2)]
        xn_flipped = [sem(f"xn_flipped{k}") for k in range(2)]
        xnT_stored = [sem(f"xnT_stored{k}") for k in range(2)]
        block = ctx.enter_context(nc.Block())

        @block.vector
        def _(dve):
            for half in range(2):
                for b in range(half * 8, half * 8 + 8):
                    nc.vector.bn_stats(stats[:, b, :], x[:, b, :]).then_inc(stats_made, 1)
                dve.wait_ge(stats_made, half * 8 + 8)
                for b in range(half * 8, half * 8 + 8):
                    nc.vector.bn_aggr(mean_var[:, b, :], stats[:, b, :]).then_inc(aggregated, 1)
            for i in range(2):
                dve.wait_ge(rstd_made, i + 1)
                for k in range(2):
                    if i:
                        dve.wait_ge(xn_flipped[k], 4)
                    for q in range(4):
                        b = i * 8 + k * 4 + q
                        nc.vector.tensor_scalar(xn[k][:, q, :], x[:, b, :], mean_var[:, b, 0:1], rstd[:, b:b + 1],
                                                ALU.subtract, ALU.mult).then_inc(xn_made[k], 1)

        @block.gpsimd
        def _(pool):
            own = Chain(pool, pool_step, 0)
            TT = nc.gpsimd.tensor_tensor
            for i in range(2):
                h = slice(8 * i, 8 * i + 8)
                pool.wait_ge(aggregated, 8 * i + 8)
                own(nc.gpsimd.tensor_scalar(var_eps[:, h], mean_var[:, h, 1], LN_EPS, None, ALU.add))
                if rms_gain is None:
                    TT(rstd[:, h], var_eps[:, h], m["minus_half"][:, h], ALU.pow).then_inc(rstd_made, 1)
                else:
                    own(TT(rstd[:, h], var_eps[:, h], m["minus_half"][:, h], ALU.pow))
                    own(TT(square[:, h], rstd[:, h], rstd[:, h], ALU.mult))
                    own(TT(square[:, h], square[:, h], mean_var[:, h, 1], ALU.mult))
                    own(nc.gpsimd.tensor_scalar(square[:, h], square[:, h], RMS_EPS, None, ALU.add))
                    own(TT(var_eps[:, h], square[:, h], m["minus_half"][:, h], ALU.pow))
                    TT(rstd[:, h], rstd[:, h], var_eps[:, h], ALU.mult).then_inc(rstd_made, 1)

        @block.tensor
        def _(pe):
            for i in range(2):
                for k in range(2):
                    if i:
                        pe.wait_ge(xnT_stored[k], 1)
                    for q in range(4):
                        pe.wait_ge(xn_made[k], i * 4 + q + 1)
                        nc.tensor.transpose(flipped[k][:, q, :], xn[k][:, q, :], identity[:, :]) \
                            .then_inc(xn_flipped[k], 1)

        @block.scalar
        def _(act):
            for i in range(2):
                for k in range(2):
                    act.wait_ge(xn_flipped[k], i * 4 + 4)
                    out = xnT[:, i * 8 + k * 4:i * 8 + k * 4 + 4, :]
                    if rms_gain is None:
                        ins = nc.scalar.copy(out, flipped[k][:, :, :])
                    else:
                        ins = nc.scalar.activation(out, flipped[k][:, :, :], ACT.Copy, scale=rms_gain[:, 0:1])
                    ins.then_inc(xnT_stored[k], 1)


def multihead(nc, m, w, tag, meanwhile, masked_keys=False, causal=False, tempered=False):
    layernorm(nc, m, tag + "_ln")
    with ExitStack() as ctx:
        def sb(name, shape):
            m[name] = ctx.enter_context(nc.sbuf_tensor(f"{tag}_{name}", shape, F32))

        sb("q_all", [P, B, T, S])
        sb("k_all", [P, B, T, S])
        for r in range(2):
            sb(f"heads_k{r}", [P, T, HT, S])
        if tempered:
            for name in ("max_all", "z_all", "z2_all"):
                sb(name, [P, B, T, HT])
            sb("q_sums", [P, B, T])
            sb("k_sums", [P, B, T])
        take_maxima(nc, m, w, tag + "_max", masked_keys, causal, tempered)
        if tempered:
            temperatures(nc, m, w, tag + "_net")
        attend(nc, m, w, tag + "_out", meanwhile, causal, tempered)


def expand_keys(nc, m, b, heads_k):
    for t in range(T):
        ins = nc.gpsimd.tensor_tensor(heads_k[:, t], m["k_all"][:, b, t, :].unsqueeze(1).broadcast_to([P, HT, S]),
                                      m["row_head"][:, :].unsqueeze(2).broadcast_to([P, HT, S]), ALU.mult)
    return ins


def take_maxima(nc, m, w, tag, masked_keys, causal, tempered):
    xnT, ctxT, q_all, k_all = m["xnT"], m["ctxT"], m["q_all"], m["k_all"]
    with cleared_semaphores(nc) as new_semaphore, ExitStack() as ctx:
        def sb(name, shape):
            return ctx.enter_context(nc.sbuf_tensor(f"{tag}_{name}", shape, F32))

        def ps(name, shape):
            return ctx.enter_context(nc.psum_tensor(f"{tag}_{name}", shape, F32))

        def sem(name):
            return new_semaphore(f"{tag}_{name}")

        q = [sb(f"q{r}", [P, T, S]) for r in range(2)]
        heads_k = [m["heads_k0"], m["heads_k1"]]
        neg_max = [sb(f"neg_max{r}", [P, P]) for r in range(2)]
        scores = [ps(f"scores{c}", [P, 4, S]) for c in range(QUADS)]
        q_ps, k_ps = ps("q_ps", [P, 4, S]), ps("k_ps", [P, 4, S])
        flip_ps = ps("flip_ps", [P, 4, S])

        ready = sem("ready")
        q_projected, k_projected = sem("q_projected"), sem("k_projected")
        q_stored, k_stored, k_expanded = sem("q_stored"), sem("k_stored"), sem("k_expanded")
        scored, max_taken, max_flipped, q_shifted = sem("scored"), sem("max_taken"), sem("max_flipped"), sem("q_shifted")
        if masked_keys:
            key_mask = sb("key_mask", [P, B, S])
            mask_made = sem("mask_made")
        if tempered:
            exps = [sb(f"exps{c}", [P, 4, S]) for c in range(QUADS)]
            bias = sb("bias", [P, T])
            exp_done, squares_summed, max_kept = sem("exp_done"), sem("squares_summed"), sem("max_kept")
        else:
            bias = w["bq"]

        k_by_vector = masked_keys or tempered

        def quad_columns(tile, c):
            t, first = c // 2, 64 * (c % 2) + ROW_MAX + c // 2
            return tile[:, first:first + 49:16]

        block = ctx.enter_context(nc.Block())

        @block.gpsimd
        def _(pool):
            def expand(b, r):
                pool.wait_ge(k_stored, b + 1)
                expand_keys(nc, m, b, heads_k[r]).then_inc(k_expanded, 1)

            def keep_maxima(b, r):
                pool.wait_ge(max_taken, (b + 1) * QUADS)
                for t in range(T):
                    ins = nc.gpsimd.tensor_copy(m["max_all"][:, b, t, :], neg_max[r][:, ROW_MAX + t::16])
                ins.then_inc(max_kept, 1)

            for r in range(2):
                nc.gpsimd.memset(neg_max[r][:, :], 0.0).then_inc(ready, 1)
            if tempered:
                nc.gpsimd.tensor_scalar(bias[:, :], w["bq"][:, :], SCORE_SCALE, None, ALU.mult).then_inc(ready, 1)
            for r in range(2):
                expand(r, r)
            with pool.Fori(0, B // 2 - 1) as i:
                for r in range(2):
                    b = i * 2 + r
                    pool.wait_ge(scored, (b + 1) * QUADS)
                    expand(b + 2, r)
                    if tempered:
                        keep_maxima(b, r)
            if tempered:
                keep_maxima(B - 2, 0)
            pool.wait_ge(scored, (B - 1) * QUADS)
            expand_keys(nc, m, 0, heads_k[0])
            if tempered:
                keep_maxima(B - 1, 1)

        @block.tensor
        def _(pe):
            def project_q(b):
                for t in range(T):
                    ins = nc.tensor.matmul(q_ps[:, t, :], w["wq"][:, t, :], xnT[:, b, :], start=True, stop=True)
                ins.then_inc(q_projected, 1)

            def project_k(b):
                for t in range(T):
                    ins = nc.tensor.matmul(k_ps[:, t, :], w["wk"][:, t, :], ctxT[:, b, :], start=True, stop=True)
                ins.then_inc(k_projected, 1)

            def flip(b, r):
                pe.wait_ge(max_taken, (b + 1) * QUADS)
                nc.tensor.transpose(flip_ps[:, 0, :], neg_max[r][:, :], m["identity"][:, :]).then_inc(max_flipped, 1)

            def score(b, r, first=False):
                pe.wait_ge(q_stored, b + 1)
                pe.wait_ge(k_expanded, b + 1)
                for c in range(QUADS):
                    t, heads = c // 2, slice(4 * (c % 2), 4 * (c % 2) + 4)
                    if not first:
                        pe.wait_ge(exp_done if tempered else max_taken, (b - 1) * QUADS + c + 1)
                    if causal:
                        nc.tensor.matmul(scores[c][:, :, :], m["ident_bf"][:, :], m["future_bf"][:, :, :],
                                         start=True, stop=False)
                    nc.tensor.matmul(scores[c][:, :, :], q[r][:, t, :], heads_k[r][:, t, heads, :],
                                     start=not causal, stop=True).then_inc(scored, 1)

            project_q(0)
            project_k(0)
            pe.wait_ge(k_stored, 1)
            project_k(1)

            def step(b, r, q_too=True, k_too=True, first=False):
                if q_too:
                    pe.wait_ge(q_stored, b + 1)
                    project_q(b + 1)
                if k_too:
                    pe.wait_ge(k_stored, b + 2)
                    project_k(b + 2)
                if not first:
                    flip(b - 1, 1 - r)
                score(b, r, first)

            step(0, 0, first=True)
            pe.wait_ge(ready, 2)
            with pe.Fori(0, B // 2 - 2) as i:
                for r in (1, 0):
                    step(i * 2 + (1 if r else 2), r)
            step(B - 3, 1)
            step(B - 2, 0, k_too=False)
            step(B - 1, 1, q_too=False, k_too=False)
            flip(B - 1, 1)

        @block.scalar
        def _(act):
            def store_q(b, r):
                act.wait_ge(q_projected, b + 1)
                for t in range(T):
                    ins = nc.scalar.activation(q[r][:, t, :], q_ps[:, t, :], ACT.Identity, bias=bias[:, t:t + 1],
                                               **(dict(scale=SCORE_SCALE, accum_out=m["q_sums"][:, b, t:t + 1])
                                                  if tempered else {}))
                ins.then_inc(q_stored, 1)

            def store_k(b):
                if not k_by_vector:
                    act.wait_ge(k_projected, b + 1)
                    for t in range(T):
                        ins = nc.scalar.activation(k_all[:, b, t, :], k_ps[:, t, :], ACT.Identity, bias=w["bk"][:, t:t + 1])
                    ins.then_inc(k_stored, 1)

            def exponentials(b, r):
                if tempered:
                    for c in range(QUADS):
                        t, h0 = c // 2, 4 * (c % 2)
                        act.wait_ge(max_taken, b * QUADS + c + 1)
                        act.wait_ge(squares_summed, b * QUADS + c + 1)
                        for h in range(4):
                            column = 16 * (h0 + h) + ROW_MAX + t
                            ins = nc.scalar.activation(exps[c][:, h, :], scores[c][:, h, :], ACT.Exp,
                                                       bias=neg_max[r][:, column:column + 1],
                                                       accum_out=m["z_all"][:, b, t, h0 + h:h0 + h + 1])
                        ins.then_inc(exp_done, 1)

            def step(b, r, q_too=True, k_too=True):
                if q_too:
                    act.wait_ge(q_shifted, b)
                    store_q(b + 1, 1 - r)
                if k_too:
                    store_k(b + 2)
                exponentials(b, r)

            if tempered:
                act.wait_ge(ready, 3)
            store_q(0, 0)
            store_k(0)
            store_k(1)
            store_q(1, 1)
            store_k(2)
            exponentials(0, 0)
            with act.Fori(0, B // 2 - 2) as i:
                for r in (1, 0):
                    step(i * 2 + (1 if r else 2), r)
            step(B - 3, 1)
            step(B - 2, 0, k_too=False)
            step(B - 1, 1, q_too=False, k_too=False)

        @block.vector
        def _(dve):
            def store_k(b):
                if k_by_vector:
                    dve.wait_ge(k_projected, b + 1)
                    for t in range(T):
                        ins = nc.vector.scalar_tensor_tensor(k_all[:, b, t, :], k_ps[:, t, :], w["bk"][:, t:t + 1],
                                                             key_mask[:, b, :] if masked_keys else m["ones_sq"][:, :],
                                                             ALU.add, ALU.mult,
                                                             **(dict(accum_out=m["k_sums"][:, b, t:t + 1])
                                                                if tempered else {}))
                    ins.then_inc(k_stored, 1)

            def sum_squares(b, c):
                t, h0 = c // 2, 4 * (c % 2)
                dve.wait_ge(exp_done, b * QUADS + c + 1)
                for h in range(4):
                    ins = nc.vector.scalar_tensor_tensor(exps[c][:, h, :], exps[c][:, h, :], 1.0, exps[c][:, h, :],
                                                         ALU.mult, ALU.mult,
                                                         accum_out=m["z2_all"][:, b, t, h0 + h:h0 + h + 1])
                ins.then_inc(squares_summed, 1)

            def maxima(b, r, first=False):
                if tempered and not first:
                    dve.wait_ge(max_kept, b)
                for c in range(QUADS):
                    dve.wait_ge(scored, b * QUADS + c + 1)
                    nc.vector.tensor_reduce(quad_columns(neg_max[r], c), scores[c][:, :, :], AX.X, ALU.max, negate=True) \
                        .then_inc(max_taken, 1)
                    if tempered and not first:
                        sum_squares(b - 1, c)

            def shift(b, r):
                dve.wait_ge(max_flipped, b + 1)
                nc.vector.tensor_tensor(q_all[:, b, :, :], q[r][:, :, :],
                                        flip_ps[:, 0, :].unsqueeze(1).broadcast_to([P, T, S]), ALU.add) \
                    .then_inc(q_shifted, 1)

            if masked_keys:
                nc.vector.tensor_scalar(key_mask[:, :, :], m["mask_bytes"][:, :, :].bitcast(U8), w["mask_mult"][:, 0:1],
                                        w["mask_add"][:, 0:1], ALU.mult, ALU.add).then_inc(mask_made, 1)
                dve.wait_ge(mask_made, 1)
            if tempered:
                dve.sem_inc(squares_summed, QUADS)
                dve.sem_inc(max_kept, 1)
            for b in range(3):
                store_k(b)
            dve.wait_ge(ready, 2)
            maxima(0, 0, first=True)
            with dve.Fori(0, B // 2 - 2) as i:
                for r in range(2):
                    b = i * 2 + r
                    store_k(b + 3)
                    shift(b, r)
                    maxima(b + 1, 1 - r)
            for b, r in ((B - 4, 0), (B - 3, 1), (B - 2, 0)):
                if b == B - 4:
                    store_k(B - 1)
                shift(b, r)
                maxima(b + 1, 1 - r)
            if tempered:
                for c in range(QUADS):
                    sum_squares(B - 1, c)
            shift(B - 1, 1)


def temperatures(nc, m, w, tag):
    with cleared_semaphores(nc) as new_semaphore, ExitStack() as ctx:
        def sb(name, shape):
            return ctx.enter_context(nc.sbuf_tensor(f"{tag}_{name}", shape, F32))

        def ps(name, shape):
            return ctx.enter_context(nc.psum_tensor(f"{tag}_{name}", shape, F32))

        C = B * NH
        qk_sum = sb("qk_sum", [P, B, T])
        qk_heads = sb("qk_heads", [P, B, T, HT])
        zi, zi2, ratio, excess = (sb(n, [P, B, NH]) for n in ("zi", "zi2", "ratio", "excess"))
        feats, h1, h2 = sb("feats", [3, C]), sb("h1", [64, C]), sb("h2", [64, C])
        log_t, clipped, inv_t = sb("log_t", [P, C]), sb("clipped", [P, C]), sb("inv_t", [P, B * T, HT])
        own, temper = sb("own", [P, B * T, HT]), sb("temper", [P, B * T])
        feats_ps, h1_ps, h2_ps, log_ps = (ps(n, [P, C]) for n in ("feats_ps", "h1_ps", "h2_ps", "log_ps"))
        step, qk_made, variance_made = (new_semaphore(f"{tag}_{n}") for n in ("step", "qk_made", "variance_made"))
        multiplied, moved = new_semaphore(f"{tag}_multiplied"), new_semaphore(f"{tag}_moved")
        block = ctx.enter_context(nc.Block())

        @block.tensor
        def _(pe):
            def product(out, weights, terms, **group):
                return nc.tensor.matmul(out, weights, terms, **(group or dict(start=True, stop=True)))

            product(feats_ps[0:3, :], m["feature_row"][:, 1, :], m["max_all"].rearrange("p b t h -> p (b t h)"),
                    start=True, stop=False)
            pe.wait_ge(qk_made, 1)
            product(feats_ps[0:3, :], m["feature_row"][:, 0, :], qk_heads.rearrange("p b t h -> p (b t h)"),
                    start=False, stop=False)
            pe.wait_ge(variance_made, 1)
            product(feats_ps[0:3, :], m["feature_row"][:, 2, :], excess.rearrange("p b n -> p (b n)"),
                    start=False, stop=True).then_inc(multiplied, 1)
            pe.wait_ge(moved, 1)
            product(h1_ps[0:64, :], w["w1"][:, :], feats[:, :]).then_inc(multiplied, 1)
            pe.wait_ge(moved, 2)
            product(h2_ps[:, :], w["w2"][:, :], h1[:, :]).then_inc(multiplied, 1)
            pe.wait_ge(moved, 3)
            product(log_ps[:, :], w["w3"][:, :], h2[:, :]).then_inc(multiplied, 1)

        @block.scalar
        def _(act):
            act.wait_ge(multiplied, 1)
            nc.scalar.copy(feats[:, :], feats_ps[0:3, :]).then_inc(moved, 1)
            act.wait_ge(multiplied, 2)
            nc.scalar.activation(h1[:, :], h1_ps[0:64, :], ACT.Gelu, bias=w["b1"][:, 0:1]).then_inc(moved, 1)
            act.wait_ge(multiplied, 3)
            nc.scalar.activation(h2[:, :], h2_ps[0:64, :], ACT.Gelu, bias=w["b2"][:, 0:1]).then_inc(moved, 1)
            act.wait_ge(moved, 4)
            nc.scalar.activation(inv_t.rearrange("p b h -> p (b h)"), clipped[:, :], ACT.Exp, scale=-1.0) \
                .then_inc(moved, 1)

        @block.vector
        def _(dve):
            own_step = Chain(dve, step, 0)
            V = nc.vector
            own_step(V.tensor_tensor(qk_sum[:, :, :], m["q_sums"][:, :, :], m["k_sums"][:, :, :], ALU.mult))
            V.tensor_tensor(qk_heads.rearrange("p b t h -> p (b t) h"),
                            qk_sum.rearrange("p b t -> p (b t)").unsqueeze(2).broadcast_to([P, B * T, HT]),
                            m["row_head"][:, :].unsqueeze(1).broadcast_to([P, B * T, HT]), ALU.mult).then_inc(qk_made, 1)
            z = m["z_all"].rearrange("p b t h -> p b (t h)")
            own_step(V.reciprocal(zi[:, :, :], z))
            own_step(V.tensor_tensor(zi2[:, :, :], zi[:, :, :], zi[:, :, :], ALU.mult))
            own_step(V.tensor_tensor(ratio[:, :, :], zi2[:, :, :], m["z2_all"].rearrange("p b t h -> p b (t h)"),
                                     ALU.mult))
            V.tensor_scalar(excess[:, :, :], ratio[:, :, :], 1.0 / S, 1.0 / ((S - 1) * S), ALU.subtract, ALU.mult) \
                .then_inc(variance_made, 1)
            dve.wait_ge(multiplied, 4)
            own_step(V.tensor_scalar(log_t[:, :], log_ps[:, :], w["b3"][:, 0:1], LOG_T_MIN, ALU.add, ALU.max))
            V.tensor_scalar(clipped[:, :], log_t[:, :], LOG_T_MAX, None, ALU.min).then_inc(moved, 1)
            dve.wait_ge(moved, 5)
            own_step(V.scalar_tensor_tensor(own[:, :, :], inv_t[:, :, :], 0.5 / SCORE_SCALE,
                                            m["row_head"][:, :].unsqueeze(1).broadcast_to([P, B * T, HT]),
                                            ALU.mult, ALU.mult))
            own_step(V.tensor_reduce(temper[:, :], own[:, :, :], AX.X, ALU.add))
            rows = m["q_all"].rearrange("p b t s -> p (b t) s")
            own_step(V.tensor_tensor(rows, rows, temper[:, :].unsqueeze(2).broadcast_to([P, B * T, S]), ALU.mult))


def attend(nc, m, w, tag, meanwhile, causal, tempered):
    x, ctxT, q_all, k_all = m["x"], m["ctxT"], m["q_all"], m["k_all"]
    with cleared_semaphores(nc) as new_semaphore, ExitStack() as ctx:
        def sb(name, shape):
            return ctx.enter_context(nc.sbuf_tensor(f"{tag}_{name}", shape, F32))

        def ps(name, shape):
            return ctx.enter_context(nc.psum_tensor(f"{tag}_{name}", shape, F32))

        def sem(name):
            return new_semaphore(f"{tag}_{name}")

        ctx_b = [sb(f"ctx_b{r}", [P, S]) for r in range(2)]
        heads_k = [m["heads_k0"], m["heads_k1"]]
        v = [sb(f"v{r}", [P, T, J, P]) for r in range(2)]
        probs = [sb(f"probs{r}", [P, T, HT, S]) for r in range(2)]
        o, recip, o_norm = sb("o", [P, T, S]), sb("recip", [P, T, S]), sb("o_norm", [P, T, S])
        scores = [ps(f"scores{c}", [P, 4, S]) for c in range(QUADS)]
        v_ps, out_ps = ps("v_ps", [P, 4, P]), ps("out_ps", [P, 4, P])
        o_ps = ps("o_ps", [P, 4, S])

        ready, operands, v_projected, v_stored = sem("ready"), sem("operands"), sem("v_projected"), sem("v_stored")
        scored, exp_done, pv_done, o_stored = sem("scored"), sem("exp_done"), sem("pv_done"), sem("o_stored")
        sums_spread, own, o_scaled = sem("sums_spread"), sem("own"), sem("o_scaled")
        projected, added = sem("projected"), sem("added")
        block = ctx.enter_context(nc.Block())

        @block.sync
        def _(sp):
            meanwhile(sp)

        @block.gpsimd
        def _(pool):
            def fetch(b, r):
                if not (isinstance(b, int) and b == 0):
                    expand_keys(nc, m, b, heads_k[r])
                nc.gpsimd.tensor_copy(ctx_b[r][:, :], ctxT[:, b, :]).then_inc(operands, 1)

            for r in range(2):
                fetch(r, r)
                nc.gpsimd.memset(v[r][:, :, :, :], 0.0).then_inc(ready, 1)
            with pool.Fori(0, B // 2 - 1) as i:
                for r in range(2):
                    b = i * 2 + r
                    pool.wait_ge(scored, (b + 1) * QUADS)
                    pool.wait_ge(v_projected, b + 1)
                    fetch(b + 2, r)

        @block.tensor
        def _(pe):
            def project_v(b, r):
                pe.wait_ge(operands, b + 1)
                nc.tensor.matmul(v_ps[:, 0:T, :], ctx_b[r][:, :], w["wv"][:, :, :], start=True, stop=True) \
                    .then_inc(v_projected, 1)

            def score(b, r, first=False):
                pe.wait_ge(operands, b + 1)
                for c in range(QUADS):
                    t = c // 2
                    if not first:
                        pe.wait_ge(exp_done, (b - 1) * QUADS + c + 1)
                    if causal:
                        nc.tensor.matmul(scores[c][:, :, :], m["ident_bf"][:, :], m["past_bf"][:, :, :],
                                         start=True, stop=False, skip_group_check=True)
                    for h in range(4):
                        ins = nc.tensor.matmul(scores[c][:, h, :], heads_k[r][:, t, 4 * (c % 2) + h, :], q_all[:, b, t, :],
                                               start=not causal, stop=True, skip_group_check=True)
                    ins.then_inc(scored, 1)

            def weigh(b, r):
                pe.wait_ge(exp_done, (b + 1) * QUADS)
                pe.wait_ge(v_stored, b + 1)
                pe.wait_ge(o_scaled, b + 1)
                for t in range(T):
                    for j in range(J):
                        for g in range(G):
                            rows = slice(32 * g, 32 * g + 32)
                            ins = nc.tensor.matmul(o_ps[rows, t, :], v[r][:, t, j, rows], probs[r][:, t, 2 * g + j, :],
                                                   start=(j == 0), stop=(j == J - 1))
                ins.then_inc(pv_done, 1)

            def spread(b):
                pe.wait_ge(o_stored, b + 1)
                nc.tensor.matmul(o_ps[:, 2:4, :], m["spread"][:, :], o[:, :, :], start=True, stop=True) \
                    .then_inc(sums_spread, 1)

            def project_out(b):
                pe.wait_ge(o_scaled, b + 2)
                pe.wait_ge(added, b + 1)
                for t in range(T):
                    ins = nc.tensor.matmul(out_ps[:, 0, :], o_norm[:, t, :], w["wo"][:, t, :],
                                           start=(t == 0), stop=(t == T - 1))
                ins.then_inc(projected, 1)

            pe.sem_inc(o_scaled, 1)
            pe.sem_inc(added, 1)
            project_v(0, 0)
            score(0, 0, first=True)
            score(1, 1)
            with pe.Fori(0, B // 2 - 1) as i:
                for r in range(2):
                    b = i * 2 + r
                    weigh(b, r)
                    project_v(b + 1, 1 - r)
                    spread(b)
                    score(b + 2, r)
                    project_out(b)
            weigh(B - 2, 0)
            project_v(B - 1, 1)
            spread(B - 2)
            project_out(B - 2)
            weigh(B - 1, 1)
            spread(B - 1)
            project_out(B - 1)

        @block.scalar
        def _(act):
            def exponentials(b, r):
                for c in range(QUADS):
                    t, heads = c // 2, slice(4 * (c % 2), 4 * (c % 2) + 4)
                    act.wait_ge(scored, b * QUADS + c + 1)
                    nc.scalar.activation(probs[r][:, t, heads, :], scores[c][:, :, :], ACT.Exp,
                                         scale=1.0 if tempered else SCORE_SCALE).then_inc(exp_done, 1)

            exponentials(0, 0)
            exponentials(1, 1)
            with act.Fori(0, B // 2 - 1) as i:
                for r in range(2):
                    act.wait_ge(pv_done, i * 2 + r + 1)
                    exponentials(i * 2 + r + 2, r)

        @block.vector
        def _(dve):
            steps = Chain(dve, own, 3 if tempered else 1)

            def store_v(b, r):
                dve.wait_ge(v_projected, b + 1)
                for j in range(J):
                    def head_j(a):
                        return a.rearrange("p t (g h c) -> p t g h c", g=G, h=J)[:, :, :, j, :]
                    ins = nc.vector.tensor_tensor(head_j(v[r][:, :, j, :]), head_j(v_ps[:, 0:T, :]),
                                                  head_j(w["bv"][:, :, :]), ALU.add)
                ins.then_inc(v_stored, 1)

            def store_o(b):
                dve.wait_ge(pv_done, b + 1)
                if tempered:
                    steps(nc.vector.tensor_scalar(recip[:, :, :], o_ps[:, 0:2, :], 0.0, None, ALU.max))
                    ins = nc.vector.scalar_tensor_tensor(o[:, :, :], o_ps[:, 0:2, :], 0.0, recip[:, :, :],
                                                         ALU.min, ALU.add)
                else:
                    ins = nc.vector.tensor_copy(o[:, :, :], o_ps[:, 0:2, :])
                ins.then_inc(o_stored, 1)

            def normalise(b):
                dve.wait_ge(o_stored, b + 1)
                dve.wait_ge(sums_spread, b + 1)
                if tempered:
                    steps(nc.vector.tensor_scalar(o_norm[:, :, :], o_ps[:, 2:4, :], 0.5, None, ALU.max))
                    steps(nc.vector.reciprocal(recip[:, :, :], o_norm[:, :, :]))
                else:
                    steps(nc.vector.reciprocal(recip[:, :, :], o_ps[:, 2:4, :]))
                nc.vector.tensor_tensor(o_norm[:, :, :], o[:, :, :], recip[:, :, :], ALU.mult).then_inc(o_scaled, 1)

            def add(b):
                dve.wait_ge(projected, b + 1)
                nc.vector.tensor_tensor(x[:, b, :], x[:, b, :], out_ps[:, 0, :], ALU.add).then_inc(added, 1)

            dve.wait_ge(ready, 2)
            store_v(0, 0)
            with dve.Fori(0, B // 2 - 1) as i:
                for r in range(2):
                    b = i * 2 + r
                    steps.begin(b)
                    store_o(b)
                    store_v(b + 1, 1 - r)
                    normalise(b)
                    steps.end()
                    add(b)
            for b in (B - 2, B - 1):
                steps.begin(b)
                store_o(b)
                if b == B - 2:
                    store_v(B - 1, 1)
                normalise(b)
                steps.end()
                add(b)


def refine_experts(nc, m, w, tag, meanwhile):
    E, HID, PAIRS, PARTS, ITERS, DT = 8, 64, 4, 3, 2, 0.1
    ALPHA, BETA, GATE = range(PARTS)
    ORDER = (BETA, ALPHA, GATE)
    BRANCHES = (2, 0, 1)
    x, xnT, identity = m["x"], m["xnT"], m["identity"]
    layernorm(nc, m, tag + "_ln")
    with cleared_semaphores(nc) as new_semaphore, ExitStack() as ctx:
        def sb(name, shape, dt=F32):
            return ctx.enter_context(nc.sbuf_tensor(f"{tag}_{name}", shape, dt))

        def sem(name):
            return new_semaphore(f"{tag}_{name}")

        def ps(name):
            return ctx.enter_context(nc.psum_tensor(f"{tag}_{name}", [P, CH], F32))

        route = sb("route", [33, CH])
        logits = sb("logits", [P, 4, E])
        best = sb("best", [P, 4, 8])
        best_at = sb("best_at", [P, 4, 8], U32)
        at = sb("at", [P, 4, 2])
        gap, gap_exp, one_more = sb("gap", [P, 4]), sb("gap_exp", [P, 4]), sb("one_more", [P, 4])
        share = sb("share", [P, 4, 2])
        choice = sb("choice", [P, 4, 4, 32])
        choice_t = sb("choice_t", [P, CH])
        choice_bf = sb("choice_bf", [P, CH], BF16)
        mask = sb("mask", [P, 2, PAIRS, CH], BF16)
        weight = sb("weight", [P, 2, CH])
        b2_part = sb("b2_part", [P, 2, 384], BF16)
        b2_bf = sb("b2_bf", [P, 2, 384], BF16)
        xi, err, v = sb("xi", [P, CH]), sb("err", [P, CH]), sb("v", [P, CH])
        hidden = sb("hidden", [P, PAIRS + 1, CH])
        chosen = sb("chosen", [P, 2, PAIRS, CH])
        gated = [[sb(f"gated{s}{k}", [P, CH]) for k in range(PARTS)] for s in range(2)]
        abs_b, exp_b = sb("abs_b", [P, CH]), sb("exp_b", [P, CH])
        soft, push, keep = sb("soft", [P, CH]), sb("push", [P, CH]), sb("keep", [P, CH])
        moved = sb("moved", [P, CH])
        v_new, move, part = sb("v_new", [P, CH]), sb("move", [P, CH]), sb("part", [P, CH])
        v_sum, move_sum, x_next = sb("v_sum", [P, CH]), sb("move_sum", [P, CH]), sb("x_next", [P, CH])
        halt_h, halt, refine = sb("halt_h", [32, CH]), sb("halt", [P, CH]), sb("refine", [P, 2, CH])
        stepped = sb("stepped", [P, CH])
        sw, sw_exp, sw_left = sb("sw", [P, 1]), sb("sw_exp", [P, 1]), sb("sw_left", [P, 1])

        HIDDEN = (PAIRS, 0, 1, 2, 3)
        names = ["route"] + [f"hidden0{p}" for p in HIDDEN[:2]] + ["logits"] + [f"hidden0{p}" for p in HIDDEN[2:]]
        names += ["choice"]
        names += [f"mask{k}{p}" for k in range(2) for p in range(PAIRS)] + ["weight0", "weight1"]
        for it in range(ITERS):
            names += [f"hidden{it}{p}" for p in HIDDEN] if it else []
            names += [f"{n}{it}" for n in ("halt_h", "refine_a", "refine_b", "halt", "refined")]
        names += ["out"]
        banks = Banks(names, [ps(f"work{k}") for k in range(2)],
                      [sem(f"work_filled{k}") for k in range(2)], [sem(f"work_freed{k}") for k in range(2)])
        ctl = [[ps(f"ctl{s}{k}") for k in range(PARTS)] for s in range(2)]
        parts_of = [2, 3]
        PER_PASS = len(BRANCHES) * sum(parts_of)
        NB = len(BRANCHES) * ITERS

        ready, sw_ready, sw_exped = sem("ready"), sem("sw_ready"), sem("sw_exped")
        gap_made, gap_exped, choice_made = sem("gap_made"), sem("gap_exped"), sem("choice_made")
        choice_cast = sem("choice_cast")
        x_set, chosen_made = sem("x_set"), [sem("chosen_made0"), sem("chosen_made1")]
        ctl_filled, ctl_act, ctl_dve = sem("ctl_filled"), sem("ctl_act"), sem("ctl_dve")
        part_made = sem("part_made")
        next_made, halt_h_stored, refine_stored, halt_stored = \
            sem("next_made"), sem("halt_h_stored"), sem("refine_stored"), sem("halt_stored")
        b2_split, v_set = sem("b2_split"), sem("v_set")
        act_step, dve_step = sem("act_step"), sem("dve_step")
        block = ctx.enter_context(nc.Block())

        @block.sync
        def _(sp):
            meanwhile(sp)

        @block.gpsimd
        def _(pool):
            nc.gpsimd.memset(choice[:, :, :, :], 0.0).then_inc(ready, 1)
            pool.wait_ge(ready, 1)
            nc.gpsimd.memset(route[32:33, :], 1.0).then_inc(ready, 1)
            with pool.Fori(0, NCH) as i:
                pool.wait_ge(gap_made, i + 1)
                nc.gpsimd.tensor_tensor(gap_exp[:, :], m["euler"][:, :], gap[:, :], ALU.pow).then_inc(gap_exped, 1)
                for it in range(ITERS):
                    for p in range(PAIRS):
                        banks.wait_freed(pool, f"hidden{it}{p}", i)
                        banks.wait_freed(pool, f"mask1{p}", i)
                        ins = nc.gpsimd.tensor_tensor(chosen[:, 1, p, :], hidden[:, p, :], mask[:, 1, p, :], ALU.mult)
                    ins.then_inc(chosen_made[1], 1)

        @block.tensor
        def _(pe):
            def mm(out, lhs, rhs, start=True, stop=True):
                return nc.tensor.matmul(out, lhs, rhs, start=start, stop=stop)

            def hide(i, it, layers, features):
                for n in range(0, len(layers), 2):
                    both = layers[n:n + 2]
                    for p in both if it else ():
                        banks.wait_free(pe, f"hidden{it}{p}", i)
                        mm(banks.bank(f"hidden{it}{p}")[:, :], w["w1"][:, 1, P * p:P * p + P], v[:, :], stop=False)
                    if it and n == 0:
                        pe.wait_ge(x_set, i * 3 + it + 1)
                    for p in both:
                        name = f"hidden{it}{p}"
                        if it == 0:
                            banks.wait_free(pe, name, i)
                        banks.fill(mm(banks.bank(name)[:, :], w["w1"][:, 0, P * p:P * p + P], features,
                                      start=(it == 0)), name)

            for k in range(2):
                pe.sem_inc(banks.freed[k], 1)
            pe.wait_ge(ready, 2)
            with pe.Fori(0, NCH) as i:
                xn = xnT[:, bass.ds(i * 4, 4), :]
                banks.wait_free(pe, "route", i)
                banks.fill(mm(banks.bank("route")[0:32, :], w["w_r1"][:, :], xn), "route")
                pe.wait_ge(x_set, i * 3 + 1)
                hide(i, 0, HIDDEN[:2], xi[:, :])
                banks.wait_free(pe, "logits", i)
                banks.wait_freed(pe, "route", i)
                for q in range(4):
                    ins = mm(banks.bank("logits")[:, 8 * q:8 * q + 8], route[:, S * q:S * q + S], w["w_r2"][:, :])
                banks.fill(ins, "logits")
                hide(i, 0, HIDDEN[2:], xi[:, :])
                banks.wait_free(pe, "choice", i)
                pe.wait_ge(choice_made, i + 1)
                for q in range(4):
                    ins = nc.tensor.transpose(banks.bank("choice")[:, S * q:S * q + S],
                                              choice[:, q].rearrange("p a e -> p (a e)"), identity[:, :])
                banks.fill(ins, "choice")
                pe.wait_ge(choice_cast, i + 1)
                for k in range(2):
                    for p in range(PAIRS):
                        banks.wait_free(pe, f"mask{k}{p}", i)
                        banks.fill(mm(banks.bank(f"mask{k}{p}")[:, :], m["pair_rows_bf"][:, k, p, :], choice_bf[:, :]),
                                   f"mask{k}{p}")
                for k in range(2):
                    banks.wait_free(pe, f"weight{k}", i)
                    banks.fill(mm(banks.bank(f"weight{k}")[:, :], m["weight_rows"][:, k, :], choice_t[:, :]), f"weight{k}")
                pe.wait_ge(b2_split, 1)
                for it in range(ITERS):
                    if it:
                        pe.wait_ge(v_set, i + 1)
                        hide(i, it, HIDDEN, xi[:, :])
                    for place, r in enumerate(BRANCHES):
                        n = it * len(BRANCHES) + place
                        pe.wait_ge(ctl_act, i * NB + n + 1)
                        pe.wait_ge(ctl_dve, i * NB + n + 1)
                        if r < 2:
                            pe.wait_ge(chosen_made[r], i * ITERS + it + 1)
                        else:
                            banks.wait_freed(pe, f"hidden{it}{PAIRS}", i)
                        for part_ in ORDER:
                            if part_ == ALPHA and it == 0:
                                continue
                            c = slice(P * part_, P * part_ + P)
                            bank = ctl[n % 2][part_]
                            if r < 2:
                                mm(bank[:, :], b2_bf[:, r, c], choice_bf[:, :], stop=False)
                                for p in range(PAIRS):
                                    ins = mm(bank[:, :], w["w2"][:, p, c], chosen[:, r, p, :], start=False,
                                             stop=(p == PAIRS - 1))
                            else:
                                ins = mm(bank[:, :], w["w_s2"][:, c], hidden[:, PAIRS, :])
                            ins.then_inc(ctl_filled, 1)
                    pe.wait_ge(next_made, i * ITERS + it + 1)
                    banks.wait_free(pe, f"halt_h{it}", i)
                    banks.fill(mm(banks.bank(f"halt_h{it}")[0:32, :], w["w_h1"][:, :], x_next[:, :]), f"halt_h{it}")
                    for k, name in enumerate(("refine_a", "refine_b")):
                        banks.wait_free(pe, f"{name}{it}", i)
                        banks.fill(mm(banks.bank(f"{name}{it}")[:, :], w["w_f1"][:, P * k:P * k + P], x_next[:, :]),
                                   f"{name}{it}")
                    banks.wait_free(pe, f"halt{it}", i)
                    pe.wait_ge(halt_h_stored, i * ITERS + it + 1)
                    banks.fill(mm(banks.bank(f"halt{it}")[:, :], w["w_h2"][:, :], halt_h[:, :]), f"halt{it}")
                    banks.wait_free(pe, f"refined{it}", i)
                    pe.wait_ge(refine_stored, (i * ITERS + it + 1) * 2)
                    for k in range(2):
                        ins = mm(banks.bank(f"refined{it}")[:, :], w["w_f2"][:, k, :], refine[:, k, :],
                                 start=(k == 0), stop=(k == 1))
                    banks.fill(ins, f"refined{it}")
                banks.wait_free(pe, "out", i)
                pe.wait_ge(x_set, i * 3 + 3)
                for q in range(4):
                    ins = nc.tensor.transpose(banks.bank("out")[:, S * q:S * q + S], xi[:, S * q:S * q + S],
                                              identity[:, :])
                banks.fill(ins, "out")

        @block.scalar
        def _(act):
            chain = Chain(act, act_step, 12)
            act.sem_inc(ctl_act, 2)

            def store_hidden(i, it, layers):
                for p in layers:
                    name = f"hidden{it}{p}"
                    banks.wait_filled(act, name, i)
                    banks.free(nc.scalar.activation(hidden[:, p, :], banks.bank(name)[:, :], ACT.Gelu,
                                                    bias=w["b1"][:, p:p + 1]), name)

            nc.scalar.activation(sw_exp[:, :], w["shared_weight"][:, :], ACT.Exp, scale=-1.0).then_inc(sw_exped, 1)
            with act.Fori(0, NCH) as i:
                chain.begin(i)
                banks.wait_filled(act, "route", i)
                banks.free(nc.scalar.activation(route[0:32, :], banks.bank("route")[0:32, :], ACT.Gelu,
                                                bias=w["b_r1"][:, 0:1]), "route")
                store_hidden(i, 0, HIDDEN)
                banks.wait_filled(act, "choice", i)
                nc.scalar.copy(choice_bf[:, :], banks.bank("choice")[:, :]).then_inc(choice_cast, 1)
                banks.free(nc.scalar.copy(choice_t[:, :], banks.bank("choice")[:, :]), "choice")
                for k in range(2):
                    for p in range(0, PAIRS, 2):
                        name = f"mask{k}{p}"
                        banks.wait_filled(act, name, i)
                        banks.free(nc.scalar.copy(mask[:, k, p, :], banks.bank(name)[:, :]), name)
                done = 0
                for it in range(ITERS):
                    if it:
                        store_hidden(i, it, HIDDEN)
                    for place, r in enumerate(BRANCHES):
                        n = it * len(BRANCHES) + place
                        s = n % 2
                        for part_ in ORDER:
                            if part_ == ALPHA and it == 0:
                                continue
                            done += 1
                            act.wait_ge(ctl_filled, i * PER_PASS + done)
                            bias = dict(bias=w["b_s2"][:, part_:part_ + 1]) if r == 2 else {}
                            if part_ == BETA:
                                chain(nc.scalar.activation(abs_b[:, :], ctl[s][part_][:, :], ACT.Abs, **bias))
                                chain(nc.scalar.activation(exp_b[:, :], abs_b[:, :], ACT.Sigmoid))
                                ins = nc.scalar.activation(gated[s][part_][:, :], exp_b[:, :], ACT.Ln)
                            else:
                                ins = nc.scalar.activation(gated[s][part_][:, :], ctl[s][part_][:, :], ACT.Sigmoid,
                                                           **bias)
                            ins.then_inc(part_made, 1)
                        act.wait_ge(part_made, i * PER_PASS + done)
                        act.sem_inc(ctl_act, 1)
                    banks.wait_filled(act, f"halt_h{it}", i)
                    nc.scalar.activation(halt_h[:, :], banks.bank(f"halt_h{it}")[0:32, :], ACT.Gelu,
                                         bias=w["b_h1"][:, 0:1]).then_inc(halt_h_stored, 1)
                    act.wait_ge(halt_h_stored, i * ITERS + it + 1)
                    act.sem_inc(banks.freed[banks.place[f"halt_h{it}"][0]], 1)
                    for k, name in enumerate(("refine_a", "refine_b")):
                        banks.wait_filled(act, f"{name}{it}", i)
                        nc.scalar.activation(refine[:, k, :], banks.bank(f"{name}{it}")[:, :], ACT.Gelu,
                                             bias=w["b_f1"][:, k:k + 1]).then_inc(refine_stored, 1)
                        act.wait_ge(refine_stored, (i * ITERS + it) * 2 + k + 1)
                        act.sem_inc(banks.freed[banks.place[f"{name}{it}"][0]], 1)
                    banks.wait_filled(act, f"halt{it}", i)
                    nc.scalar.activation(halt[:, :], banks.bank(f"halt{it}")[:, :], ACT.Sigmoid,
                                         bias=w["b_h2"][:, 0:1]).then_inc(halt_stored, 1)
                    act.wait_ge(halt_stored, i * ITERS + it + 1)
                    act.sem_inc(banks.freed[banks.place[f"halt{it}"][0]], 1)
                chain.end()

        @block.vector
        def _(dve):
            V = nc.vector
            pre = Chain(dve, sw_ready, 0)
            dve.sem_inc(ctl_dve, 2)
            dve.wait_ge(sw_exped, 1)
            pre(V.tensor_scalar(sw_exp[:, :], sw_exp[:, :], 1.0, None, ALU.add))
            pre(V.reciprocal(sw[:, :], sw_exp[:, :]))
            pre(V.tensor_scalar(sw_left[:, :], sw[:, :], -1.0, 1.0, ALU.mult, ALU.add))
            b2, b2_left = w["b2"][:, :, :], chosen[:, 0, 0:2, 0:384]
            pre(V.tensor_copy(b2_part[:, :, :], b2))
            pre(V.tensor_scalar(b2_bf[:, :, :], b2_part[:, :, :], w["split_rows"][:, 0:1], None, ALU.mult))
            for s in (1, 2):
                pre(V.tensor_tensor(b2_left, b2 if s == 1 else b2_left, b2_part[:, :, :], ALU.subtract))
                pre(V.tensor_copy(b2_part[:, :, :], b2_left))
                pre(V.scalar_tensor_tensor(b2_bf[:, :, :], b2_part[:, :, :], w["split_rows"][:, s:s + 1], b2_bf[:, :, :],
                                           ALU.mult, ALU.add))
            dve.sem_inc(b2_split, 1)
            dve.wait_ge(ready, 2)
            chain = Chain(dve, dve_step, 39)
            with dve.Fori(0, NCH) as i:
                chain.begin(i)
                V.tensor_copy(xi[:, :].rearrange("p (q s) -> p q s", q=4), xnT[:, bass.ds(i * 4, 4), :]) \
                    .then_inc(x_set, 1)
                banks.wait_filled(dve, "logits", i)
                banks.free(V.tensor_copy(logits[:, :, :], banks.bank("logits")[:, 0:32]
                                         .rearrange("p (q e) -> p q e", q=4)), "logits")
                banks.wait_freed(dve, "logits", i)
                V.memset(one_more[:, :], 0.0)
                for q in range(4):
                    ins = V.max(best[:, q, :], logits[:, q, :])
                chain(ins)
                V.tensor_tensor(gap[:, :], best[:, :, 1], best[:, :, 0], ALU.subtract).then_inc(gap_made, 1)
                for q in range(4):
                    ins = V.max_index(best_at[:, q, :], best[:, q, :], logits[:, q, :])
                chain(ins)
                chain(V.tensor_copy(at[:, :, :], best_at[:, :, 0:2]))
                for k in range(2):
                    for s in range(3):
                        ins = V.tensor_tensor(choice[:, :, k, E * s:E * s + E], m["iota8"][:, :, :],
                                              at[:, :, k:k + 1].broadcast_to([P, 4, E]), ALU.is_equal)
                chain(ins)
                dve.wait_ge(gap_exped, i + 1)
                chain(V.tensor_scalar(one_more[:, :], gap_exp[:, :], 1.0, None, ALU.add))
                chain(V.reciprocal(share[:, :, 0], one_more[:, :]))
                chain(V.tensor_tensor(share[:, :, 1], share[:, :, 0], gap_exp[:, :], ALU.mult))
                for k in range(2):
                    ins = V.tensor_tensor(choice[:, :, 2 + k, 0:E], choice[:, :, k, 0:E],
                                          share[:, :, k:k + 1].broadcast_to([P, 4, E]), ALU.mult)
                ins.then_inc(choice_made, 1)
                for k in range(2):
                    for p in range(1, PAIRS, 2):
                        name = f"mask{k}{p}"
                        banks.wait_filled(dve, name, i)
                        banks.free(V.tensor_copy(mask[:, k, p, :], banks.bank(name)[:, :]), name)
                done = 0
                for it in range(ITERS):
                    dve.wait_ge(x_set, i * 3 + it + 1)
                    V.tensor_scalar(err[:, :], xi[:, :], w["mu"][:, 0:1], None, ALU.subtract)
                    for p in range(PAIRS):
                        banks.wait_freed(dve, f"hidden{it}{p}", i)
                        banks.wait_freed(dve, f"mask0{p}", i)
                        ins = V.tensor_tensor(chosen[:, 0, p, :], hidden[:, p, :], mask[:, 0, p, :], ALU.mult)
                    ins.then_inc(chosen_made[0], 1)
                    if it == 0:
                        for k in range(2):
                            banks.wait_filled(dve, f"weight{k}", i)
                            banks.free(V.tensor_scalar(weight[:, k, :], banks.bank(f"weight{k}")[:, :], sw_left[:, 0:1],
                                                       None, ALU.mult), f"weight{k}")
                    for place, r in enumerate(BRANCHES):
                        n = it * len(BRANCHES) + place
                        s = n % 2
                        first_part = done
                        done += parts_of[it]
                        dve.wait_ge(part_made, i * PER_PASS + first_part + 1)
                        beta = ctl[s][BETA][:, :]
                        if r < 2:
                            chain(V.scalar_tensor_tensor(soft[:, :], beta, 0.0, gated[s][BETA][:, :],
                                                         ALU.max, ALU.subtract))
                        else:
                            chain(V.tensor_scalar(part[:, :], beta, w["b_s2"][:, BETA:BETA + 1], 0.0, ALU.add, ALU.max))
                            chain(V.tensor_tensor(soft[:, :], part[:, :], gated[s][BETA][:, :], ALU.subtract))
                        chain(V.scalar_tensor_tensor(push[:, :], soft[:, :], -1.0, err[:, :], ALU.mult, ALU.mult))
                        fresh = push
                        if it:
                            dve.wait_ge(part_made, i * PER_PASS + first_part + 2)
                            chain(V.tensor_tensor(keep[:, :], gated[s][ALPHA][:, :], v[:, :], ALU.mult))
                            chain(V.tensor_tensor(v_new[:, :], keep[:, :], push[:, :], ALU.add))
                            fresh = v_new
                        share_v = v_sum if r == 2 and it == 0 else part
                        if r == 2:
                            chain(V.tensor_scalar(share_v[:, :], fresh[:, :], sw[:, 0:1], None, ALU.mult))
                        else:
                            chain(V.tensor_tensor(share_v[:, :], fresh[:, :], weight[:, r, :], ALU.mult))
                            if it == 0:
                                V.tensor_tensor(v_sum[:, :], v_sum[:, :], share_v[:, :], ALU.add)
                        dve.wait_ge(part_made, i * PER_PASS + done)
                        if r == 2:
                            ins = V.tensor_tensor(move_sum[:, :], gated[s][GATE][:, :], share_v[:, :], ALU.mult)
                        else:
                            chain(V.tensor_tensor(move[:, :], gated[s][GATE][:, :], share_v[:, :], ALU.mult))
                            if place < len(BRANCHES) - 1:
                                chain(V.tensor_tensor(move_sum[:, :], move_sum[:, :], move[:, :], ALU.add))
                                ins = V.scalar_tensor_tensor(moved[:, :], move_sum[:, :], DT, xi[:, :], ALU.mult, ALU.add)
                            else:
                                V.scalar_tensor_tensor(x_next[:, :], move[:, :], DT, moved[:, :], ALU.mult, ALU.add) \
                                    .then_inc(next_made, 1)
                        if place < len(BRANCHES) - 1:
                            ins.then_inc(ctl_dve, 1)
                        else:
                            dve.sem_inc(ctl_dve, 1)
                        dve.wait_ge(ctl_dve, i * NB + n + 3)
                    if it < ITERS - 1:
                        V.tensor_copy(v[:, :], v_sum[:, :]).then_inc(v_set, 1)
                        dve.wait_ge(v_set, i + 1)
                    banks.wait_filled(dve, f"refined{it}", i)
                    dve.wait_ge(halt_stored, i * ITERS + it + 1)
                    banks.free(V.scalar_tensor_tensor(stepped[:, :], banks.bank(f"refined{it}")[:, :],
                                                      w["b_f2"][:, 0:1], halt[:, :], ALU.add, ALU.mult), f"refined{it}")
                    banks.wait_freed(dve, f"refined{it}", i)
                    V.scalar_tensor_tensor(xi[:, :], stepped[:, :], w["integration_weight"][:, 0:1], xi[:, :],
                                           ALU.mult, ALU.add).then_inc(x_set, 1)
                banks.wait_filled(dve, "out", i)
                xs = x[:, bass.ds(i * 4, 4), :]
                banks.free(V.tensor_tensor(xs, xs, banks.bank("out")[:, :].rearrange("p (q s) -> p q s", q=4),
                                           ALU.add), "out")
                chain.end()


def top1_experts(nc, m, w, tag, meanwhile):
    E, FT = 14, 2
    NT = E * FT
    RING = 4
    x, xnT, identity = m["x"], m["xnT"], m["identity"]
    layernorm(nc, m, tag + "_ln")
    with cleared_semaphores(nc) as new_semaphore, ExitStack() as ctx:
        def sb(name, shape, dt=F32):
            return ctx.enter_context(nc.sbuf_tensor(f"{tag}_{name}", shape, dt))

        def sem(name):
            return new_semaphore(f"{tag}_{name}")

        def ps(name):
            return ctx.enter_context(nc.psum_tensor(f"{tag}_{name}", [P, CH], F32))

        def ring(kind, names, n):
            return Banks(names, [ps(f"{kind}{k}") for k in range(n)],
                         [sem(f"{kind}_filled{k}") for k in range(n)], [sem(f"{kind}_freed{k}") for k in range(n)])

        xc = sb("xc", [P, CH])
        logits = sb("logits", [P, 4, E])
        best, best_at, at = sb("best", [P, 4, 8]), sb("best_at", [P, 4, 8], U32), sb("at", [P, 4])
        neg_best, exps, total, weight = sb("neg_best", [P, 4]), sb("exps", [P, E]), sb("total", [P, 4]), sb("weight", [P, 4])
        choice = sb("choice", [P, 4, P])
        choice_t, choice_bf = sb("choice_t", [P, CH]), sb("choice_bf", [P, CH], BF16)
        hidden = [sb(f"hidden{k}", [P, CH]) for k in range(RING)]
        chosen = [sb(f"chosen{k}", [P, CH]) for k in range(RING)]
        y_t = sb("y_t", [P, CH])
        EARLY = 2
        work = ring("work", ["logits"] + [f"hidden{n}" for n in range(EARLY)] + ["choice"] +
                    [f"hidden{n}" for n in range(EARLY, NT)] + ["out"], 4)
        masks = ring("mask", [f"mask{e}" for e in range(E)], 3)
        acc = ring("acc", ["acc"], 1)
        ready, xc_set, neg_made, total_made, choice_made = \
            sem("ready"), sem("xc_set"), sem("neg_made"), sem("total_made"), sem("choice_made")
        choice_cast, chosen_made, chosen_used = sem("choice_cast"), sem("chosen_made"), sem("chosen_used")
        dve_step, act_step = sem("dve_step"), sem("act_step")
        block = ctx.enter_context(nc.Block())

        @block.sync
        def _(sp):
            meanwhile(sp)

        @block.gpsimd
        def _(pool):
            nc.gpsimd.memset(choice[:, :, :], 0.0).then_inc(ready, 1)

        @block.tensor
        def _(pe):
            mm = nc.tensor.matmul
            for r in (work, masks, acc):
                for s in r.freed:
                    pe.sem_inc(s, 1)
            pe.sem_inc(chosen_used, RING)
            with pe.Fori(0, NCH) as i:
                pe.wait_ge(xc_set, i + 1)
                work.wait_free(pe, "logits", i)
                for q in range(4):
                    ins = mm(work.bank("logits")[:, E * q:E * q + E], xc[:, S * q:S * q + S], w["router_w"][:, :],
                             start=True, stop=True)
                work.fill(ins, "logits")

                def first(n):
                    work.wait_free(pe, f"hidden{n}", i)
                    work.fill(mm(work.bank(f"hidden{n}")[:, :], w["w1"][:, n, :], xc[:, :], start=True, stop=True),
                              f"hidden{n}")

                for n in range(EARLY):
                    first(n)
                work.wait_free(pe, "choice", i)
                pe.wait_ge(choice_made, i + 1)
                for q in range(4):
                    ins = nc.tensor.transpose(work.bank("choice")[:, S * q:S * q + S], choice[:, q, :], identity[:, :])
                work.fill(ins, "choice")

                def second(n):
                    pe.wait_ge(chosen_made, i * NT + n + 1 + RING)
                    mm(acc.bank("acc")[:, :], w["w2"][:, n, :], chosen[n % RING][:, :], start=False,
                       stop=(n == NT - 1)).then_inc(chosen_used, 1)

                LAG = 3
                for n in range(NT + LAG):
                    if n < NT:
                        e = n // FT
                        if n >= EARLY:
                            first(n)
                        if n % FT == 0:
                            masks.wait_free(pe, f"mask{e}", i)
                            pe.wait_ge(choice_cast, i + 1)
                            masks.fill(mm(masks.bank(f"mask{e}")[:, :], m["expert_rows_bf"][:, e, :], choice_bf[:, :],
                                          start=True, stop=True), f"mask{e}")
                        if n == 1:
                            acc.wait_free(pe, "acc", i)
                            work.wait_freed(pe, "choice", i)
                            mm(acc.bank("acc")[:, :], w["b2"][:, :], choice_t[:, :], start=True, stop=False)
                    if n >= LAG:
                        second(n - LAG)
                work.wait_free(pe, "out", i)
                acc.wait_freed(pe, "acc", i)
                for q in range(4):
                    ins = nc.tensor.transpose(work.bank("out")[:, S * q:S * q + S], y_t[:, S * q:S * q + S],
                                              identity[:, :])
                work.fill(ins, "out")

        @block.scalar
        def _(act):
            A = nc.scalar
            with act.Fori(0, NCH) as i:
                A.copy(xc[:, :].rearrange("p (q s) -> p q s", q=4), xnT[:, bass.ds(i * 4, 4), :]).then_inc(xc_set, 1)
                act.wait_ge(neg_made, i + 1)
                for q in range(4):
                    ins = A.activation(exps[:, :], logits[:, q, :], ACT.Exp, bias=neg_best[:, q:q + 1],
                                       accum_out=total[:, q:q + 1])
                    if q < 3:
                        ins.then_inc(act_step, 1)
                        act.wait_ge(act_step, i * 3 + q + 1)
                ins.then_inc(total_made, 1)
                work.wait_filled(act, "choice", i)
                A.copy(choice_bf[:, :], work.bank("choice")[:, :]).then_inc(choice_cast, 1)
                work.free(A.copy(choice_t[:, :], work.bank("choice")[:, :]), "choice")
                for n in range(NT):
                    act.wait_ge(chosen_made, i * NT + n + 1)
                    work.wait_filled(act, f"hidden{n}", i)
                    work.free(A.activation(hidden[n % RING][:, :], work.bank(f"hidden{n}")[:, :], ACT.Gelu,
                                           bias=w["b1"][:, n:n + 1]), f"hidden{n}")
                act.wait_ge(chosen_used, i * NT + NT + RING)
                acc.free(A.copy(y_t[:, :], acc.bank("acc")[:, :]), "acc")

        @block.vector
        def _(dve):
            V = nc.vector
            dve.sem_inc(chosen_made, RING)
            chain = Chain(dve, dve_step, 4)
            dve.wait_ge(ready, 1)
            with dve.Fori(0, NCH) as i:
                chain.begin(i)
                work.wait_filled(dve, "logits", i)
                work.free(V.tensor_copy(logits[:, :, :], work.bank("logits")[:, 0:4 * E]
                                        .rearrange("p (q e) -> p q e", q=4)), "logits")
                work.wait_freed(dve, "logits", i)
                V.memset(at[:, :], 0.0)
                for q in range(4):
                    ins = V.max(best[:, q, :], logits[:, q, :])
                chain(ins)
                V.tensor_scalar(neg_best[:, :], best[:, :, 0], -1.0, None, ALU.mult).then_inc(neg_made, 1)
                for q in range(4):
                    ins = V.max_index(best_at[:, q, :], best[:, q, :], logits[:, q, :])
                chain(ins)
                chain(V.tensor_copy(at[:, :], best_at[:, :, 0]))
                V.tensor_tensor(choice[:, :, 0:E], m["iota14"][:, :, :],
                                at[:, :].unsqueeze(2).broadcast_to([P, 4, E]), ALU.is_equal).then_inc(choice_made, 1)
                dve.wait_ge(total_made, i + 1)
                chain(V.reciprocal(weight[:, :], total[:, :]))
                for n in range(NT):
                    e = n // FT
                    if n % FT == 0:
                        masks.wait_filled(dve, f"mask{e}", i)
                    work.wait_freed(dve, f"hidden{n}", i)
                    dve.wait_ge(chosen_used, i * NT + n + 1)
                    V.tensor_tensor(chosen[n % RING][:, :], hidden[n % RING][:, :], masks.bank(f"mask{e}")[:, :],
                                    ALU.mult).then_inc(chosen_made, 1)
                    if n % FT == FT - 1:
                        dve.wait_ge(chosen_made, i * NT + n + 1 + RING)
                        dve.sem_inc(masks.freed[masks.place[f"mask{e}"][0]], 1)
                work.wait_filled(dve, "out", i)
                for q in range(4):
                    xb = x[:, i * 4 + q, :]
                    ins = V.scalar_tensor_tensor(xb, work.bank("out")[:, S * q:S * q + S], weight[:, q:q + 1], xb,
                                                 ALU.mult, ALU.add)
                work.free(ins, "out")
                chain.end()


def gated_lora(nc, m, w, tag, meanwhile):
    E, R = 8, 16
    x, xnT, identity = m["x"], m["xnT"], m["identity"]
    layernorm(nc, m, tag + "_ln")
    with cleared_semaphores(nc) as new_semaphore, ExitStack() as ctx:
        def sb(name, shape):
            return ctx.enter_context(nc.sbuf_tensor(f"{tag}_{name}", shape, F32))

        def ps(name, shape):
            return ctx.enter_context(nc.psum_tensor(f"{tag}_{name}_ps", shape, F32))

        neg_top, total, inv = sb("neg_top", [P, B]), sb("total", [P, B]), sb("inv", [P, B])
        below, exps, gate = sb("below", [P, B, E]), sb("exps", [P, B, E]), sb("gates", [P, B, E])
        low = [sb(f"low_rank{i}", [P, 4, E, R]) for i in range(NCH)]
        low_t = [sb(f"low_t{i}", [P, 4, S]) for i in range(NCH)]
        gate_ps, low_ps = ps("gate", [P, B, 4 * E]), [ps(f"low{i}", [P, 4, S]) for i in range(NCH)]
        flip_ps, out_ps = ps("flip", [P, 4, S]), [ps(f"out{k}", [P, 4, S]) for k in range(2)]
        gated, projected, below_made, exps_made, step = \
            [new_semaphore(f"{tag}_{n}") for n in ("gated", "projected", "below_made", "exps_made", "step")]
        low_made, flipped, flip_stored, out_made, added = \
            [new_semaphore(f"{tag}_{n}") for n in ("low_made", "flipped", "flip_stored", "out_made", "added")]
        block = ctx.enter_context(nc.Block())

        @block.sync
        def _(sp):
            meanwhile(sp)

        @block.tensor
        def _(pe):
            mm = nc.tensor.matmul
            for b in range(B):
                ins = mm(gate_ps[:, b, 0:E], xnT[:, b, :], w["gate"][:, :], start=True, stop=True)
            ins.then_inc(gated, 1)
            for i in range(NCH):
                for q in range(4):
                    ins = mm(low_ps[i][:, q, :], xnT[:, 4 * i + q, :], w["down"][:, :], start=True, stop=True)
                ins.then_inc(projected, 1)
            for i in range(NCH):
                pe.wait_ge(low_made, i + 1)
                if i:
                    pe.wait_ge(flip_stored, i)
                for q in range(4):
                    ins = nc.tensor.transpose(flip_ps[:, q, :], low[i][:, q].rearrange("p e r -> p (e r)"),
                                              identity[:, :])
                ins.then_inc(flipped, 1)
                if i >= 2:
                    pe.wait_ge(added, i - 1)
                pe.wait_ge(flip_stored, i + 1)
                for q in range(4):
                    o = out_ps[i % 2][:, q, :]
                    mm(o, xnT[:, 4 * i + q, :], w["weight"][:, :], start=True, stop=False)
                    ins = mm(o, low_t[i][:, q, :], w["up"][:, :], start=False, stop=True)
                ins.then_inc(out_made, 1)

        @block.scalar
        def _(act):
            act.wait_ge(below_made, 1)
            nc.scalar.activation(exps[:, :, :], below[:, :, :], ACT.Exp).then_inc(exps_made, 1)
            for i in range(NCH):
                act.wait_ge(flipped, i + 1)
                nc.scalar.copy(low_t[i][:, :, :], flip_ps[:, :, :]).then_inc(flip_stored, 1)

        @block.vector
        def _(dve):
            V = nc.vector
            chain = Chain(dve, step, 0)

            def add(i):
                dve.wait_ge(out_made, i + 1)
                xs = x[:, 4 * i:4 * i + 4, :]
                V.tensor_tensor(xs, xs, out_ps[i % 2][:, :, :], ALU.add).then_inc(added, 1)

            def each_gate(row):
                return row[:, :].unsqueeze(2).broadcast_to([P, B, E])

            dve.wait_ge(gated, 1)
            chain(V.tensor_reduce(neg_top[:, :], gate_ps[:, :, 0:E], AX.X, ALU.max, negate=True))
            V.tensor_tensor(below[:, :, :], gate_ps[:, :, 0:E], each_gate(neg_top), ALU.add).then_inc(below_made, 1)
            dve.wait_ge(exps_made, 1)
            chain(V.tensor_reduce(total[:, :], exps[:, :, :], AX.X, ALU.add))
            chain(V.reciprocal(inv[:, :], total[:, :]))
            chain(V.scalar_tensor_tensor(gate[:, :, :], exps[:, :, :], 1.0 / R, each_gate(inv), ALU.mult, ALU.mult))
            for i in range(NCH):
                dve.wait_ge(projected, i + 1)
                V.tensor_tensor(low[i].rearrange("p q e r -> p (q e) r"),
                                low_ps[i].rearrange("p q (e r) -> p (q e) r", r=R),
                                gate[:, 4 * i:4 * i + 4, :].rearrange("p q e -> p (q e)").unsqueeze(2)
                                .broadcast_to([P, 4 * E, R]), ALU.mult).then_inc(low_made, 1)
            for i in range(NCH):
                add(i)


class Stream:
    pass


def two_attentions(nc, m, w, tag, meanwhile):
    x, xnT, ctxT, identity = m["x"], m["xnT"], m["ctxT"], m["identity"]
    layernorm(nc, m, tag + "_ln")
    with cleared_semaphores(nc) as new_semaphore, ExitStack() as ctx:
        Q4 = [P, 4, S]
        names = ["res0"]
        for a in range(2):
            names += [f"{n}{a}" for n in ("q", "k", "v", "scores", "length", "flip", "pv", "xT")]
        names += ["hid", "fc"]
        BANKS = 4

        def stream(n):
            st = Stream()

            def sb(name, shape):
                return ctx.enter_context(nc.sbuf_tensor(f"{tag}_{name}{n}_sb", shape, F32))

            def sem(name):
                return new_semaphore(f"{tag}_{name}{n}")

            st.first = 4 * n
            st.xc, st.ctx_c = sb("xc", Q4), sb("ctx_c", Q4)
            st.res = [sb("res0", Q4), sb("res1", Q4), sb("res2", Q4)]
            st.qT, st.kT, st.v = sb("qT", Q4), sb("kT", Q4), sb("v", Q4)
            st.sT = sb("sT", Q4)
            st.masked, st.probs, st.probsT = sb("masked", Q4), sb("probs", Q4), sb("probsT", Q4)
            st.nonzero, st.length, st.length_all = sb("nonzero", [1, 4, S]), sb("length", [1, 4]), sb("length_all", [P, 4])
            st.neg_max, st.sums, st.inv = sb("neg_max", [P, 4]), sb("sums", [P, 4]), sb("inv", [P, 4])
            st.y, st.z = sb("y", Q4), sb("z", Q4)
            st.stats, st.mean_var = sb("stats", [P, 4, 6]), sb("mean_var", [P, 4, 2])
            st.var_eps, st.rstd = sb("var_eps", [P, 4]), sb("rstd", [P, 4])
            st.hid = sb("hid", Q4)
            st.banks = Banks(names, [ctx.enter_context(nc.psum_tensor(f"{tag}_bank{n}{k}", Q4, F32))
                                     for k in range(BANKS)],
                             [sem(f"bank{k}_filled") for k in range(BANKS)], [sem(f"bank{k}_freed") for k in range(BANKS)])
            st.inputs_set, st.length_made, st.neg_made = sem("inputs_set"), sem("length_made"), sem("neg_made")
            st.probs_made, st.eps_added, st.rstd_made = sem("probs_made"), sem("eps_added"), sem("rstd_made")
            st.stage_made, st.dve_step = sem("stage_made"), sem("dve_step")
            return st

        streams = [stream(n) for n in range(2)]
        PASSES = NCH // len(streams)
        block = ctx.enter_context(nc.Block())

        @block.sync
        def _(sp):
            meanwhile(sp)

        @block.gpsimd
        def _(pool):
            with pool.Fori(0, PASSES) as i:
                for n in range(3):
                    for st in streams:
                        pool.wait_ge(st.eps_added, i * 3 + n + 1)
                        nc.gpsimd.tensor_tensor(st.rstd[:, :], st.var_eps[:, :], m["minus_half"][:, 0:4], ALU.pow) \
                            .then_inc(st.rstd_made, 1)

        @block.tensor
        def _(pe):
            def each(st, name, i, products):
                st.banks.wait_free(pe, name, i)
                for out, lhs, rhs in products:
                    ins = nc.tensor.matmul(out, lhs, rhs, start=True, stop=True)
                st.banks.fill(ins, name)

            def flip(st, name, i, source):
                st.banks.wait_free(pe, name, i)
                for q in range(4):
                    ins = nc.tensor.transpose(st.banks.bank(name)[:, q, :], source[:, q, :], identity[:, :])
                st.banks.fill(ins, name)

            def project(st, i, a):
                q_in, kv_in = (st.sT, st.ctx_c) if a else (st.xc, st.xc)
                if a:
                    st.banks.wait_freed(pe, "xT0", i)
                each(st, f"q{a}", i, [(st.banks.bank(f"q{a}")[:, :, :], w[f"Wq{a + 1}"][:, :], q_in[:, :, :])])
                each(st, f"k{a}", i, [(st.banks.bank(f"k{a}")[:, :, :], w[f"Wk{a + 1}"][:, :], kv_in[:, :, :])])
                each(st, f"v{a}", i, [(st.banks.bank(f"v{a}")[:, q, :], kv_in[:, q, :], w[f"Wv{a + 1}"][:, :])
                                      for q in range(4)])

            for st in streams:
                for s in st.banks.freed:
                    pe.sem_inc(s, 1)
            with pe.Fori(0, PASSES) as i:
                for st in streams:
                    pe.wait_ge(st.inputs_set, i + 1)
                    flip(st, "res0", i, st.xc)
                for a in range(2):
                    for st in streams:
                        project(st, i, a)
                    for st in streams:
                        st.banks.wait_freed(pe, f"q{a}", i)
                        st.banks.wait_freed(pe, f"k{a}", i)
                        each(st, f"scores{a}", i, [(st.banks.bank(f"scores{a}")[:, q, :], st.qT[:, q, :], st.kT[:, q, :])
                                                   for q in range(4)])
                    for st in streams:
                        pe.wait_ge(st.length_made, i * 2 + a + 1)
                        each(st, f"length{a}", i, [(st.banks.bank(f"length{a}")[:, 0, 0:4], m["ones_sq"][0:1, :],
                                                    st.length[:, :])])
                    for st in streams:
                        pe.wait_ge(st.probs_made, i * 2 + a + 1)
                        flip(st, f"flip{a}", i, st.probs)
                    for st in streams:
                        st.banks.wait_freed(pe, f"flip{a}", i)
                        st.banks.wait_freed(pe, f"v{a}", i)
                        each(st, f"pv{a}", i, [(st.banks.bank(f"pv{a}")[:, q, :], st.probsT[:, q, :], st.v[:, q, :])
                                               for q in range(4)])
                    for st in streams:
                        pe.wait_ge(st.stage_made, i * 3 + a + 1)
                        flip(st, f"xT{a}", i, st.res[a + 1])
                for st in streams:
                    st.banks.wait_freed(pe, "xT1", i)
                    each(st, "hid", i, [(st.banks.bank("hid")[:, :, :], w["fc1_w"][:, :], st.sT[:, :, :])])
                for st in streams:
                    st.banks.wait_freed(pe, "hid", i)
                    each(st, "fc", i, [(st.banks.bank("fc")[:, q, :], st.hid[:, q, :], w["fc2_w"][:, :]) for q in range(4)])

        @block.scalar
        def _(act):
            A = nc.scalar

            def store(st, name, i, out):
                st.banks.wait_filled(act, name, i)
                st.banks.free(A.copy(out[:, :, :], st.banks.bank(name)[:, :, :]), name)

            with act.Fori(0, PASSES) as i:
                for st in streams:
                    A.copy(st.xc[:, :, :], xnT[:, bass.ds(i * 8 + st.first, 4), :])
                    A.copy(st.ctx_c[:, :, :], ctxT[:, bass.ds(i * 8 + st.first, 4), :]).then_inc(st.inputs_set, 1)
                for st in streams:
                    store(st, "res0", i, st.res[0])
                for a in range(2):
                    for st in streams:
                        store(st, f"q{a}", i, st.qT)
                        store(st, f"k{a}", i, st.kT)
                    for st in streams:
                        act.wait_ge(st.neg_made, i * 2 + a + 1)
                        for q in range(4):
                            ins = A.activation(st.probs[:, q, :], st.masked[:, q, :], ACT.Exp, bias=st.neg_max[:, q:q + 1],
                                               scale=SCORE_SCALE, accum_out=st.sums[:, q:q + 1])
                        ins.then_inc(st.probs_made, 1)
                    for st in streams:
                        store(st, f"flip{a}", i, st.probsT)
                    for st in streams:
                        store(st, f"xT{a}", i, st.sT)
                for st in streams:
                    st.banks.wait_filled(act, "hid", i)
                    st.banks.free(A.activation(st.hid[:, :, :], st.banks.bank("hid")[:, :, :], ACT.Relu,
                                               bias=w["fc1_b"][:, 0:1]), "hid")

        @block.vector
        def _(dve):
            V = nc.vector
            for st in streams:
                st.chain = Chain(dve, st.dve_step, 23)

            def wide(row):
                return row[:, :].unsqueeze(1).broadcast_to(Q4)

            def norm(st, i, n, out):
                z, y = st.z, st.y
                for q in range(4):
                    ins = V.bn_stats(st.stats[:, q, :], z[:, q, :])
                st.chain(ins)
                V.memset(st.var_eps[:, :], LN_EPS)
                for q in range(4):
                    ins = V.bn_aggr(st.mean_var[:, q, :], st.stats[:, q, :])
                st.chain(ins)
                V.tensor_tensor(st.var_eps[:, :], st.var_eps[:, :], st.mean_var[:, :, 1], ALU.add) \
                    .then_inc(st.eps_added, 1)
                yield
                dve.wait_ge(st.rstd_made, i * 3 + n + 1)
                for q in range(4):
                    ins = V.tensor_scalar(y[:, q, :], z[:, q, :], st.mean_var[:, q, 0:1], st.rstd[:, q:q + 1],
                                          ALU.subtract, ALU.mult)
                st.chain(ins)
                st.chain(V.tensor_tensor(z[:, :, :], y[:, :, :], wide(w[f"ln{n + 1}_g"]), ALU.mult))
                V.tensor_tensor(out[:, :, :], z[:, :, :], wide(w[f"ln{n + 1}_b"]), ALU.add).then_inc(st.stage_made, 1)
                dve.wait_ge(st.stage_made, i * 3 + n + 1)

            def steps(st, i):
                chain, banks, y, z, neg = st.chain, st.banks, st.y, st.z, st.y
                chain.begin(i)
                banks.wait_freed(dve, "res0", i)
                for a in range(2):
                    name = f"v{a}"
                    banks.wait_filled(dve, name, i)
                    banks.free(V.tensor_copy(st.v[:, :, :], banks.bank(name)[:, :, :]), name)
                    yield
                    name = f"scores{a}"
                    banks.wait_filled(dve, name, i)
                    chain(V.tensor_scalar(st.nonzero[:, :, :], banks.bank(name)[0:1, :, :], 0.0, None, ALU.not_equal))
                    V.tensor_reduce(st.length[:, :], st.nonzero[:, :, :], AX.X, ALU.add).then_inc(st.length_made, 1)
                    yield
                    banks.wait_filled(dve, f"length{a}", i)
                    banks.free(V.tensor_copy(st.length_all[:, :], banks.bank(f"length{a}")[:, 0, 0:4]), f"length{a}")
                    banks.wait_freed(dve, f"length{a}", i)
                    for q in range(4):
                        ins = V.tensor_scalar(neg[:, q, :], m["iota128"][:, :], st.length_all[:, q:q + 1], NEG,
                                              ALU.is_ge, ALU.mult)
                    chain(ins)
                    if a == 0:
                        chain(V.tensor_tensor(neg[:, :, :], neg[:, :, :], wide(m["future_f32"]), ALU.min))
                    banks.free(V.tensor_tensor(st.masked[:, :, :], neg[:, :, :], banks.bank(name)[:, :, :], ALU.add), name)
                    banks.wait_freed(dve, name, i)
                    chain(V.tensor_reduce(st.inv[:, :], st.masked[:, :, :], AX.X, ALU.max, negate=True))
                    V.tensor_scalar(st.neg_max[:, :], st.inv[:, :], SCORE_SCALE, None, ALU.mult).then_inc(st.neg_made, 1)
                    yield
                    dve.wait_ge(st.probs_made, i * 2 + a + 1)
                    dve.wait_ge(st.neg_made, i * 2 + a + 1)
                    chain(V.reciprocal(st.inv[:, :], st.sums[:, :]))
                    banks.wait_filled(dve, f"pv{a}", i)
                    for q in range(4):
                        ins = V.scalar_tensor_tensor(z[:, q, :], banks.bank(f"pv{a}")[:, q, :], st.inv[:, q:q + 1],
                                                     st.res[a][:, q, :], ALU.mult, ALU.add)
                    banks.free(ins, f"pv{a}")
                    banks.wait_freed(dve, f"pv{a}", i)
                    yield from norm(st, i, a, st.res[a + 1])
                    yield
                banks.wait_filled(dve, "fc", i)
                banks.free(V.tensor_tensor(y[:, :, :], banks.bank("fc")[:, :, :], st.res[2][:, :, :], ALU.add), "fc")
                banks.wait_freed(dve, "fc", i)
                chain(V.tensor_tensor(z[:, :, :], y[:, :, :], wide(w["fc2_b"]), ALU.add))
                yield from norm(st, i, 2, y)
                xs = x[:, bass.ds(i * 8 + st.first, 4), :]
                chain(V.tensor_tensor(xs, xs, y[:, :, :], ALU.add))
                chain.end()

            with dve.Fori(0, PASSES) as i:
                turns = [steps(st, i) for st in streams]
                while turns:
                    turns = [t for t in turns if next(t, "ended") != "ended"]


def product_keys(nc, m, w, tag, meanwhile):
    H, K, DK = 8, 32, 128
    E = K * K
    ET = E // P
    x, xnT, identity = m["x"], m["xnT"], m["identity"]
    layernorm(nc, m, tag + "_ln", rms_gain=w["norm_w"])
    with cleared_semaphores(nc) as new_semaphore, ExitStack() as ctx:
        def sb(name, shape, dt=F32):
            return ctx.enter_context(nc.sbuf_tensor(f"{tag}_{name}_sb", shape, dt))

        def sem(name):
            return new_semaphore(f"{tag}_{name}")

        def ps(name, shape):
            return ctx.enter_context(nc.psum_tensor(f"{tag}_{name}", shape, F32))

        RING = 4
        fold = sb("fold", [P, H, 2, K])
        xb = sb("xb", [P, S])
        sim = [sb(f"sim{r}", [P, H, 2, K]) for r in range(2)]
        top = sb("top", [P, H, 2, 8])
        pairs = sb("pairs", [P, H, 8, 8])
        best = sb("best", [P, H, 8])
        least = [sb(f"least{r}", [P, H]) for r in range(2)]
        sums = [sb(f"sums{k}", [P, K, K]) for k in range(RING)]
        kept = [sb(f"kept{k}", [P, E]) for k in range(RING)]
        hid, given = sb("hid", [P, ET, S]), sb("given", [P, ET, S])
        sim_ps, hid_ps, given_ps, out_ps = ps("sim_ps", [P, 512]), ps("hid_ps", [P, ET, S]), ps("given_ps", [P, ET, S]), \
            ps("out_ps", [P, 512])
        fold_made, fold_stored, xb_set, scored, sim_stored, sums_made, kept_made, kept_flipped = [
            sem(n) for n in ("fold_made", "fold_stored", "xb_set", "scored", "sim_stored", "sums_made", "kept_made",
                             "kept_flipped")]
        hid_made, hid_stored, given_made, out_made, added, least_made = [
            sem(n) for n in ("hid_made", "hid_stored", "given_made", "out_made", "added", "least_made")]
        dve_step = sem("dve_step")
        block = ctx.enter_context(nc.Block())

        @block.sync
        def _(sp):
            meanwhile(sp)

        @block.tensor
        def _(pe):
            mm = nc.tensor.matmul
            for h in range(H):
                for j in range(2):
                    ins = mm(sim_ps[:, (2 * h + j) * K:(2 * h + j) * K + K], w["w_q"][:, 2 * h + j, :],
                             w["keys"][:, 2 * h + j, :], start=True, stop=True)
            ins.then_inc(fold_made, 1)
            pe.wait_ge(fold_stored, 1)
            pe.sem_inc(kept_flipped, RING)
            pe.sem_inc(added, 1)

            def score(b):
                pe.wait_ge(xb_set, b + 1)
                pe.wait_ge(sim_stored, b)
                mm(sim_ps[:, :], xb[:, :], fold[:, :, :, :], start=True, stop=True).then_inc(scored, 1)

            def hide(b):
                for e in range(ET):
                    ins = mm(hid_ps[:, e, :], w["down"][:, e, :], xnT[:, b, :], start=True, stop=True)
                ins.then_inc(hid_made, 1)

            def flip(b, h):
                pe.wait_ge(kept_made, b * H + h + 1 + RING)
                for e in range(ET):
                    ins = mm(given_ps[:, e, :], kept[h % RING][:, P * e:P * e + P], identity[:, :],
                             start=(h == 0 and e % 4 == 0), stop=(h == H - 1), skip_group_check=True)
                ins.then_inc(kept_flipped, 1)

            def batch(b, last=False):
                for h in range(H):
                    flip(b, h)
                    if h == 0 and not last:
                        score(b + 1)
                if not last:
                    pe.wait_ge(hid_stored, b + 1)
                    hide(b + 1)
                pe.wait_ge(given_made, b + 1)
                pe.wait_ge(added, b + 1)
                for e in range(ET):
                    ins = mm(out_ps[:, 0:D], given[:, e, :], w["up"][:, e, :], start=(e == 0), stop=(e == ET - 1))
                ins.then_inc(out_made, 1)

            pe.wait_ge(xb_set, 1)
            mm(sim_ps[:, :], xb[:, :], fold[:, :, :, :], start=True, stop=True).then_inc(scored, 1)
            hide(0)
            with pe.Fori(0, B - 1) as b:
                batch(b)
            batch(B - 1, last=True)

        @block.scalar
        def _(act):
            A = nc.scalar

            def gelu(b, first=False):
                act.wait_ge(hid_made, b + 1)
                if not first:
                    act.wait_ge(given_made, b)
                for k in range(2):
                    ins = A.activation(hid[:, 4 * k:4 * k + 4, :], hid_ps[:, 4 * k:4 * k + 4, :], ACT.Gelu)
                ins.then_inc(hid_stored, 1)

            A.copy(xb[:, :], xnT[:, 0, :]).then_inc(xb_set, 1)
            act.wait_ge(fold_made, 1)
            A.copy(fold[:, :, :, :].rearrange("p h j k -> p (h j k)"), sim_ps[:, :]).then_inc(fold_stored, 1)

            def store_scores(b, r):
                act.wait_ge(scored, b + 1)
                A.copy(sim[r][:, :, :, :].rearrange("p h j k -> p (h j k)"), sim_ps[:, :]).then_inc(sim_stored, 1)

            def prepare(b, r):
                act.wait_ge(scored, b)
                A.copy(xb[:, :], xnT[:, b, :]).then_inc(xb_set, 1)
                store_scores(b, r)
                gelu(b)

            store_scores(0, 0)
            gelu(0, first=True)
            with act.Fori(0, B // 2 - 1) as i:
                for r in (1, 0):
                    prepare(i * 2 + (1 if r else 2), r)
            prepare(B - 1, 1)

        @block.gpsimd
        def _(pool):
            pool.sem_inc(sums_made, RING)
            with pool.Fori(0, B // 2) as i:
                for r in range(2):
                    b = i * 2 + r
                    for h in range(H):
                        if h == 0:
                            pool.wait_ge(sim_stored, b + 1)
                        pool.wait_ge(kept_made, b * H + h + 1)
                        nc.gpsimd.tensor_tensor(sums[h % RING][:, :, :],
                                                sim[r][:, h, 0, :].unsqueeze(2).broadcast_to([P, K, K]),
                                                sim[r][:, h, 1, :].unsqueeze(1).broadcast_to([P, K, K]), ALU.add) \
                            .then_inc(sums_made, 1)

        @block.vector
        def _(dve):
            V = nc.vector
            chain = Chain(dve, dve_step, 4)
            LEAD = 3
            dve.sem_inc(kept_made, RING)

            def await_scores(b, r):
                dve.wait_ge(sim_stored, b + 1)
                V.memset(least[r][:, :], 0.0)

            def halves_best(r, heads):
                for h in heads:
                    for j in range(2):
                        ins = V.max(top[:, h, j, :], sim[r][:, h, j, :])
                return ins

            def pair_sums():
                return V.tensor_tensor(pairs[:, :, :, :], top[:, :, 0, :].unsqueeze(3).broadcast_to([P, H, 8, 8]),
                                       top[:, :, 1, :].unsqueeze(2).broadcast_to([P, H, 8, 8]), ALU.add)

            def pairs_best(r):
                V.memset(least[r][:, :], 0.0)
                for h in range(H):
                    ins = V.max(best[:, h, :], pairs[:, h, :, :])
                return ins

            def threshold(r):
                return V.tensor_scalar(least[r][:, :], best[:, :, 7], 0.0, None, ALU.max)

            def keep(b, r, h):
                k = h % RING
                dve.wait_ge(sums_made, b * H + h + 1 + RING)
                dve.wait_ge(kept_flipped, b * H + h + 1)
                flat = sums[k][:, :, :].rearrange("p a c -> p (a c)")
                V.scalar_tensor_tensor(kept[k][:, :], flat, least[r][:, h:h + 1], flat, ALU.is_ge, ALU.mult) \
                    .then_inc(kept_made, 1)

            def give(b):
                dve.wait_ge(hid_stored, b + 1)
                dve.wait_ge(kept_flipped, b * H + H + RING)
                for k in range(2):
                    s = slice(4 * k, 4 * k + 4)
                    ins = V.tensor_tensor(given[:, s, :], hid[:, s, :], given_ps[:, s, :], ALU.mult)
                ins.then_inc(given_made, 1)

            def add(b):
                dve.wait_ge(out_made, b + 1)
                V.tensor_tensor(x[:, b, :], x[:, b, :], out_ps[:, 0:D], ALU.add).then_inc(added, 1)

            def batch(b, r):
                await_scores(b + 1, 1 - r)
                ins = halves_best(1 - r, range(H))
                ins.then_inc(dve_step, 1)
                keep(b, r, 3)
                dve.wait_ge(dve_step, (b + 1) * 4 + 1)
                pair_sums().then_inc(dve_step, 1)
                keep(b, r, 4)
                dve.wait_ge(dve_step, (b + 1) * 4 + 2)
                pairs_best(1 - r).then_inc(dve_step, 1)
                keep(b, r, 5)
                dve.wait_ge(dve_step, (b + 1) * 4 + 3)
                threshold(1 - r).then_inc(dve_step, 1)
                for h in range(6, H):
                    keep(b, r, h)
                give(b)
                dve.wait_ge(dve_step, (b + 1) * 4 + 4)
                for h in range(LEAD):
                    keep(b + 1, 1 - r, h)
                add(b)

            await_scores(0, 0)
            chain.begin(0)
            chain(halves_best(0, range(H)))
            chain(pair_sums())
            chain(pairs_best(0))
            chain(threshold(0))
            chain.end()
            for h in range(LEAD):
                keep(0, 0, h)
            with dve.Fori(0, B // 2 - 1) as i:
                for r in range(2):
                    batch(i * 2 + r, r)
            batch(B - 2, 0)
            for h in range(LEAD, H):
                keep(B - 1, 1, h)
            give(B - 1)
            add(B - 1)


def bf16(constant):
    import numpy as np
    bits = np.ascontiguousarray(constant, np.float32).view(np.uint32) >> 16
    return np.ascontiguousarray(bits.astype(np.uint16)).view(np.float32)


def _layout(a):
    import numpy as np
    f = np.float32
    out = {}
    p = np.arange(P)
    out["identity"] = np.eye(P, dtype=f)
    out["ident_bf"] = bf16(np.eye(P))
    neg = np.where(p[None, :] > p[:, None], NEG, 0.0)
    out["future_bf"] = bf16(np.broadcast_to(neg[:, None], (P, 4, P)))
    out["past_bf"] = bf16(np.broadcast_to(neg.T[:, None], (P, 4, P)))
    out["minus_half"] = np.full((P, B), -0.5, f)
    out["euler"] = np.full((P, 4), np.e, f)
    out["spread"] = (p[:, None] == 16 * (p[None, :] // 16) + ROW_MAX).astype(f)
    out["row_head"] = (p[:, None] // 16 == np.arange(HT)[None]).astype(f)
    means = np.zeros((P, 3, 3), f)
    means[:, 0, 0], means[:, 1, 1], means[:, 2, 2] = 1.0 / (S * S), -1.0 / S, 1.0
    out["feature_row"] = means
    out["x"] = a["x"].transpose(1, 0, 2)
    out["ctxT"] = a["ctx_1024"].transpose(2, 0, 1)
    out["mask_bytes"] = np.broadcast_to(a["mask_BxS2_bk0"].view(np.uint32)[None], (P, B, S // 4))

    def heads(w):
        z = np.zeros(w.shape[:-1] + (NH, 16), f)
        z[..., :HD] = w.reshape(w.shape[:-1] + (NH, HD))
        return z.reshape(w.shape[:-1] + (T, P))

    for tag, wq, wk, wv, wo, bq, bk, bv, bo in (
        ("l0", a["L0_xattn_wq"], a["L0_xattn_wk"], a["L0_xattn_wv"], a["L0_xattn_wo"],
         a["L0_xattn_bq"], a["L0_xattn_bk"], a["L0_xattn_bv"], a["L0_xattn_bo"]),
        ("l1", a["L1_xattn_Wq"].T, a["L1_xattn_Wk"].T, a["L1_xattn_Wv"].T, a["L1_xattn_Wo"].T,
         a["L1_xattn_bq"], a["L1_xattn_bk"], a["L1_xattn_bv"], a["L1_xattn_bo"]),
        ("l3", a["L3_xattn_Wq"].T, a["L3_xattn_Wk"].T, a["L3_xattn_Wv"].T, a["L3_xattn_Wo"].T,
         np.zeros(P, f), np.zeros(P, f), np.zeros(P, f), a["L3_xattn_bo"]),
    ):
        out[tag + "_wq"] = heads(wq)
        out[tag + "_wk"] = heads(wk)
        out[tag + "_wv"] = heads(wv)
        out[tag + "_wo"] = heads(wo.T).transpose(2, 1, 0)
        out[tag + "_wo"][ROW_MAX, 0, :] = bo
        q, k, v = heads(bq), heads(bk), heads(bv)
        for t in range(T):
            k[t, p % 16 == ROW_MAX + t] = 1
        v[:, p % 16 == ROW_MAX] = 1
        if tag == "l0":
            q[:, p % 16 == ROW_MASK] = 1
            k[:, p % 16 == ROW_MASK] = 1
        out[tag + "_bq"] = q.T
        out[tag + "_bk"] = k.T
        out[tag + "_bv"] = np.broadcast_to(v[None], (P, T, P))
    full = MASKED / SCORE_SCALE
    of_max, of_mask = (p % 16 >= ROW_MAX) & (p % 16 < ROW_MASK), p % 16 == ROW_MASK
    out["l0_mask_mult"] = np.where(of_max, 0, np.where(of_mask, full, 1))[:, None].astype(f)
    out["l0_mask_add"] = np.where(of_max, 1, np.where(of_mask, -full, 0))[:, None].astype(f)
    out["l1_w1"] = a["L1_xattn_w1"].T
    out["l1_b1"] = a["L1_xattn_b1"][:, None]
    out["l1_w2"] = np.concatenate([a["L1_xattn_w2"].T, np.zeros((64, 64), f)], axis=1)
    out["l1_b2"] = a["L1_xattn_b2"][:, None]
    out["l1_w3"] = np.broadcast_to(a["L1_xattn_w3"].T, (64, P))
    out["l1_b3"] = np.broadcast_to(a["L1_xattn_b3"][None], (P, 1))
    _layout_ffn(a, out)
    return pack(out)


GROUPS = ("l0", "l0f", "l1", "l1f", "l2", "l2f", "l3", "l3f")
ALONE = ("x", "ctxT")


def group_of(name):
    tag = name.split("_")[0]
    return tag if tag in GROUPS else "common"


def pack(arrays):
    import numpy as np
    packed, where, width = {}, {}, {}
    for name, v in arrays.items():
        if v.dtype != np.float32 or name in ALONE:
            packed[name] = np.ascontiguousarray(v)
            continue
        g = group_of(name)
        flat = np.zeros((P, v[0].size), np.float32)
        flat[:v.shape[0]] = v.reshape(v.shape[0], -1)
        where[name] = (g, width.get(g, 0), v.shape)
        width[g] = width.get(g, 0) + flat.shape[1]
        packed.setdefault(g, []).append(flat)
    return {n: np.concatenate(v, axis=1) if isinstance(v, list) else v for n, v in packed.items()}, where


def _layout_ffn(a, out):
    import numpy as np
    f = np.float32
    p = np.arange(P)
    col = lambda v: v.reshape(-1, P).T if v.size >= P else v[:, None]
    E = 8
    g = lambda n: a["L0_ffn_" + n]
    out["iota8"] = np.broadcast_to(np.arange(E, dtype=f), (P, 4, E))
    out["ones_sq"] = np.ones((P, P), f)
    rows = np.arange(4)[:, None] * 2 + p[None, :] // 64
    row_of = 32 * np.arange(2)[:, None, None] + rows[None]
    out["pair_rows_bf"] = bf16(row_of[None] == p[:, None, None, None])
    out["weight_rows"] = np.broadcast_to((p[:, None] // 32 == 2 + np.arange(2)[None])[:, :, None], (P, 2, P)).astype(f)
    out["l0f_w_r1"] = g("w_r1")
    out["l0f_b_r1"] = g("b_r1")[:, None]
    out["l0f_w_r2"] = np.concatenate([g("w_r2"), g("b_r2")[None]], 0)
    w1 = np.concatenate([g("expert_w1").transpose(1, 0, 2).reshape(256, 512), g("w_s1"), np.zeros((256, 64), f)], 1)
    out["l0f_w1"] = w1.reshape(2, P, 640).transpose(1, 0, 2)
    b1 = np.zeros((P, 5), f)
    b1[:, :4] = g("expert_b1").reshape(4, P).T
    b1[:64, 4] = g("b_s1")
    out["l0f_b1"] = b1
    out["l0f_w2"] = g("expert_w2").reshape(4, P, 384).transpose(1, 0, 2)
    b2 = np.zeros((P, 2, 384), f)
    for k in range(2):
        for s in range(3):
            b2[32 * k + E * s:32 * k + E * s + E, k] = g("expert_b2")
    out["l0f_b2"] = b2
    out["l0f_split_rows"] = ((p[:, None] % 32) // E == np.arange(3)[None]).astype(f)
    out["l0f_w_s2"] = np.concatenate([g("w_s2"), np.zeros((64, 384), f)])
    out["l0f_b_s2"] = g("b_s2").reshape(3, P).T
    out["l0f_shared_weight"] = np.broadcast_to(g("shared_weight").reshape(1, 1), (P, 1))
    out["l0f_w_h1"] = g("w_h1")
    out["l0f_b_h1"] = g("b_h1")[:, None]
    out["l0f_w_h2"] = np.broadcast_to(g("w_h2"), (32, P))
    out["l0f_b_h2"] = np.broadcast_to(g("b_h2")[None], (P, 1))
    out["l0f_w_f1"] = g("w_f1")
    out["l0f_b_f1"] = g("b_f1").reshape(2, P).T
    out["l0f_w_f2"] = g("w_f2").reshape(2, P, P).transpose(1, 0, 2)
    out["l0f_b_f2"] = g("b_f2")[:, None]
    out["l0f_integration_weight"] = g("integration_weight")[:, None]
    out["l0f_mu"] = g("mu")[:, None]
    out["iota14"] = np.broadcast_to(np.arange(14, dtype=f), (P, 4, 14))
    out["expert_rows_bf"] = bf16(np.broadcast_to(np.eye(P)[:, :14, None], (P, 14, P)))
    out["l1f_router_w"] = a["L1_ffn_router_w"]
    out["l1f_w1"] = a["L1_ffn_w1"].transpose(1, 0, 2).reshape(P, 28, P)
    out["l1f_b1"] = a["L1_ffn_b1"].reshape(28, P).T
    out["l1f_w2"] = a["L1_ffn_w2"].reshape(28, P, P).transpose(1, 0, 2)
    out["l1f_b2"] = np.concatenate([a["L1_ffn_b2"], np.zeros((P - 14, P), f)])
    out["l3f_weight"] = a["L3_ffn_weight"].T
    out["l3f_gate"] = a["L3_ffn_gate_w"].T
    out["l3f_down"] = a["L3_ffn_lora_U"].reshape(P, P).T
    out["l3f_up"] = a["L3_ffn_lora_V"].transpose(0, 2, 1).reshape(P, P)
    out["iota128"] = np.broadcast_to(np.arange(P, dtype=f), (P, P))
    out["future_f32"] = np.where(p[None, :] > p[:, None], NEG, 0.0).astype(f)
    for n in ("Wq1", "Wk1", "Wv1", "Wq2", "Wk2", "Wv2", "fc1_w", "fc2_w"):
        out["l2_" + n] = a["L2_xattn_" + n]
    out["l2_fc1_b"] = a["L2_xattn_fc1_b"][:, None]
    for n in ("fc2_b", "ln1_g", "ln1_b", "ln2_g", "ln2_b", "ln3_g", "ln3_b"):
        out["l2_" + n] = np.broadcast_to(a["L2_xattn_" + n], (P, P))
    out["l2f_norm_w"] = a["L2_ffn_norm_w"][:, None]
    out["l2f_w_q"] = a["L2_ffn_w_q"].reshape(16, P, P).transpose(1, 0, 2)
    out["l2f_keys"] = a["L2_ffn_keys"].transpose(3, 0, 2, 1).reshape(P, 16, 32)
    out["l2f_down"] = a["L2_ffn_expert_down"].T.reshape(P, 8, P)
    out["l2f_up"] = a["L2_ffn_expert_up"].reshape(8, P, P).transpose(1, 0, 2)


LAYERS = ("l0_xattn", "l0_ffn", "l1_xattn", "l1_ffn", "l2_xattn", "l2_ffn", "l3_xattn", "l3_ffn")
IN_PLACE_OF = {"l2f": "l0f", "l3": "l0"}


def build(nc, dram, where, out, layers=LAYERS):
    with ExitStack() as ctx:
        m, group, loaded = {}, {}, {}
        for n, d in dram.items():
            if n in IN_PLACE_OF:
                continue
            shape = list(d.shape)
            for late, early in IN_PLACE_OF.items():
                if n == early:
                    shape[1] = max(shape[1], dram[late].shape[1])
            group[n] = ctx.enter_context(nc.sbuf_tensor(n + "_in", shape, d.dtype))
        for late, early in IN_PLACE_OF.items():
            group[late] = group[early]
        for n, d in dram.items():
            loaded[n] = ctx.enter_context(nc.semaphore(n + "_loaded"))
            if n not in GROUPS and n != "common":
                m[n] = group[n]
        by_group = {g: {} for g in GROUPS + ("common",)}
        for name, (g, first, shape) in where.items():
            size = 1
            for s in shape[1:]:
                size *= s
            ap = group[g][0:shape[0], first:first + size]
            if name.endswith("_bf"):
                ap, shape = ap.bitcast(BF16), shape[:-1] + (2 * shape[-1],)
            if len(shape) > 2:
                axes = "abcd"[:len(shape) - 1]
                ap = ap.rearrange(f"p ({' '.join(axes)}) -> p {' '.join(axes)}", **dict(zip(axes, shape[1:])))
            if g == "common":
                m[name] = ap
            else:
                by_group[g][name[len(g) + 1:]] = ap
        m["xnT"] = ctx.enter_context(nc.sbuf_tensor("xnT", [P, B, S], F32))
        stored = ctx.enter_context(nc.semaphore("stored"))

        def load(sp, *names):
            for n in names:
                index = (slice(None), slice(0, dram[n].shape[1])) + tuple(slice(None) for _ in dram[n].shape[2:])
                partitions = slice(0, dram[n].shape[0])
                sp.dma_start(group[n][(partitions,) + index[1:]], dram[n]).then_inc(loaded[n], 16)

        def wait(sp, *names):
            for n in names:
                sp.wait_ge(loaded[n], 16)

        with nc.Block() as block:
            @block.sync
            def _(sp):
                load(sp, "x", "common", "l0", "ctxT", *[n for n in m if n in dram and n not in ALONE])
                wait(sp, "x", "common")
                wait(sp, "l0", "ctxT", *[n for n in m if n in dram and n not in ALONE])
                load(sp, "l0f", "l1", "l1f", "l2", "l3f")
        run = [
            ("l0_xattn", multihead, "l0", dict(masked_keys=True), lambda sp: wait(sp, "l0f")),
            ("l0_ffn", refine_experts, "l0f", {}, lambda sp: (load(sp, "l3"), wait(sp, "l1"))),
            ("l1_xattn", multihead, "l1", dict(tempered=True), lambda sp: (load(sp, "l2f"), wait(sp, "l1f"))),
            ("l1_ffn", top1_experts, "l1f", {}, lambda sp: wait(sp, "l2")),
            ("l2_xattn", two_attentions, "l2", {}, lambda sp: wait(sp, "l2f")),
            ("l2_ffn", product_keys, "l2f", {}, lambda sp: wait(sp, "l3")),
            ("l3_xattn", multihead, "l3", dict(causal=True), lambda sp: wait(sp, "l3f")),
            ("l3_ffn", gated_lora, "l3f", {}, lambda sp: None),
        ]
        if layers != LAYERS:
            first = [r[2] for r in run if r[0] == layers[0]][0]
            with nc.Block() as block:
                @block.sync
                def _(sp):
                    if first in IN_PLACE_OF:
                        wait(sp, IN_PLACE_OF[first])
                        load(sp, first)
                    wait(sp, first)
        for name, layer, tag, options, meanwhile in run:
            if name in layers:
                layer(nc, m, by_group[tag], tag, meanwhile if layers == LAYERS else (lambda sp: None), **options)
        with nc.Block() as block:
            @block.sync
            def _(sp):
                sp.dma_start(out, m["x"][:, :, :]).then_inc(stored, 16)
                sp.wait_ge(stored, 16)


def kernel(**inputs):
    import numpy as np
    import concourse.bacc as bacc
    from concourse.bass_utils import run_bass_kernel_spmd

    nc = bacc.Bacc("TRN2", target_bir_lowering=False, num_devices=1)
    arrays, where = _layout({k: np.asarray(v) for k, v in inputs.items()})
    dram = {n: nc.dram_tensor(f"in_{n}", list(v.shape), mybir.dt.from_np(v.dtype), kind="ExternalInput").ap()
            for n, v in arrays.items()}
    out = nc.dram_tensor("out_x", [P, B, D], F32, kind="ExternalOutput").ap()
    build(nc, dram, where, out)
    r = run_bass_kernel_spmd(nc, [{f"in_{n}": v for n, v in arrays.items()}], core_ids=[0])
    return np.ascontiguousarray(r.results[0]["out_x"].transpose(1, 0, 2))
```
